# Optimizing a Trainium2 kernel written in Bass

```python
import numpy as np
import jax
import jax.numpy as jnp

def _softmax(x, axis=-1):
    return jax.nn.softmax(x, axis=axis)

def _gelu(x):
    return jax.nn.gelu(x, approximate=True)

def _silu(x):
    return jax.nn.silu(x)

def _sigmoid(x):
    return jax.nn.sigmoid(x)

def _layernorm(x, axis=-1, eps=1e-05):
    m = jnp.mean(x, axis=axis, keepdims=True)
    v = jnp.var(x, axis=axis, keepdims=True)
    return (x - m) / jnp.sqrt(v + eps)

def _scatter_add(tgt, idx, src, axis=0):
    return tgt.at[idx].add(src)

def _segment_sum(src, seg, n):
    return jax.ops.segment_sum(src, seg, n)
kernel_name = 'mk_seq_preln_d2_jaxref_r8_e6001b'

def setup_inputs(seed: int=0):
    np.random.seed(seed)
    _w = jnp.asarray

    def _L0_attn_setup():
        import jax, jax.numpy as jnp
        import numpy as np
        import math
        HIDDEN = 256
        NUM_HEADS = 16
        HEAD_SIZE = HIDDEN // NUM_HEADS
        BATCH = 2
        SEQ = 256
        key = jax.random.key(seed)
        k_x, k_wq, k_bq, k_wo, k_bo = jax.random.split(key, 5)
        scale_in = 1.0 / math.sqrt(HIDDEN)
        return {'x': jax.random.normal(k_x, (BATCH, SEQ, HIDDEN), dtype=jnp.float32), 'Wqkv': jax.random.normal(k_wq, (HIDDEN, 3 * HIDDEN), dtype=jnp.float32) * scale_in, 'bqkv': jax.random.normal(k_bq, (3 * HIDDEN,), dtype=jnp.float32) * 0.01, 'Wo': jax.random.normal(k_wo, (HIDDEN, HIDDEN), dtype=jnp.float32) * scale_in, 'bo': jax.random.normal(k_bo, (HIDDEN,), dtype=jnp.float32) * 0.01}
    _L0_attn_in = _L0_attn_setup()

    def _L0_ffn_setup():
        import jax, jax.numpy as jnp
        import numpy as np
        D = 256
        H = 16
        KV = 4
        DH = 128
        RD = 64
        E = 8
        TOPK = 2
        I = 128
        EPS = 1e-06
        THETA = 1000000.0

        def rmsnorm(h, w, eps=EPS):
            dt = h.dtype
            h32 = h.astype(jnp.float32)
            var = jnp.mean(h32 * h32, axis=-1, keepdims=True)
            return (w * (h32 * jax.lax.rsqrt(var + eps))).astype(dt)

        def rotate_half(t):
            half = t.shape[-1] // 2
            return jnp.concatenate([-t[..., half:], t[..., :half]], axis=-1)
        key = jax.random.key(seed)
        ks = jax.random.split(key, 16)
        s = lambda k, shape, sc: jax.random.normal(k, shape, dtype=jnp.float32) * sc
        B, S = (1, 256)
        return {'x': s(ks[0], (B, S, D), 1.0), 'ln1_w': jnp.ones((D,), jnp.float32), 'ln2_w': jnp.ones((D,), jnp.float32), 'wq': s(ks[1], (D, H * DH), 0.02), 'wk': s(ks[2], (D, KV * DH), 0.02), 'wv': s(ks[3], (D, KV * DH), 0.02), 'wo': s(ks[4], (H * DH, D), 0.02), 'qnorm_w': jnp.ones((H * DH,), jnp.float32), 'knorm_w': jnp.ones((KV * DH,), jnp.float32), 'router_w': s(ks[5], (D, E), 0.02), 'router_bias': s(ks[6], (E,), 0.1), 'wg': s(ks[7], (E, D, I), 0.02), 'wu': s(ks[8], (E, D, I), 0.02), 'wd': s(ks[9], (E, I, D), 0.02)}
    _L0_ffn_in = _L0_ffn_setup()

    def _L1_attn_setup():
        import jax, jax.numpy as jnp
        import numpy as np
        D_INNER = 256
        STATE_DIM = 16
        DT_MIN = 0.0001

        def _softplus(x):
            return jnp.log1p(jnp.exp(-jnp.abs(x))) + jnp.maximum(x, 0)

        def _reference_tuple_inner(u, Wdt, bdt, Wb, bb, Wc, bc, a_raw, B_base, C_base, D):
            B, L, d = u.shape
            N = a_raw.shape[1]
            A = -_softplus(a_raw)
            dt = _softplus(jnp.einsum('bld,de->ble', u, Wdt) + bdt) + DT_MIN
            b_t = jnp.einsum('bld,de->ble', u, Wb) + bb
            c_t = jnp.einsum('bld,de->ble', u, Wc) + bc

            def step(x, inp):
                u_s, dt_s, b_s, c_s = inp
                Abar = jnp.exp(dt_s[:, :, None] * A)
                Bbar = dt_s[:, :, None] * (b_s[:, :, None] * B_base)
                x = Abar * x + Bbar * u_s[:, :, None]
                y = jnp.sum(c_s[:, :, None] * C_base * x, axis=-1) + D * u_s
                return (x, y)
            carry0 = jnp.zeros((B, d, N), dtype=u.dtype)
            xs = (jnp.swapaxes(u, 0, 1), jnp.swapaxes(dt, 0, 1), jnp.swapaxes(b_t, 0, 1), jnp.swapaxes(c_t, 0, 1))
            carry_out, ys = jax.lax.scan(step, carry0, xs)
            y = jnp.swapaxes(ys, 0, 1)
            return (carry_out, y)
        key = jax.random.key(seed)
        ks = jax.random.split(key, 11)
        B, L, d, N = (4, 512, D_INNER, STATE_DIM)
        u = jax.random.normal(ks[0], (B, L, d), dtype=jnp.float32)
        s = 0.02
        return {'u': u, 'Wdt': jax.random.normal(ks[1], (d, d), jnp.float32) / jnp.sqrt(d), 'bdt': jnp.zeros((d,), jnp.float32), 'Wb': jax.random.normal(ks[2], (d, d), jnp.float32) / jnp.sqrt(d), 'bb': jnp.zeros((d,), jnp.float32), 'Wc': jax.random.normal(ks[3], (d, d), jnp.float32) / jnp.sqrt(d), 'bc': jnp.zeros((d,), jnp.float32), 'a_raw': s * jax.random.normal(ks[4], (d, N), jnp.float32), 'B_base': s * jax.random.normal(ks[5], (d, N), jnp.float32), 'C_base': s * jax.random.normal(ks[6], (d, N), jnp.float32), 'D': jnp.zeros((d,), jnp.float32)}
    _L1_attn_in = _L1_attn_setup()

    def _L1_ffn_setup():
        import jax, jax.numpy as jnp
        import numpy as np
        NUM_EXPERTS = 32
        TOP_K = 8
        THRESHOLD = 0.8
        HIDDEN = 256
        INTER = 96
        key = jax.random.key(seed)
        k1, k2, k3, k4 = jax.random.split(key, 4)
        hidden_states = jax.random.normal(k1, (2, 128, HIDDEN), jnp.float32)
        gate_weight = jax.random.normal(k2, (NUM_EXPERTS, HIDDEN), jnp.float32) * 0.02
        gate_up_proj = jax.random.normal(k3, (NUM_EXPERTS, 2 * INTER, HIDDEN), jnp.float32) * 0.02
        down_proj = jax.random.normal(k4, (NUM_EXPERTS, HIDDEN, INTER), jnp.float32) * 0.02
        return {'hidden_states': hidden_states, 'gate_weight': gate_weight, 'gate_up_proj': gate_up_proj, 'down_proj': down_proj}
    _L1_ffn_in = _L1_ffn_setup()
    _d = {'L0_attn_x': _L0_attn_in['x'], 'L0_attn_Wqkv': _L0_attn_in['Wqkv'], 'L0_attn_bqkv': _L0_attn_in['bqkv'], 'L0_attn_Wo': _L0_attn_in['Wo'], 'L0_attn_bo': _L0_attn_in['bo'], 'L0_ffn_ln1_w': _L0_ffn_in['ln1_w'], 'L0_ffn_ln2_w': _L0_ffn_in['ln2_w'], 'L0_ffn_wq': _L0_ffn_in['wq'], 'L0_ffn_wk': _L0_ffn_in['wk'], 'L0_ffn_wv': _L0_ffn_in['wv'], 'L0_ffn_wo': _L0_ffn_in['wo'], 'L0_ffn_qnorm_w': _L0_ffn_in['qnorm_w'], 'L0_ffn_knorm_w': _L0_ffn_in['knorm_w'], 'L0_ffn_router_w': _L0_ffn_in['router_w'], 'L0_ffn_router_bias': _L0_ffn_in['router_bias'], 'L0_ffn_wg': _L0_ffn_in['wg'], 'L0_ffn_wu': _L0_ffn_in['wu'], 'L0_ffn_wd': _L0_ffn_in['wd'], 'L1_attn_Wdt': _L1_attn_in['Wdt'], 'L1_attn_bdt': _L1_attn_in['bdt'], 'L1_attn_Wb': _L1_attn_in['Wb'], 'L1_attn_bb': _L1_attn_in['bb'], 'L1_attn_Wc': _L1_attn_in['Wc'], 'L1_attn_bc': _L1_attn_in['bc'], 'L1_attn_a_raw': _L1_attn_in['a_raw'], 'L1_attn_B_base': _L1_attn_in['B_base'], 'L1_attn_C_base': _L1_attn_in['C_base'], 'L1_attn_D': _L1_attn_in['D'], 'L1_ffn_gate_weight': _L1_ffn_in['gate_weight'], 'L1_ffn_gate_up_proj': _L1_ffn_in['gate_up_proj'], 'L1_ffn_down_proj': _L1_ffn_in['down_proj']}
    _x0 = _d['L0_attn_x']
    _d['L0_attn_x'] = jax.random.normal(jax.random.fold_in(jax.random.key(seed), 1), (1, 1024, 256), dtype=_x0.dtype)
    del _x0
    return _d

def reference(L0_attn_x, L0_attn_Wqkv, L0_attn_bqkv, L0_attn_Wo, L0_attn_bo, L0_ffn_ln1_w, L0_ffn_ln2_w, L0_ffn_wq, L0_ffn_wk, L0_ffn_wv, L0_ffn_wo, L0_ffn_qnorm_w, L0_ffn_knorm_w, L0_ffn_router_w, L0_ffn_router_bias, L0_ffn_wg, L0_ffn_wu, L0_ffn_wd, L1_attn_Wdt, L1_attn_bdt, L1_attn_Wb, L1_attn_bb, L1_attn_Wc, L1_attn_bc, L1_attn_a_raw, L1_attn_B_base, L1_attn_C_base, L1_attn_D, L1_ffn_gate_weight, L1_ffn_gate_up_proj, L1_ffn_down_proj):

    def _L0_attn_ref(x, Wqkv, bqkv, Wo, bo):
        import jax, jax.numpy as jnp
        import numpy as np
        import math
        HIDDEN = 256
        NUM_HEADS = 16
        HEAD_SIZE = HIDDEN // NUM_HEADS
        BATCH = 2
        SEQ = 256
        b, s, _ = x.shape
        kqv = x @ Wqkv + bqkv
        kqv = kqv.reshape(b, s, 3, NUM_HEADS, HEAD_SIZE)
        q = kqv[:, :, 0]
        k = kqv[:, :, 1]
        v = kqv[:, :, 2]
        scores = jnp.einsum('bsnh,btnh->bnst', k, q) / math.sqrt(HEAD_SIZE)
        ones = jnp.ones_like(scores)
        scores = jnp.triu(scores) + -10000.0 * jnp.tril(ones, k=-1)
        attn = jax.nn.softmax(scores, axis=2)
        out = jnp.einsum('bnkq,bknh->bqnh', attn, v)
        out = out.reshape(b, s, NUM_HEADS * HEAD_SIZE)
        return out @ Wo + bo

    def _L0_ffn_ref(x, ln1_w, ln2_w, wq, wk, wv, wo, qnorm_w, knorm_w, router_w, router_bias, wg, wu, wd):
        import jax, jax.numpy as jnp
        import numpy as np
        D = 256
        H = 16
        KV = 4
        DH = 128
        RD = 64
        E = 8
        TOPK = 2
        I = 128
        EPS = 1e-06
        THETA = 1000000.0

        def rmsnorm(h, w, eps=EPS):
            dt = h.dtype
            h32 = h.astype(jnp.float32)
            var = jnp.mean(h32 * h32, axis=-1, keepdims=True)
            return (w * (h32 * jax.lax.rsqrt(var + eps))).astype(dt)

        def rotate_half(t):
            half = t.shape[-1] // 2
            return jnp.concatenate([-t[..., half:], t[..., :half]], axis=-1)
        B, S, _ = x.shape
        res = x
        h = rmsnorm(x, ln1_w)
        q = h @ wq
        k = h @ wk
        v = h @ wv
        q = rmsnorm(q, qnorm_w)
        k = rmsnorm(k, knorm_w)
        q = q.reshape(B, S, H, DH).transpose(0, 2, 1, 3)
        k = k.reshape(B, S, KV, DH).transpose(0, 2, 1, 3)
        v = v.reshape(B, S, KV, DH).transpose(0, 2, 1, 3)
        pos = jnp.arange(S, dtype=jnp.float32)
        inv_freq = 1.0 / THETA ** (jnp.arange(0, RD, 2, dtype=jnp.float32) / RD)
        ang = pos[:, None] * inv_freq[None, :]
        emb = jnp.concatenate([ang, ang], axis=-1)
        cos, sin = (jnp.cos(emb), jnp.sin(emb))

        def rope(t):
            rot, pas = (t[..., :RD], t[..., RD:])
            rot = rot * cos + rotate_half(rot) * sin
            return jnp.concatenate([rot, pas], axis=-1)
        q, k = (rope(q), rope(k))
        rep = H // KV
        k = jnp.repeat(k, rep, axis=1)
        v = jnp.repeat(v, rep, axis=1)
        scores = jnp.einsum('bhqd,bhkd->bhqk', q, k) / np.sqrt(DH)
        causal = jnp.tril(jnp.ones((S, S), dtype=bool))
        scores = jnp.where(causal, scores, jnp.finfo(jnp.float32).min)
        attn = jax.nn.softmax(scores.astype(jnp.float32), axis=-1).astype(q.dtype)
        o = jnp.einsum('bhqk,bhkd->bhqd', attn, v)
        o = o.transpose(0, 2, 1, 3).reshape(B, S, H * DH) @ wo
        x1 = res + o
        h2 = rmsnorm(x1, ln2_w)
        t = h2.reshape(-1, D)
        T = t.shape[0]
        logits = t.astype(jnp.float32) @ router_w
        sig = jax.nn.sigmoid(logits)
        _, topi = jax.lax.top_k(sig + router_bias, TOPK)
        aff = jnp.take_along_axis(sig, topi, axis=-1)
        aff = aff / jnp.sum(aff, axis=-1, keepdims=True)
        combine = jnp.zeros((T, E), jnp.float32).at[jnp.arange(T)[:, None], topi].set(aff)
        gate = jnp.einsum('td,edi->tei', t, wg)
        up = jnp.einsum('td,edi->tei', t, wu)
        act = jax.nn.silu(gate) * up
        moe = jnp.einsum('te,tei,eid->td', combine.astype(t.dtype), act, wd)
        return x1 + moe.reshape(B, S, D)

    def _L1_attn_ref(u, Wdt, bdt, Wb, bb, Wc, bc, a_raw, B_base, C_base, D):
        import jax, jax.numpy as jnp
        import numpy as np
        D_INNER = 256
        STATE_DIM = 16
        DT_MIN = 0.0001

        def _softplus(x):
            return jnp.log1p(jnp.exp(-jnp.abs(x))) + jnp.maximum(x, 0)

        def _reference_tuple_inner(u, Wdt, bdt, Wb, bb, Wc, bc, a_raw, B_base, C_base, D):
            B, L, d = u.shape
            N = a_raw.shape[1]
            A = -_softplus(a_raw)
            dt = _softplus(jnp.einsum('bld,de->ble', u, Wdt) + bdt) + DT_MIN
            b_t = jnp.einsum('bld,de->ble', u, Wb) + bb
            c_t = jnp.einsum('bld,de->ble', u, Wc) + bc

            def step(x, inp):
                u_s, dt_s, b_s, c_s = inp
                Abar = jnp.exp(dt_s[:, :, None] * A)
                Bbar = dt_s[:, :, None] * (b_s[:, :, None] * B_base)
                x = Abar * x + Bbar * u_s[:, :, None]
                y = jnp.sum(c_s[:, :, None] * C_base * x, axis=-1) + D * u_s
                return (x, y)
            carry0 = jnp.zeros((B, d, N), dtype=u.dtype)
            xs = (jnp.swapaxes(u, 0, 1), jnp.swapaxes(dt, 0, 1), jnp.swapaxes(b_t, 0, 1), jnp.swapaxes(c_t, 0, 1))
            carry_out, ys = jax.lax.scan(step, carry0, xs)
            y = jnp.swapaxes(ys, 0, 1)
            return (carry_out, y)
        return _reference_tuple_inner(u, Wdt, bdt, Wb, bb, Wc, bc, a_raw, B_base, C_base, D)[1]

    def _L1_ffn_ref(hidden_states, gate_weight, gate_up_proj, down_proj):
        import jax, jax.numpy as jnp
        import numpy as np
        NUM_EXPERTS = 32
        TOP_K = 8
        THRESHOLD = 0.8
        HIDDEN = 256
        INTER = 96
        B, S, H = hidden_states.shape
        x = hidden_states.reshape(-1, H)
        logits = x @ gate_weight.T
        probs = jax.nn.softmax(logits.astype(jnp.float32), axis=-1).astype(logits.dtype)
        top_vals, top_idx = jax.lax.top_k(probs, TOP_K)
        renorm = top_vals / jnp.clip(jnp.sum(top_vals, axis=-1, keepdims=True), 1e-12)
        cum = jnp.cumsum(renorm, axis=-1)
        num_keep = jnp.minimum(jnp.sum((cum < THRESHOLD).astype(jnp.int32), axis=-1) + 1, TOP_K)
        active = jnp.arange(TOP_K)[None, :] < num_keep[:, None]
        rw = top_vals * active.astype(top_vals.dtype)
        rw = rw / jnp.clip(jnp.sum(rw, axis=-1, keepdims=True), 1e-12)
        combine = jnp.sum(jax.nn.one_hot(top_idx, NUM_EXPERTS, dtype=rw.dtype) * rw[..., None], axis=1)

        def body(acc, params):
            w_gu, w_d, ce = params
            gu = x @ w_gu.T
            g, u = jnp.split(gu, 2, axis=-1)
            h = jax.nn.silu(g) * u
            return (acc + h @ w_d.T * ce[:, None], None)
        out, _ = jax.lax.scan(body, jnp.zeros_like(x), (gate_up_proj, down_proj, combine.T))
        return out.reshape(B, S, H)
    x = L0_attn_x
    x = x + _L0_attn_ref(_layernorm(x, axis=-1), L0_attn_Wqkv, L0_attn_bqkv, L0_attn_Wo, L0_attn_bo)
    x = x + _L0_ffn_ref(_layernorm(x, axis=-1), L0_ffn_ln1_w, L0_ffn_ln2_w, L0_ffn_wq, L0_ffn_wk, L0_ffn_wv, L0_ffn_wo, L0_ffn_qnorm_w, L0_ffn_knorm_w, L0_ffn_router_w, L0_ffn_router_bias, L0_ffn_wg, L0_ffn_wu, L0_ffn_wd)
    x = x + _L1_attn_ref(_layernorm(x, axis=-1), L1_attn_Wdt, L1_attn_bdt, L1_attn_Wb, L1_attn_bb, L1_attn_Wc, L1_attn_bc, L1_attn_a_raw, L1_attn_B_base, L1_attn_C_base, L1_attn_D)
    x = x + _L1_ffn_ref(_layernorm(x, axis=-1), L1_ffn_gate_weight, L1_ffn_gate_up_proj, L1_ffn_down_proj)
    return x

_drawn_inputs = setup_inputs


def setup_inputs(seed=0):
    import zlib

    import numpy as np

    out = dict(_drawn_inputs(seed))
    spreads = {'L0_ffn_ln1_w': (1.0, 0.6),
     'L0_ffn_ln2_w': (1.0, 0.6),
     'L0_ffn_qnorm_w': (1.0, 0.6),
     'L0_ffn_knorm_w': (1.0, 0.6),
     'L1_attn_bdt': (0.0, 0.8),
     'L1_attn_bb': (0.0, 0.8),
     'L1_attn_bc': (0.0, 0.8),
     'L1_attn_D': (0.0, 2.0)}
    factors = {'L0_attn_bqkv': 4.924,
     'L0_attn_bo': 5.744,
     'L0_ffn_wq': 3.19,
     'L0_ffn_wk': 3.21,
     'L0_ffn_router_w': 8.0,
     'L0_ffn_router_bias': 8.0,
     'L0_ffn_wg': 8.0,
     'L0_ffn_wu': 8.0,
     'L0_ffn_wd': 8.0,
     'L1_attn_Wdt': 8.0,
     'L1_attn_Wb': 8.0,
     'L1_attn_Wc': 8.0,
     'L1_attn_a_raw': 8.0,
     'L1_attn_B_base': 8.0,
     'L1_attn_C_base': 8.0,
     'L1_ffn_gate_weight': 8.0,
     'L1_ffn_gate_up_proj': 8.0,
     'L1_ffn_down_proj': 8.0}
    for name, (base, spread) in spreads.items():
        noise = np.random.default_rng([zlib.crc32(name.encode()), seed]).standard_normal(out[name].shape)
        drawn = base * np.exp(spread * noise) if base else spread * noise
        out[name] = jnp.asarray(drawn.astype(out[name].dtype))
    for name, factor in factors.items():
        out[name] = (out[name] * factor).astype(out[name].dtype)
    return out
```

```python
from contextlib import ExitStack

import concourse.bass as bass
from concourse import mybir

F32 = mybir.dt.float32
F32R = mybir.dt.float32r
BF16 = mybir.dt.bfloat16
U32 = mybir.dt.uint32
ALU = mybir.AluOpType
ACT = mybir.ActivationFunctionType
X_AXIS = mybir.AxisListType.X

P = 128
S = 1024
D = 256
KD = D // P
NT = S // P
CH = 512
NC = S // CH
TC = CH // P
H1, HD1 = 16, 16
PR1 = H1 // 2
H2, KV2, DH2, RD = 16, 4, 128, 64
E1, I1, TOP1 = 8, 128, 2
E2, I2, TOP2 = 32, 96, 8
THRESHOLD = 0.8
NST = 16
DT_MIN = 0.0001
MASKED = -1.0e30
PIECE = 1024



def weight_stream():
    out = []
    for c in range(NC):
        out += [(("wqkv", c, k), k, 3 * D) for k in range(KD)]
        out.append((("wo1", c), 2, KD * D))
    for c in range(NC):
        out += [(("w2", c, g), 3 + g, KD * CH) for g in range(6)]
        out += [(("wo2", c, j), 9 + j, 4 * D) for j in range(KV2)]
    out += [(("rw", 0), 13, KD * E1)]
    out += [(("moe", 0, e), 14 + e, 2 * KD * I1 + D) for e in range(E1)]
    out += [(("ssm", w), 22 + w, KD * D) for w in range(3)]
    out += [(("rw", 1), 25, KD * E2)]
    out += [(("moe", 1, e), 26 + e, 2 * KD * I2 + D) for e in range(E2)]
    return out


N_PIECES = 26 + E2



def weave(main, side):
    out, at = [], 0
    for n, step in enumerate(main):
        out.append(step)
        upto = -(-(n + 1) * len(side) // len(main))
        out += side[at:upto]
        at = upto
    return out + side[at:]


def norm_steps(stage, c):
    return [("norm", stage, c)] + [("normT", stage, c, k) for k in range(KD)]


def attention1(c):
    def maxima(g):
        out = []
        for p in (2 * g, 2 * g + 1):
            for t in range(TC * c, TC * c + TC):
                out += [("max1", c, t, p, None)] if c == 0 else [("max1", c, t, p, i) for i in (0, 1)]
            out.append(("qT1", c, p, 1))
        return out

    def scores(g):
        jobs = [(c, g, sb, i) for sb in range(TC * c + TC) for i in (0, 1)]
        out = []
        for n, job in enumerate(jobs):
            out.append(("score1",) + job)
            if n >= 1:
                out.append(("pv1",) + jobs[n - 1])
        return out + [("pv1",) + jobs[-1]]

    tiles = range(TC * c, TC * c + TC)
    out = [("qkv1", tiles[0])]
    for t in tiles[1:]:
        out += [("qkv1", t)] + [("kT1", t - 1, half) for half in (0, 1)]
    out += [("kT1", tiles[-1], half) for half in (0, 1)]
    out += [("qT1", c, p, 0) for p in range(PR1)]
    out += maxima(0)
    for g in range(4):
        side = ([("out1", c, g - 1)] if g else []) + (maxima(g + 1) if g < 3 else [])
        out += weave(scores(g), side)
    out.append(("out1", c, 3))
    out += [("aT1", c, k) for k in range(KD)]
    out += [("wo1", c, tp) for tp in range(TC // 2)]
    return out


def attention2(c):
    units = [(c, j, hp) for j in range(KV2) for hp in range(2)]

    def maxima(u):
        out = [("qT2", u, i) for i in (0, 1)]
        for t in range(TC * c, TC * c + TC):
            out += [("max2", u, t, None)] if c == 0 else [("max2", u, t, i) for i in (0, 1)]
        return out + [("mT2", u)]

    def scores(u):
        n = TC * c + TC
        out = []
        for sb in range(n):
            out.append(("score2", u, sb))
            if sb:
                out.append(("pv2", u, sb - 1))
        return out + [("pv2", u, n - 1)]

    def finish(u):
        return [("out2", u)] + [("wo2", u, tp) for tp in range(TC // 2)]

    out = norm_steps(1, c)
    out += [("qkv2", c, g, tp) for g in range(6) for tp in range(TC // 2)]
    out.append(("rms2", c))
    out += [("rope", c, t, "k") for t in range(TC)]
    out += [("kT2", c, j) for j in range(KV2)]
    out += [("rope", c, t, "q") for t in range(TC)]
    out += maxima(units[0])
    for n, u in enumerate(units):
        side = (finish(units[n - 1]) if n else []) + (maxima(units[n + 1]) if n + 1 < len(units) else [])
        out += weave(scores(u), side)
    out += finish(units[-1])
    return out


def experts(stage, n):
    jobs = [(stage, e, c) for e in range(n) for c in range(NC)]
    out = []
    for i, job in enumerate(jobs):
        out.append(("gateup",) + job)
        if i:
            out += [("down",) + jobs[i - 1] + (tp,) for tp in range(TC // 2)]
    return out + [("down",) + jobs[-1] + (tp,) for tp in range(TC // 2)]


def all_steps():
    out = []
    for c in range(NC):
        out += norm_steps(0, c) + attention1(c)
    for c in range(NC):
        out += attention2(c)
    for c in range(NC):
        out += norm_steps(2, c)
    out += [("router", 0)] + experts(0, E1)
    for c in range(NC):
        out += norm_steps(3, c)
    out += [("rates",)]
    out += [("proj", w, ob) for w in range(3) for ob in range(KD)]
    for ob in range(KD):
        out += [("scan", ob, n) for n in range(NST)] + [("y", ob)]
    out += [("yT", tp) for tp in range(NT // 2)]
    for c in range(NC):
        out += norm_steps(4, c)
    out += [("router", 1)] + experts(1, E2)
    return out


STEPS = all_steps()

RINGS = {
    "T": {"qkv1": (1, 1), "max1": (1, 1), "score1": (1, 1), "qkv2": (1, 1), "max2": (1, 1), "score2": (1, 1),
          "gateup": (1, 1), "proj": (1, 1)},
    "M": {"normT": (1, 1), "kT1": (1, 1), "qT1": (1, 2), "out1": (1, 1), "aT1": (1, 1), "wo1": (1, 1),
          "kT2": (1, 1), "qT2": (1, 1), "mT2": (1, 1), "out2": (2, 1), "wo2": (1, 1), "router": (1, 1),
          "down": (1, 1), "yT": (1, 1)},
    "O": {"o1": (1, 1), "o2": (2, 1), "y": (2, 1)},
}


def ring_table(ring):
    kinds = RINGS[ring]
    released, filled, n, table = [0, 0], [0, 0], 0, {}
    for step in STEPS:
        key = step
        if ring == "O":
            if step[0] == "score1" and step[3] == 0 and step[4] == 0:
                key = ("o1", step[1], step[2])
            elif step[0] == "score2" and step[2] == 0:
                key = ("o2", step[1])
            elif step[0] == "scan" and step[2] == 0:
                key = ("y", step[1])
            else:
                continue
        if key[0] not in kinds:
            continue
        slots, ends = kinds[key[0]]
        table[key] = []
        for _ in range(slots):
            s = n % 2
            filled[s] += 1
            table[key].append((s, released[s], filled[s], released[s] + ends))
            released[s] += ends
            n += 1
    return table


def ordinals():
    count, out = {}, {}
    for step in STEPS:
        count[step[0]] = count.get(step[0], 0) + 1
        out[step] = count[step[0]]
    return out


def build(nc, a, out_dram):
    tab = {r: ring_table(r) for r in RINGS}
    nth = ordinals()
    stream = weight_stream()
    mts = [st for st in STEPS if st[0] == "mT2"]
    outs = [st for st in STEPS if st[0] == "out2"]
    gus = [st for st in STEPS if st[0] == "gateup"]
    order = {name: n for n, (name, _, _) in enumerate(stream)}

    with ExitStack() as ctx:
        def psum(name, shape):
            return ctx.enter_context(nc.psum_tensor(name, shape, F32))

        def sb(name, shape, dt=F32):
            return ctx.enter_context(nc.sbuf_tensor(name, shape, dt))

        sems = {}

        def sem(name):
            if name not in sems:
                sems[name] = ctx.enter_context(nc.semaphore(name))
            return sems[name]

        psT = [psum("psT0", [P, 2, CH]), psum("psT1", [P, 2, CH])]
        psO = psum("psO", [P, 2, CH])
        psM = [psum("psM0", [P, CH]), psum("psM1", [P, CH])]

        x = sb("x", [P, NT, D])
        xn = sb("xn", [P, NT, D])
        normed = sb("normed", [P, TC, D])
        xTh = sb("xTh", [P, KD, S], F32R)
        xTl = sb("xTl", [P, KD, S], F32R)
        w_raw = sb("w_raw", [P, 2, PIECE])
        w_hi = sb("w_hi", [P, 2, PIECE], F32R)
        w_lo = sb("w_lo", [P, 2, PIECE], F32R)
        probs = sb("probs", [P, 2, 2, CH])
        ident = sb("ident", [P, P])
        ones = sb("ones", [P, P])
        ident_b = sb("ident_b", [P, P], BF16)
        mask_q = sb("mask_q", [P, P], BF16)
        mask_k = sb("mask_k", [P, P], BF16)
        iota = sb("iota", [P, E2])
        iota_i = sb("iota_i", [P, E2], mybir.dt.int32)
        lnw = sb("lnw", [P, 5, KD])
        bn6 = sb("bn6", [P, TC, 6])
        mv = sb("mv", [P, TC, 2])
        rs = sb("rs", [P, 3, TC])
        FN, RN = 17840, 16 * 1024
        fr = sb("fr", [P, FN])
        rr = sb("rr", [P, RN], F32R)

        class Carve:
            def __init__(self, base, limit):
                self.base, self.limit, self.at = base, limit, 0

            def take(self, *dims):
                n = int(np_prod(dims))
                v = self.base[:, self.at:self.at + n]
                self.at += n
                assert self.at <= self.limit, (self.at, self.limit)
                if len(dims) == 2:
                    return v.rearrange("p (a b) -> p a b", b=dims[1])
                if len(dims) == 3:
                    return v.rearrange("p (a b c) -> p a b c", b=dims[1], c=dims[2])
                return v

        def np_prod(dims):
            n = 1
            for d in dims:
                n *= d
            return n

        f, r = Carve(fr, FN), Carve(rr, RN)
        bqkv_b = f.take(3 * D)
        bo_b = f.take(D)
        qkv_tok = f.take(3 * D)
        q_stack = f.take(TC, H1, 64)
        k_stack = f.take(H1, 64)
        v_aug = f.take(NT, H1, HD1 + 1)
        o1_T = f.take(CH)
        a_tok = f.take(TC, D)
        den1 = f.take(TC, 4)
        kT1 = r.take(PR1, S)
        qT1 = r.take(H1, CH)
        f, r = Carve(fr, FN), Carve(rr, RN)
        q_tok = f.take(TC, H2, DH2)
        k_tok = f.take(TC, KV2, DH2)
        p_sum = k_tok.rearrange("p a b c -> p (a b c)")[:, 0:2 * CH].rearrange("p (a b) -> p a b", b=CH)
        o_raw = k_tok.rearrange("p a b c -> p (a b c)")[:, 2 * CH:4 * CH].rearrange("p (a b) -> p a b", b=CH)
        v_tok = f.take(NT, CH)
        qkw = f.take(2, CH)
        cos_t = f.take(NT, RD)
        sin_t = f.take(NT, RD)
        neg_max = f.take(TC, P)
        rec2 = f.take(CH)
        ssq = f.take(TC, 8)
        kTh = r.take(KV2, S)
        kTl = r.take(KV2, S)
        qTh = r.take(2, 2, CH)
        qTl = r.take(2, 2, CH)
        negmT = r.take(CH)
        pick = r.take(2, P)
        oTh = r.take(2, CH)
        oTl = r.take(2, CH)
        f, r = Carve(fr, FN), Carve(rr, RN)
        logits = f.take(NT, E2)
        rt = f.take(NT, E2)
        comb = f.take(NT, E2)
        top8 = f.take(NT, 8)
        idx_u = f.take(NT, 8)
        idx_f = f.take(NT, 8)
        cum = f.take(NT, 8)
        onehot = f.take(NT, 8, E2)
        tok1 = f.take(NT)
        tok2 = f.take(NT)
        gate = f.take(2, CH)
        act = f.take(2, CH)
        aTh = r.take(2, CH)
        aTl = r.take(2, CH)
        uT = f.take(KD, S)
        dtT = f.take(KD, S)
        bT = f.take(KD, S)
        cT = f.take(KD, S)
        decay = f.take(2, S)
        state = f.take(2, S)
        sp_a = decay[:, 0]
        sp_b = decay[:, 1]
        sp_c = state[:, 0]
        diag = f.take(2, P)
        yT = uT
        rbias = sb("rbias", [P, E1])
        vecs = sb("vecs", [P, 4, KD])
        mats = sb("mats", [P, 3, KD * NST])
        sp_s = sb("sp_s", [P, 3, KD * NST])
        neg_a = sb("neg_a", [P, KD * NST])
        bc_s = sb("bc_s", [P, KD * NST])

        block = ctx.enter_context(nc.Block())

        def wait_full(eng, ring, use, i=0):
            slot, _, fills, _ = tab[ring][use][i]
            eng.wait_ge(sem(f"{ring}_full{slot}"), fills)
            return slot

        def wait_read(eng, ring, use, i=0):
            slot, _, _, ends = tab[ring][use][i]
            eng.wait_ge(sem(f"{ring}_read{slot}"), ends)

        @block.sync
        def _(sp):
            sp.dma_start(x[:], a["x"].rearrange("a (t p) d -> p (a t) d", p=P)).then_inc(sem("x_loaded"), 16)
            for dst, src in ((bqkv_b, a["bqkv"].partition_broadcast(P)), (bo_b, a["bo"].partition_broadcast(P)),
                             (lnw[:], a["lnw"]), (rbias[:], a["rbias"].partition_broadcast(P)), (vecs[:], a["vecs"]), (mats[:], a["mats"])):
                sp.dma_start(dst, src).then_inc(sem("consts_loaded"), 16)
            rows = []
            for n, (name, at, width) in enumerate(stream):
                if n >= 2:
                    sp.wait_ge(sem("w_split"), n - 1)
                sp.dma_start(w_raw[:, n % 2, 0:width], a["weights"][at, :, 0:width]).then_inc(sem(f"w_loaded{n % 2}"), 16)
                if name[0] == "w2" and name[2] != 1:
                    g = name[2]
                    if len(rows) >= 2:
                        wait_read(sp, "T", rows[-2])
                    sp.dma_start(qkw[:, len(rows) % 2], a["qkw"][g].partition_broadcast(P)).then_inc(
                        sem(f"row_loaded{len(rows) % 2}"), 16)
                    rows.append(("qkv2", name[1], g, TC // 2 - 1))
                if n == KD:
                    sp.dma_start(cos_t, a["cos"]).then_inc(sem("tables_loaded"), 16)
                    sp.dma_start(sin_t, a["sin"]).then_inc(sem("tables_loaded"), 16)
            wait_read(sp, "M", ("down", 1, E2 - 1, NC - 1, TC // 2 - 1))
            sp.dma_start(out_dram.rearrange("a (t p) d -> p (a t) d", p=P), x[:]).then_inc(sem("stored"), 16)
            sp.wait_ge(sem("stored"), 16)

        @block.gpsimd
        def _(pool):
            g = nc.gpsimd
            chained = [0]

            def link(ins):
                chained[0] += 1
                ins.then_inc(sem("pool_chain"), 1)
                pool.wait_ge(sem("pool_chain"), chained[0])

            g.memset(ident[:], 0.0)
            g.memset(ones[:], 1.0)
            g.memset(mask_q[:], 0.0)
            g.memset(q_stack, 0.0)
            g.memset(k_stack, 0.0)
            g.memset(v_aug, 1.0)
            g.memset(qT1.bitcast(F32), 0.0)
            link(g.memset(mask_k[:], 0.0))
            link(g.memset(k_stack[:, :, 48:49], 1.0))
            link(g.affine_select(out=ident[:], in_=ident[:], compare_op=ALU.not_equal, fill=1.0, base=0,
                                 pattern=[[-1, P]], channel_multiplier=1))
            g.tensor_copy(ident_b[:], ident[:])
            g.affine_select(out=mask_q[:], in_=mask_q[:], compare_op=ALU.is_ge, fill=MASKED, base=0,
                            pattern=[[-1, P]], channel_multiplier=1)
            g.affine_select(out=mask_k[:], in_=mask_k[:], compare_op=ALU.is_ge, fill=MASKED, base=0,
                            pattern=[[1, P]], channel_multiplier=-1)
            link(g.iota(iota_i[:], pattern=[[1, E2]], base=0, channel_multiplier=0))
            g.tensor_copy(iota[:], iota_i[:]).then_inc(sem("consts_ready"), 1)

            last_use = {}
            for step in STEPS:
                kind = step[0]
                if kind == "qkv1":
                    for k in range(KD):
                        last_use[("wqkv", step[1] // TC, k)] = step
                elif kind == "wo1":
                    last_use[("wo1", step[1])] = step
                elif kind == "qkv2":
                    last_use[("w2", step[1], step[2])] = step
                elif kind == "wo2":
                    last_use[("wo2", step[1][0], step[1][1])] = step
                elif kind == "router":
                    last_use[("rw", step[1])] = step
                elif kind == "down":
                    last_use[("moe", step[1], step[2])] = step
                elif kind == "proj":
                    last_use[("ssm", step[1])] = step
            after = {}
            for n, (name, _, _) in enumerate(stream):
                after.setdefault(last_use[name], []).append(n + 2)

            split_upto = [0]

            def split_next():
                n = split_upto[0]
                if n >= len(stream):
                    return
                name, _, width = stream[n]
                pool.wait_ge(sem(f"w_loaded{n % 2}"), 16 * (n // 2 + 1))
                if n >= 2:
                    use = last_use[stream[n - 2][0]]
                    wait_full(pool, "T" if use[0] in RINGS["T"] else "M", use)
                hi, lo, raw = w_hi[:, n % 2, 0:width], w_lo[:, n % 2, 0:width], w_raw[:, n % 2, 0:width]
                link(g.tensor_scalar(hi, raw, 1.0, 0.0, ALU.mult, ALU.add))
                g.tensor_tensor(lo, raw, hi.bitcast(F32), ALU.subtract).then_inc(sem("w_split"), 1)
                split_upto[0] += 1

            split_next()
            split_next()
            for step in STEPS:
                kind = step[0]
                if kind == "qkv2" and step[1:] == (0, 0, 0):
                    wait_read(pool, "M", ("wo1", NC - 1, TC // 2 - 1))
                    g.memset(neg_max, 0.0)
                    link(g.memset(pick.bitcast(F32), 0.0))
                    for i in (0, 1):
                        ins = g.affine_select(out=pick[:, i], in_=pick[:, i].bitcast(F32), compare_op=ALU.not_equal, fill=1.0,
                                              base=-i, pattern=[[0, P]], channel_multiplier=1)
                    ins.then_inc(sem("pick_ready"), 1)
                if kind == "score2":
                    u, sbk = step[1], step[2]
                    c = u[0]
                    off = max(0, sbk - TC * c) * P
                    n = nth[step]
                    wait_read(pool, "T", step)
                    pr = probs[:, n % 2]
                    if sbk == 0:
                        if u == (c, 0, 0):
                            wait_full(pool, "M", ("kT2", c, KV2 - 1))
                        elif nth[("out2", u)] > 1:
                            wait_full(pool, "M", outs[nth[("out2", u)] - 2], 1)
                        g.tensor_scalar(p_sum, pr, 1.0, 0.0, ALU.mult, ALU.add).then_inc(sem("p_sum"), 1)
                    else:
                        pool.wait_ge(sem("p_sum"), n - 1)
                        g.tensor_tensor(p_sum[:, :, off:CH], p_sum[:, :, off:CH], pr[:, :, off:CH],
                                        ALU.add).then_inc(sem("p_sum"), 1)
                if kind == "gateup":
                    n = nth[step]
                    s = n % 2
                    pool.wait_ge(sem("act_hi"), n)
                    if n >= 3:
                        wait_full(pool, "M", ("down",) + gus[n - 3][1:] + (TC // 2 - 1,))
                    m = I1 if step[1] == 0 else I2
                    g.tensor_tensor(aTl[0:m, s], act[0:m, s], aTh[0:m, s].bitcast(F32), ALU.subtract)\
                        .then_inc(sem("act_lo"), 1)
                if kind == "scan":
                    n = nth[step]
                    if n == 1:
                        pool.wait_ge(sem("bc_ready"), 1)
                    if n >= 3:
                        pool.wait_ge(sem("scan_summed"), n - 2)
                    col = step[1] * NST + step[2]
                    g.tensor_scalar(diag[:, n % 2], ident[:], bc_s[:, col:col + 1], 1.0, ALU.mult, ALU.mult)\
                        .then_inc(sem("diag_ready"), 1)
                for _ in after.get(step, ()):
                    split_next()

        @block.scalar
        def _(sc):
            s_ = nc.scalar
            chained = [0]

            def link(ins):
                chained[0] += 1
                ins.then_inc(sem("act_chain"), 1)
                sc.wait_ge(sem("act_chain"), chained[0])

            def full(ring, use, i=0):
                return wait_full(sc, ring, use, i)

            def read(ring, slot, ins):
                ins.then_inc(sem(f"{ring}_read{slot}"), 1)

            sc.wait_ge(sem("consts_loaded"), 16 * 6)
            roots, squares = 0, 0
            for step in STEPS:
                kind = step[0]
                if kind == "norm":
                    for _ in range(1 + (step[1] == 1)):
                        roots += 1
                        sc.wait_ge(sem("var_ready"), roots)
                        s_.activation(rs[:, 1, :], rs[:, 0, :], ACT.Sqrt).then_inc(sem("root_ready"), 1)
                elif kind == "normT":
                    _, st, c, k = step
                    m = full("M", step)
                    s_.activation(xTh[:, k, c * CH:(c + 1) * CH], psM[m][:], ACT.Identity,
                                  scale=lnw[:, st, k:k + 1]).then_inc(sem("xTh_ready"), 1)
                elif kind == "qkv1":
                    t = step[1]
                    i = t % TC
                    wait_read(sc, "T", step)
                    if t == 0:
                        sc.wait_ge(sem("consts_ready"), 1)
                    q3 = qkv_tok[:, 0:D].rearrange("p (h d) -> p h d", d=HD1)
                    k3 = qkv_tok[:, D:2 * D].rearrange("p (h d) -> p h d", d=HD1)
                    v3 = qkv_tok[:, 2 * D:3 * D].rearrange("p (h d) -> p h d", d=HD1)
                    s_.activation(q_stack[:, i, :, 0:16].bitcast(F32R), q3, ACT.Copy, scale=HD1 ** -0.5)
                    s_.activation(q_stack[:, i, :, 32:48].bitcast(F32R), q3, ACT.Copy, scale=HD1 ** -0.5)
                    if t >= 1:
                        wait_full(sc, "M", ("kT1", t - 1, 1))
                    s_.activation(k_stack[:, :, 0:16].bitcast(F32R), k3, ACT.Copy)
                    s_.activation(k_stack[:, :, 16:32].bitcast(F32R), k3, ACT.Copy)
                    s_.activation(v_aug[:, t, :, 0:HD1], v3, ACT.Copy).then_inc(sem("stack_hi"), 1)
                elif kind == "kT1":
                    t, half = step[1], step[2]
                    m = full("M", step)
                    ins = s_.activation(kT1[:, 4 * half:4 * half + 4, t * P:(t + 1) * P],
                                        psM[m][:].rearrange("p (a b) -> p a b", b=P), ACT.Copy)
                    read("M", m, ins)
                elif kind == "qT1":
                    p = step[2]
                    m = full("M", step)
                    read("M", m, s_.activation(qT1[0:64, 2 * p, :], psM[m][0:64, :], ACT.Copy))
                elif kind == "score1":
                    _, c, g, sbk, i = step
                    n = nth[step]
                    t = full("T", step)
                    if n >= 3:
                        sc.wait_ge(sem("pv1_done"), n - 2)
                    off = max(0, sbk - TC * c) * P
                    read("T", t, s_.activation(probs[:, n % 2, :, off:CH], psT[t][:, :, off:CH], ACT.Exp))
                elif kind == "out1":
                    _, c, g = step
                    o = tab["O"][("o1", c, g)][0][0]
                    sc.wait_ge(sem("pv1_done"), nth[("pv1", c, g, TC * c + TC - 1, 1)])
                    if nth[step] > 1:
                        wait_full(sc, "M", ("out1", c, g - 1) if g else ("out1", c - 1, 3))
                    s_.activation(o1_T, psO[:, o], ACT.Copy).then_inc(sem("o1_out"), 1)
                elif kind == "aT1":
                    _, c, k = step
                    m = full("M", step)
                    s_.activation(xTh[:, k, c * CH:(c + 1) * CH], psM[m][:], ACT.Copy).then_inc(sem("aT1_hi"), 1)
                elif kind == "qkv2":
                    _, c, g, tp = step
                    t = full("T", step)
                    if g == 1:
                        read("T", t, s_.activation(v_tok[:, TC * c + 2 * tp:TC * c + 2 * tp + 2], psT[t][:], ACT.Copy))
                    else:
                        if squares:
                            sc.wait_ge(sem("ssq_ready"), squares)
                        squares += 1
                        link(s_.activation(rec2, psT[t][:, 0], ACT.Square, accum_out=ssq[:, 2 * tp, g:g + 1]))
                        s_.activation(rec2, psT[t][:, 1], ACT.Square, accum_out=ssq[:, 2 * tp + 1, g:g + 1])\
                            .then_inc(sem("ssq_ready"), 1)
                elif kind == "rms2":
                    sc.wait_ge(sem("ms_ready"), nth[step])
                    s_.activation(rs[:, 1, :], rs[:, 0, :], ACT.Sqrt)
                    s_.activation(mv[:, :, 1], mv[:, :, 0], ACT.Sqrt).then_inc(sem("ms_root"), 1)
                elif kind == "rope":
                    _, c, t, which = step
                    if which == "k" and t == 0:
                        sc.wait_ge(sem("r_ready"), nth[("rms2", c)])
                    tok, r_ = (q_tok[:, t], rs[:, 2, t:t + 1]) if which == "q" else (k_tok[:, t], rs[:, 1, t:t + 1])
                    s_.activation(tok[:, :, RD:DH2], tok[:, :, RD:DH2], ACT.Copy, scale=r_).then_inc(sem("pass_scaled"), 1)
                elif kind == "kT2":
                    _, c, j = step
                    m = full("M", step)
                    s_.activation(kTh[:, j, c * CH:(c + 1) * CH], psM[m][:], ACT.Copy).then_inc(sem("kT2_hi"), 1)
                elif kind == "qT2":
                    u, i = step[1], step[2]
                    m = full("M", step)
                    n = nth[("mT2", u)]
                    s_.activation(qTh[:, n % 2, i], psM[m][:], ACT.Copy).then_inc(sem("qT2_hi"), 1)
                elif kind == "mT2":
                    m = full("M", step)
                    read("M", m, s_.activation(negmT, psM[m][:], ACT.Copy))
                elif kind == "score2":
                    _, u, sbk = step
                    n = nth[step]
                    t = full("T", step)
                    if n >= 3:
                        sc.wait_ge(sem("pv2_done"), n - 2)
                        sc.wait_ge(sem("p_sum"), n - 2)
                    off = max(0, sbk - TC * u[0]) * P
                    read("T", t, s_.activation(probs[:, n % 2, :, off:CH], psT[t][:, :, off:CH], ACT.Exp))
                elif kind == "out2":
                    u = step[1]
                    n = nth[step]
                    c = u[0]
                    sc.wait_ge(sem("pv2_done"), nth[("pv2", u, TC * c + TC - 1)])
                    if n > 1:
                        sc.wait_ge(sem("oT_ready"), n - 1)
                    s_.activation(o_raw, psO[:], ACT.Copy).then_inc(sem("o2_out"), 1)
                elif kind == "router":
                    st = step[1]
                    if st == 0:
                        m = full("M", step)
                        read("M", m, s_.activation(logits[:, :, 0:E1], psM[m][:, 0:NT * E1].rearrange("p (t e) -> p t e", e=E1),
                                                   ACT.Sigmoid))
                    else:
                        wait_read(sc, "M", step)
                        s_.activation(rt, logits, ACT.Exp).then_inc(sem("logits_out"), 1)
                elif kind == "gateup":
                    _, st, e, c = step
                    n = nth[step]
                    s = n % 2
                    m = I1 if st == 0 else I2
                    t = full("T", step)
                    if n >= 3:
                        wait_read(sc, "T", gus[n - 3])
                    s_.activation(gate[0:m, s], psT[t][0:m, 0], ACT.Silu).then_inc(sem("silu"), 1)
                    wait_read(sc, "T", step)
                    if n >= 3:
                        wait_full(sc, "M", ("down",) + gus[n - 3][1:] + (TC // 2 - 1,))
                    s_.activation(aTh[0:m, s], act[0:m, s], ACT.Copy).then_inc(sem("act_hi"), 1)
                elif kind == "rates":
                    link(s_.activation(sp_s[:, 0], mats[:, 0], ACT.Abs))
                    s_.activation(sp_s[:, 1], sp_s[:, 0], ACT.Exp, scale=-1.0).then_inc(sem("rate_exp"), 1)
                    sc.wait_ge(sem("rate_one"), 1)
                    s_.activation(sp_s[:, 0], sp_s[:, 2], ACT.Ln).then_inc(sem("rate_log"), 1)
                elif kind == "proj":
                    _, w, ob = step
                    if w == 0:
                        wait_read(sc, "T", step)
                        if ob:
                            sc.wait_ge(sem("dt_ready"), ob)
                        link(s_.activation(sp_a, dtT[:, ob], ACT.Abs))
                        s_.activation(sp_b, sp_a, ACT.Exp, scale=-1.0).then_inc(sem("sp_exp"), 1)
                        sc.wait_ge(sem("sp_one"), ob + 1)
                        s_.activation(sp_a, sp_c, ACT.Ln).then_inc(sem("sp_log"), 1)
                elif kind == "scan":
                    _, ob, k = step
                    n = nth[step]
                    if n == 1:
                        sc.wait_ge(sem("dt_ready"), KD)
                    if n >= 3:
                        sc.wait_ge(sem("scanned"), n - 2)
                    s_.activation(decay[:, n % 2], dtT[:, ob], ACT.Exp,
                                  scale=neg_a[:, ob * NST + k:ob * NST + k + 1]).then_inc(sem("decay_ready"), 1)

        @block.vector
        def _(ve):
            v = nc.vector
            chained = [0]

            def link(ins):
                chained[0] += 1
                ins.then_inc(sem("dve_chain"), 1)
                ve.wait_ge(sem("dve_chain"), chained[0])

            def full(ring, use, i=0):
                return wait_full(ve, ring, use, i)

            def read(ring, slot, ins):
                ins.then_inc(sem(f"{ring}_read{slot}"), 1)

            def stats(src, c):
                for i in range(TC):
                    v_ins = v.bn_stats(bn6[:, i], src(i))
                link(v_ins)
                for i in range(TC):
                    v_ins = v.bn_aggr(mv[:, i], bn6[:, i])
                link(v_ins)

            roots = 0

            def root():
                nonlocal roots
                roots += 1
                ve.wait_ge(sem("root_ready"), roots)
                link(v.reciprocal(rs[:, 2, :], rs[:, 1, :]))

            def layernorm(c, dst):
                stats(lambda i: x[:, TC * c + i], c)
                v.tensor_scalar(rs[:, 0, :], mv[:, :, 1], 1e-5, None, ALU.add).then_inc(sem("var_ready"), 1)
                root()
                for i in range(TC):
                    ins = v.tensor_scalar(dst(i), x[:, TC * c + i], mv[:, i, 0:1], rs[:, 2, i:i + 1],
                                          ALU.subtract, ALU.mult)
                return ins

            def rmsnorm(c):
                stats(lambda i: xn[:, TC * c + i], c)
                link(v.tensor_tensor(rs[:, 1, :], mv[:, :, 0], mv[:, :, 0], ALU.mult))
                v.scalar_tensor_tensor(rs[:, 0, :], rs[:, 1, :], 1e-6, mv[:, :, 1], ALU.add, ALU.add)\
                    .then_inc(sem("var_ready"), 1)
                root()
                for i in range(TC):
                    ins = v.tensor_scalar(normed[:, i], xn[:, TC * c + i], rs[:, 2, i:i + 1], None, ALU.mult)
                return ins

            v.memset(psO[:], 0.0).then_inc(sem("psO_clear"), 1)
            ve.wait_ge(sem("x_loaded"), 16)
            ve.wait_ge(sem("consts_loaded"), 16 * 6)
            for step in STEPS:
                kind = step[0]
                if kind == "norm":
                    _, st, c = step
                    if st == 1:
                        wait_read(ve, "M", ("wo1", c, TC // 2 - 1))
                    elif st == 2:
                        wait_read(ve, "M", ("wo2", (c, KV2 - 1, 1), TC // 2 - 1))
                    elif st == 3:
                        wait_read(ve, "M", ("down", 0, E1 - 1, NC - 1, TC // 2 - 1))
                    elif st == 4:
                        wait_read(ve, "M", ("yT", NT // 2 - 1))
                    if st in (0, 3, 4):
                        layernorm(c, lambda i: normed[:, i]).then_inc(sem("normed_ready"), 1)
                    elif st == 1:
                        link(layernorm(c, lambda i: xn[:, TC * c + i]))
                        rmsnorm(c).then_inc(sem("normed_ready"), 1)
                    else:
                        rmsnorm(c).then_inc(sem("normed_ready"), 1)
                        for i in range(TC):
                            t = TC * c + i
                            ins = v.tensor_tensor(x[:, t], x[:, t], xn[:, t], ALU.add)
                        link(ins)
                elif kind == "normT":
                    _, st, c, k = step
                    m = full("M", step)
                    ve.wait_ge(sem("xTh_ready"), nth[step])
                    cols = slice(c * CH, (c + 1) * CH)
                    if st == 3:
                        link(v.tensor_copy(uT[:, k, cols], psM[m][:]))
                    read("M", m, v.scalar_tensor_tensor(xTl[:, k, cols], psM[m][:], lnw[:, st, k:k + 1],
                                                        xTh[:, k, cols].bitcast(F32), ALU.mult, ALU.subtract))
                elif kind == "qkv1":
                    t = step[1]
                    i = t % TC
                    s = full("T", step)
                    if t >= 1:
                        ve.wait_ge(sem("stack_hi"), t)
                        ve.wait_ge(sem("stack_lo"), t)
                    read("T", s, v.tensor_tensor(qkv_tok, psT[s][:].rearrange("p a b -> p (a b)")[:, 0:3 * D], bqkv_b, ALU.add))
                    ve.wait_ge(sem("stack_hi"), nth[step])
                    q3 = qkv_tok[:, 0:D].rearrange("p (h d) -> p h d", d=HD1)
                    k3 = qkv_tok[:, D:2 * D].rearrange("p (h d) -> p h d", d=HD1)
                    if t >= TC:
                        v.memset(q_stack[:, i, :, 48:49], 0.0)
                    v.scalar_tensor_tensor(q_stack[:, i, :, 16:32].bitcast(F32R), q3, HD1 ** -0.5,
                                           q_stack[:, i, :, 0:16], ALU.mult, ALU.subtract)
                    v.tensor_tensor(k_stack[:, :, 32:48].bitcast(F32R), k3, k_stack[:, :, 0:16], ALU.subtract)\
                        .then_inc(sem("stack_lo"), 1)
                elif kind == "qT1":
                    p = step[2]
                    m = full("M", step)
                    read("M", m, v.tensor_copy(qT1[64:P, 2 * p + 1, :], psM[m][64:P, :]))
                elif kind == "max1":
                    _, c, t, p, i = step
                    s = full("T", step)
                    w = (t + 1) * P
                    if i is None:
                        dst = q_stack[:, t % TC, 2 * p:2 * p + 2, 48]
                        src = psT[s][:, :, 0:w]
                    else:
                        dst = q_stack[:, t % TC, 2 * p + i, 48:49]
                        src = psT[s][:].rearrange("p a b -> p (a b)")[:, 0:w]
                    read("T", s, v.tensor_reduce(dst, src, X_AXIS, ALU.max, negate=True))
                elif kind == "out1":
                    _, c, g = step
                    m = full("M", step)
                    o4 = psM[m][:].rearrange("p (t h e) -> p t h e", t=TC, h=4)
                    if nth[step] > 1:
                        wait_read(ve, "M", ("out1", c, g - 1) if g else ("out1", c - 1, 3))
                    link(v.reciprocal(den1, o4[:, :, :, HD1]))
                    read("M", m, v.tensor_tensor(a_tok.rearrange("p t (h d) -> p t h d", d=HD1)[:, :, 4 * g:4 * g + 4],
                                         o4[:, :, :, 0:HD1],
                                         den1.unsqueeze(3).to_broadcast([P, TC, 4, HD1]), ALU.mult))
                elif kind == "aT1":
                    _, c, k = step
                    m = full("M", step)
                    ve.wait_ge(sem("aT1_hi"), nth[step])
                    read("M", m, v.tensor_tensor(xTl[:, k, c * CH:(c + 1) * CH], psM[m][:],
                                         xTh[:, k, c * CH:(c + 1) * CH].bitcast(F32), ALU.subtract))
                elif kind == "wo1":
                    _, c, tp = step
                    m = full("M", step)
                    for i in (0, 1):
                        t = TC * c + 2 * tp + i
                        ins = v.tensor_tensor(x[:, t], x[:, t], bo_b, ALU.add)
                    link(ins)
                    t = TC * c + 2 * tp
                    read("M", m, v.tensor_tensor(x[:, t:t + 2], x[:, t:t + 2], psM[m][:].rearrange("p (a b) -> p a b", b=D), ALU.add))
                elif kind == "qkv2":
                    _, c, g, tp = step
                    if g == 1:
                        continue
                    s = full("T", step)
                    rows = 5 * c + (0 if g == 0 else g - 1)
                    ve.wait_ge(sem(f"row_loaded{rows % 2}"), 16 * (rows // 2 + 1))
                    ve.wait_ge(sem("ssq_ready"), 2 * rows + tp + 1)
                    if c == 1 and g == 0 and tp == 0:
                        ve.wait_ge(sem("oT_ready"), 2 * KV2)
                    if g == 0:
                        dst = k_tok[:, 2 * tp:2 * tp + 2].rearrange("p a b c -> p a (b c)")
                    else:
                        dst = q_tok[:, 2 * tp:2 * tp + 2, 4 * (g - 2):4 * (g - 2) + 4].rearrange("p a b c -> p a (b c)")
                    read("T", s, v.tensor_tensor(dst, psT[s][:], qkw[:, rows % 2].unsqueeze(1).to_broadcast([P, 2, CH]), ALU.mult))
                elif kind == "rms2":
                    c = step[1]
                    link(v.tensor_reduce(rs[:, 0, :], ssq[:, :, 2:6], X_AXIS, ALU.add))
                    v.tensor_scalar(mv[:, :, 0], ssq[:, :, 0], 1.0 / (KV2 * DH2), 1e-6, ALU.mult, ALU.add)
                    v.tensor_scalar(rs[:, 0, :], rs[:, 0, :], 1.0 / (H2 * DH2), 1e-6, ALU.mult, ALU.add)\
                        .then_inc(sem("ms_ready"), 1)
                    ve.wait_ge(sem("ms_root"), nth[step])
                    link(v.reciprocal(rs[:, 2, :], rs[:, 1, :]))
                    v.tensor_scalar(rs[:, 2, :], rs[:, 2, :], DH2 ** -0.5, None, ALU.mult)
                    v.reciprocal(rs[:, 1, :], mv[:, :, 1]).then_inc(sem("r_ready"), 1)
                    ve.wait_ge(sem("r_ready"), nth[step])
                elif kind == "rope":
                    _, c, t, which = step
                    if c == 0 and which == "k" and t == 0:
                        ve.wait_ge(sem("tables_loaded"), 32)
                    nh = H2 if which == "q" else KV2
                    tok, r_ = (q_tok[:, t], rs[:, 2, t:t + 1]) if which == "q" else (k_tok[:, t], rs[:, 1, t:t + 1])
                    HR = RD // 2
                    t1 = probs[:, 0].rearrange("p a b -> p (a b)")[:, 0:nh * RD].rearrange("p (h d) -> p h d", d=RD)
                    t2 = probs[:, 1].rearrange("p a b -> p (a b)")[:, 0:nh * RD].rearrange("p (h d) -> p h d", d=RD)
                    ct = cos_t[:, TC * c + t].unsqueeze(1).to_broadcast([P, nh, RD])
                    sn = sin_t[:, TC * c + t].unsqueeze(1)
                    if nth[step] > 1:
                        ve.wait_ge(sem("roped"), nth[step] - 1)
                    v.scalar_tensor_tensor(t1, tok[:, :, 0:RD], r_, ct, ALU.mult, ALU.mult)
                    v.scalar_tensor_tensor(t2[:, :, 0:HR], tok[:, :, HR:RD], r_,
                                           sn[:, :, 0:HR].to_broadcast([P, nh, HR]), ALU.mult, ALU.mult)
                    link(v.scalar_tensor_tensor(t2[:, :, HR:RD], tok[:, :, 0:HR], r_,
                                                sn[:, :, HR:RD].to_broadcast([P, nh, HR]), ALU.mult, ALU.mult))
                    v.tensor_tensor(tok[:, :, 0:RD], t1, t2, ALU.add).then_inc(sem("roped"), 1)
                elif kind == "kT2":
                    _, c, j = step
                    m = full("M", step)
                    ve.wait_ge(sem("kT2_hi"), nth[step])
                    cols = slice(c * CH, (c + 1) * CH)
                    read("M", m, v.tensor_tensor(kTl[:, j, cols], psM[m][:], kTh[:, j, cols].bitcast(F32), ALU.subtract))
                elif kind == "qT2":
                    u, i = step[1], step[2]
                    m = full("M", step)
                    n = nth[("mT2", u)]
                    ve.wait_ge(sem("qT2_hi"), nth[step])
                    read("M", m, v.tensor_tensor(qTl[:, n % 2, i], psM[m][:], qTh[:, n % 2, i].bitcast(F32), ALU.subtract))
                elif kind == "max2":
                    _, u, t, i = step
                    s = full("T", step)
                    if t == TC * u[0] and i in (None, 0):
                        if nth[("mT2", u)] == 1:
                            ve.wait_ge(sem("pick_ready"), 1)
                        else:
                            wait_full(ve, "M", mts[nth[("mT2", u)] - 2])
                    w = (t + 1) * P
                    if i is None:
                        dst, src = neg_max[:, t % TC, 0:2], psT[s][:, :, 0:w]
                    else:
                        dst, src = neg_max[:, t % TC, i:i + 1], psT[s][:].rearrange("p a b -> p (a b)")[:, 0:w]
                    read("T", s, v.tensor_reduce(dst, src, X_AXIS, ALU.max, negate=True))
                elif kind == "out2":
                    u = step[1]
                    n = nth[step]
                    ve.wait_ge(sem("o2_out"), n)
                    for i in (0, 1):
                        m = full("M", step, i)
                        read("M", m, v.reciprocal(rec2, psM[m][:]))
                        wait_read(ve, "M", step, i)
                        link(v.tensor_tensor(o_raw[:, i], o_raw[:, i], rec2, ALU.mult))
                    link(v.tensor_copy(oTh, o_raw))
                    v.tensor_tensor(oTl, o_raw, oTh.bitcast(F32), ALU.subtract).then_inc(sem("oT_ready"), 1)
                elif kind == "wo2":
                    _, u, tp = step
                    m = full("M", step)
                    t = TC * u[0] + 2 * tp
                    read("M", m, v.tensor_tensor(xn[:, t:t + 2], xn[:, t:t + 2], psM[m][:].rearrange("p (a b) -> p a b", b=D), ALU.add))
                elif kind == "router":
                    st = step[1]
                    if st == 0:
                        wait_read(ve, "M", step)
                        link(v.tensor_tensor(rt[:, :, 0:E1], logits[:, :, 0:E1],
                                             rbias[:].unsqueeze(1).to_broadcast([P, NT, E1]), ALU.add))
                    else:
                        m = full("M", step)
                        lg = psM[m][:, 0:NT * E2].rearrange("p (t e) -> p t e", e=E2)
                        link(v.tensor_reduce(tok1, lg, X_AXIS, ALU.max))
                        read("M", m, v.tensor_tensor(logits, lg, tok1.unsqueeze(2).to_broadcast([P, NT, E2]), ALU.subtract))
                        ve.wait_ge(sem("logits_out"), 1)
                        link(v.tensor_reduce(tok1, rt, X_AXIS, ALU.add))
                        link(v.reciprocal(tok1, tok1))
                        link(v.tensor_tensor(rt, rt, tok1.unsqueeze(2).to_broadcast([P, NT, E2]), ALU.mult))
                    e_n, top = (E1, TOP1) if st == 0 else (E2, TOP2)
                    for t in range(NT):
                        ins = v.max(top8[:, t], rt[:, t, 0:e_n])
                    link(ins)
                    for t in range(NT):
                        ins = v.max_index(idx_u[:, t].bitcast(U32), top8[:, t], rt[:, t, 0:e_n])
                    link(ins)
                    link(v.tensor_copy(idx_f, idx_u.bitcast(U32)))
                    for j in range(top):
                        ins = v.tensor_tensor(onehot[:, :, j, 0:e_n], iota[:, 0:e_n].unsqueeze(1).to_broadcast([P, NT, e_n]),
                                              idx_f[:, :, j:j + 1].to_broadcast([P, NT, e_n]), ALU.is_equal)
                    link(ins)
                    if st == 0:
                        link(v.tensor_tensor(comb[:, :, 0:E1], onehot[:, :, 0, 0:E1], onehot[:, :, 1, 0:E1], ALU.add))
                        link(v.tensor_tensor(comb[:, :, 0:E1], comb[:, :, 0:E1], logits[:, :, 0:E1], ALU.mult))
                        link(v.tensor_reduce(tok1, comb[:, :, 0:E1], X_AXIS, ALU.add))
                        link(v.reciprocal(tok1, tok1))
                        link(v.tensor_tensor(comb[:, :, 0:E1], comb[:, :, 0:E1],
                                             tok1.unsqueeze(2).to_broadcast([P, NT, E1]), ALU.mult))
                    else:
                        link(v.tensor_reduce(tok1, top8, X_AXIS, ALU.add))
                        link(v.tensor_scalar(tok1, tok1, 1e-12, None, ALU.max))
                        link(v.reciprocal(tok1, tok1))
                        link(v.tensor_tensor(cum, top8, tok1.unsqueeze(2).to_broadcast([P, NT, 8]), ALU.mult))
                        for j in range(1, TOP2):
                            link(v.tensor_tensor(cum[:, :, j], cum[:, :, j], cum[:, :, j - 1], ALU.add))
                        link(v.tensor_scalar(cum, cum, THRESHOLD, None, ALU.is_lt))
                        link(v.tensor_tensor(top8[:, :, 1:8], top8[:, :, 1:8], cum[:, :, 0:7], ALU.mult))
                        link(v.tensor_reduce(tok1, top8, X_AXIS, ALU.add))
                        link(v.tensor_scalar(tok1, tok1, 1e-12, None, ALU.max))
                        link(v.reciprocal(tok1, tok1))
                        link(v.tensor_tensor(top8, top8, tok1.unsqueeze(2).to_broadcast([P, NT, 8]), ALU.mult))
                        for j in range(top):
                            ins = v.tensor_tensor(onehot[:, :, j], onehot[:, :, j],
                                                  top8[:, :, j:j + 1].to_broadcast([P, NT, E2]), ALU.mult)
                        link(ins)
                        link(v.tensor_tensor(onehot[:, :, 0:4], onehot[:, :, 0:4], onehot[:, :, 4:8], ALU.add))
                        link(v.tensor_tensor(onehot[:, :, 0:2], onehot[:, :, 0:2], onehot[:, :, 2:4], ALU.add))
                        link(v.tensor_tensor(comb, onehot[:, :, 0], onehot[:, :, 1], ALU.add))
                elif kind == "gateup":
                    _, st, e, c = step
                    n = nth[step]
                    s = n % 2
                    m = I1 if st == 0 else I2
                    t = full("T", step)
                    ve.wait_ge(sem("silu"), n)
                    if n >= 3:
                        ve.wait_ge(sem("act_lo"), n - 2)
                    read("T", t, v.tensor_tensor(act[0:m, s], gate[0:m, s], psT[t][0:m, 1], ALU.mult))
                elif kind == "down":
                    _, st, e, c, tp = step
                    m = full("M", step)
                    for i in (0, 1):
                        t = TC * c + 2 * tp + i
                        ins = v.scalar_tensor_tensor(x[:, t], psM[m][:, i * D:(i + 1) * D], comb[:, t, e:e + 1], x[:, t],
                                                     ALU.mult, ALU.add)
                        if i == 0:
                            pass
                    read("M", m, ins)
                elif kind == "rates":
                    ve.wait_ge(sem("rate_exp"), 1)
                    v.tensor_tensor(bc_s[:], mats[:, 1], mats[:, 2], ALU.mult).then_inc(sem("bc_ready"), 1)
                    v.tensor_scalar(sp_s[:, 2], sp_s[:, 1], 1.0, None, ALU.add).then_inc(sem("rate_one"), 1)
                    ve.wait_ge(sem("rate_one"), 1)
                    link(v.scalar_tensor_tensor(sp_s[:, 1], sp_s[:, 2], -1.0, sp_s[:, 1], ALU.add, ALU.subtract))
                    ve.wait_ge(sem("rate_log"), 1)
                    link(v.tensor_tensor(sp_s[:, 0], sp_s[:, 0], sp_s[:, 1], ALU.subtract))
                    link(v.scalar_tensor_tensor(sp_s[:, 0], mats[:, 0], 0.0, sp_s[:, 0], ALU.max, ALU.add))
                    link(v.tensor_scalar(neg_a[:], sp_s[:, 0], -1.0, None, ALU.mult))
                elif kind == "proj":
                    _, w, ob = step
                    t = full("T", step)
                    src = psT[t][:].rearrange("p a b -> p (a b)")
                    if w == 0:
                        read("T", t, v.tensor_scalar(dtT[:, ob], src, vecs[:, 0, ob:ob + 1], None, ALU.add))
                        ve.wait_ge(sem("sp_exp"), ob + 1)
                        v.tensor_scalar(sp_c, sp_b, 1.0, None, ALU.add).then_inc(sem("sp_one"), 1)
                        ve.wait_ge(sem("sp_one"), ob + 1)
                        link(v.scalar_tensor_tensor(sp_b, sp_c, -1.0, sp_b, ALU.add, ALU.subtract))
                        ve.wait_ge(sem("sp_log"), ob + 1)
                        link(v.tensor_tensor(sp_b, sp_a, sp_b, ALU.subtract))
                        link(v.scalar_tensor_tensor(sp_b, dtT[:, ob], 0.0, sp_b, ALU.max, ALU.add))
                        v.tensor_scalar(dtT[:, ob], sp_b, DT_MIN, None, ALU.add).then_inc(sem("dt_ready"), 1)
                        ve.wait_ge(sem("dt_ready"), ob + 1)
                    elif w == 1:
                        read("T", t, v.scalar_tensor_tensor(bT[:, ob], src, vecs[:, 1, ob:ob + 1], dtT[:, ob], ALU.add, ALU.mult))
                        wait_read(ve, "T", step)
                        link(v.tensor_tensor(bT[:, ob], bT[:, ob], uT[:, ob], ALU.mult))
                    else:
                        read("T", t, v.tensor_scalar(cT[:, ob], src, vecs[:, 2, ob:ob + 1], None, ALU.add))
                elif kind == "scan":
                    _, ob, k = step
                    n = nth[step]
                    ve.wait_ge(sem("decay_ready"), n)
                    if n >= 3:
                        ve.wait_ge(sem("scan_summed"), n - 2)
                    v.tensor_tensor_scan(state[:, n % 2], decay[:, n % 2], bT[:, ob], 0.0, ALU.mult, ALU.add)\
                        .then_inc(sem("scanned"), 1)
                elif kind == "y":
                    ob = step[1]
                    ve.wait_ge(sem("scan_summed"), nth[("scan", ob, NST - 1)])
                    link(v.tensor_tensor(cT[:, ob], psO[:].rearrange("p a b -> p (a b)"), cT[:, ob], ALU.mult))
                    v.scalar_tensor_tensor(yT[:, ob], uT[:, ob], vecs[:, 3, ob:ob + 1], cT[:, ob], ALU.mult, ALU.add)\
                        .then_inc(sem("y_ready"), 1)
                elif kind == "yT":
                    tp = step[1]
                    m = full("M", step)
                    read("M", m, v.tensor_tensor(x[:, 2 * tp:2 * tp + 2], x[:, 2 * tp:2 * tp + 2],
                                         psM[m][:].rearrange("p (a b) -> p a b", b=D), ALU.add))

        @block.tensor
        def _(pe):
            mm = nc.tensor.matmul
            tr = nc.tensor.transpose

            def take(ring, key, i=0):
                slot, releases, _, _ = tab[ring][key][i]
                if releases:
                    pe.wait_ge(sem(f"{ring}_read{slot}"), releases)
                return slot

            def filled(ring, slot, ins):
                ins.then_inc(sem(f"{ring}_full{slot}"), 1)

            def weights(name):
                n = order[name]
                pe.wait_ge(sem("w_split"), n + 1)
                return w_hi[:, n % 2], w_lo[:, n % 2]

            def three(out, hi, lo, rhi, rlo, start=True, stop=True):
                mm(out, hi, rlo, start=start, stop=False)
                mm(out, lo, rhi, start=False, stop=False)
                return mm(out, hi, rhi, start=False, stop=stop)

            pe.wait_ge(sem("consts_ready"), 1)
            pe.wait_ge(sem("psO_clear"), 1)
            for step in STEPS:
                kind = step[0]
                if kind == "normT":
                    _, st, c, k = step
                    pe.wait_ge(sem("normed_ready"), nth[("norm", st, c)])
                    m = take("M", step)
                    for i in range(TC):
                        ins = tr(psM[m][:, i * P:(i + 1) * P], normed[:, i, k * P:(k + 1) * P], ident[:])
                    filled("M", m, ins)
                elif kind == "qkv1":
                    t = step[1]
                    c = t // TC
                    wait_read(pe, "M", ("normT", 0, c, KD - 1))
                    s = take("T", step)
                    tc = slice(t * P, (t + 1) * P)
                    wk = [weights(("wqkv", c, k)) for k in range(KD)]
                    for k in range(KD):
                        hi, lo = wk[k]
                        for b, (a0, a1) in enumerate(((0, CH), (CH, 3 * D))):
                            ins = three(psT[s][:, b, 0:a1 - a0], xTh[:, k, tc], xTl[:, k, tc], hi[:, a0:a1], lo[:, a0:a1],
                                        start=k == 0, stop=k == KD - 1)
                        if k == KD - 1:
                            filled("T", s, ins)
                elif kind == "kT1":
                    t, half = step[1], step[2]
                    pe.wait_ge(sem("stack_lo"), t + 1)
                    m = take("M", step)
                    ks = k_stack.rearrange("p h e -> p (h e)")
                    for j in range(4):
                        a0 = (4 * half + j) * P
                        ins = tr(psM[m][:, j * P:(j + 1) * P], ks[:, a0:a0 + P], ident[:])
                    filled("M", m, ins)
                elif kind == "qT1":
                    _, c, p, again = step
                    pe.wait_ge(sem("stack_lo"), TC * (c + 1))
                    if again:
                        for use in [k for k in tab["T"] if k[0] == "max1" and k[1] == c and k[3] == p][-2:]:
                            wait_read(pe, "T", use)
                    m = take("M", step)
                    qs = q_stack.rearrange("p t h e -> p t (h e)")
                    for i in range(TC):
                        ins = tr(psM[m][:, i * P:(i + 1) * P], qs[:, i, p * P:(p + 1) * P], ident[:])
                    filled("M", m, ins)
                elif kind == "max1":
                    _, c, t, p, i = step
                    for half in (0, 1):
                        wait_read(pe, "M", ("kT1", TC * c + TC - 1, half))
                    wait_read(pe, "M", ("qT1", c, p, 0))
                    s = take("T", step)
                    tc = slice((t % TC) * P, (t % TC + 1) * P)
                    w = (t + 1) * P
                    for b in (0, 1):
                        if i is None:
                            h, a0, a1 = 2 * p + b, 0, w
                        else:
                            h, a0, a1 = 2 * p + i, b * CH, min(w, b * CH + CH)
                        last = a1 == w
                        ins = mm(psT[s][:, b, 0:a1 - a0], qT1[:, h, tc], kT1[:, p, a0:a1], start=True, stop=not last)
                        if last:
                            ins = mm(psT[s][:, b, a1 - a0 - P:a1 - a0], ident_b[:], mask_q[:], start=False, stop=True)
                    filled("T", s, ins)
                elif kind == "score1":
                    _, c, g, sbk, i = step
                    p = 2 * g + i
                    wait_read(pe, "M", ("qT1", c, p, 1))
                    s = take("T", step)
                    diag_block = sbk >= TC * c
                    off = max(0, sbk - TC * c) * P
                    for b in (0, 1):
                        ins = mm(psT[s][:, b, off:CH], kT1[:, p, sbk * P:(sbk + 1) * P], qT1[:, 2 * p + b, off:CH],
                                 start=True, stop=not diag_block)
                        if diag_block:
                            ins = mm(psT[s][:, b, off:off + P], ident_b[:], mask_k[:], start=False, stop=True)
                    filled("T", s, ins)
                elif kind == "pv1":
                    _, c, g, sbk, i = step
                    n = nth[step]
                    wait_read(pe, "T", ("score1",) + step[1:])
                    o = tab["O"][("o1", c, g)][0][0]
                    if sbk == 0 and i == 0 and nth[("out1", c, g)] > 2:
                        pe.wait_ge(sem("o1_out"), nth[("out1", c, g)] - 2)
                    off = max(0, sbk - TC * c) * P
                    for b in (0, 1):
                        h = 4 * g + 2 * i + b
                        q0 = 32 * (2 * i + b)
                        ins = mm(psO[q0:q0 + HD1 + 1, o, off:CH], v_aug[:, sbk, h], probs[:, n % 2, b, off:CH],
                                 start=sbk == 0, stop=sbk == TC * c + TC - 1)
                    ins.then_inc(sem("pv1_done"), 1)
                elif kind == "out1":
                    _, c, g = step
                    pe.wait_ge(sem("o1_out"), nth[step])
                    m = take("M", step)
                    for i in range(TC):
                        ins = tr(psM[m][:, i * P:(i + 1) * P], o1_T[:, i * P:(i + 1) * P], ident[:])
                    filled("M", m, ins)
                elif kind == "aT1":
                    _, c, k = step
                    for g in range(4):
                        wait_read(pe, "M", ("out1", c, g))
                    m = take("M", step)
                    for i in range(TC):
                        ins = tr(psM[m][:, i * P:(i + 1) * P], a_tok[:, i, k * P:(k + 1) * P], ident[:])
                    filled("M", m, ins)
                elif kind == "wo1":
                    _, c, tp = step
                    for k in range(KD):
                        wait_read(pe, "M", ("aT1", c, k))
                    hi, lo = weights(("wo1", c))
                    m = take("M", step)
                    for i in (0, 1):
                        for k in range(KD):
                            tc = slice((TC * c + 2 * tp + i) * P, (TC * c + 2 * tp + i + 1) * P)
                            ins = three(psM[m][:, i * D:(i + 1) * D], xTh[:, k, tc], xTl[:, k, tc],
                                        hi[:, k * D:(k + 1) * D], lo[:, k * D:(k + 1) * D], start=k == 0, stop=k == KD - 1)
                    filled("M", m, ins)
                elif kind == "qkv2":
                    _, c, g, tp = step
                    wait_read(pe, "M", ("normT", 1, c, KD - 1))
                    hi, lo = weights(("w2", c, g))
                    s = take("T", step)
                    for i in (0, 1):
                        t = TC * c + 2 * tp + i
                        tc = slice(t * P, (t + 1) * P)
                        for k in range(KD):
                            ins = three(psT[s][:, i], xTh[:, k, tc], xTl[:, k, tc], hi[:, k * CH:(k + 1) * CH],
                                        lo[:, k * CH:(k + 1) * CH], start=k == 0, stop=k == KD - 1)
                    filled("T", s, ins)
                elif kind == "kT2":
                    _, c, j = step
                    pe.wait_ge(sem("roped"), 2 * TC * c + TC)
                    pe.wait_ge(sem("pass_scaled"), 2 * TC * c + TC)
                    m = take("M", step)
                    for i in range(TC):
                        ins = tr(psM[m][:, i * P:(i + 1) * P], k_tok[:, i, j], ident[:])
                    filled("M", m, ins)
                elif kind == "qT2":
                    u, i = step[1], step[2]
                    c, j, hp = u
                    pe.wait_ge(sem("roped"), 2 * TC * (c + 1))
                    pe.wait_ge(sem("pass_scaled"), 2 * TC * (c + 1))
                    m = take("M", step)
                    for t in range(TC):
                        ins = tr(psM[m][:, t * P:(t + 1) * P], q_tok[:, t, 4 * j + 2 * hp + i], ident[:])
                    filled("M", m, ins)
                elif kind == "max2":
                    _, u, t, i = step
                    c, j, hp = u
                    for h in (0, 1):
                        wait_read(pe, "M", ("qT2", u, h))
                    wait_read(pe, "M", ("kT2", c, KV2 - 2))
                    wait_read(pe, "M", ("kT2", c, KV2 - 1))
                    s = take("T", step)
                    n = nth[("mT2", u)]
                    tc = slice((t % TC) * P, (t % TC + 1) * P)
                    w = (t + 1) * P
                    for b in (0, 1):
                        if i is None:
                            h, a0, a1 = b, 0, w
                        else:
                            h, a0, a1 = i, b * CH, min(w, b * CH + CH)
                        last = a1 == w
                        ins = mm(psT[s][:, b, 0:a1 - a0], qTh[:, n % 2, h, tc], kTh[:, j, a0:a1], start=True, stop=not last)
                        if last:
                            ins = mm(psT[s][:, b, a1 - a0 - P:a1 - a0], ident_b[:], mask_q[:], start=False, stop=True)
                    filled("T", s, ins)
                elif kind == "mT2":
                    u = step[1]
                    keys = [k for k in tab["T"] if k[0] == "max2" and k[1] == u][-2:]
                    for key in keys:
                        wait_read(pe, "T", key)
                    m = take("M", step)
                    for i in range(TC):
                        ins = tr(psM[m][:, i * P:(i + 1) * P], neg_max[:, i], ident[:])
                    filled("M", m, ins)
                elif kind == "score2":
                    _, u, sbk = step
                    c, j, hp = u
                    n = nth[("mT2", u)]
                    wait_read(pe, "M", ("mT2", u))
                    s = take("T", step)
                    diag_block = sbk >= TC * c
                    off = max(0, sbk - TC * c) * P
                    kb = slice(sbk * P, (sbk + 1) * P)
                    for b in (0, 1):
                        out = psT[s][:, b, off:CH]
                        three(out, kTh[:, j, kb], kTl[:, j, kb], qTh[:, n % 2, b, off:CH], qTl[:, n % 2, b, off:CH], stop=False)
                        ins = mm(out, pick[:, b], negmT[:, off:CH], start=False, stop=not diag_block)
                        if diag_block:
                            ins = mm(psT[s][:, b, off:off + P], ident_b[:], mask_k[:], start=False, stop=True)
                    filled("T", s, ins)
                elif kind == "pv2":
                    _, u, sbk = step
                    c, j, hp = u
                    n = nth[step]
                    wait_read(pe, "T", ("score2",) + step[1:])
                    for tp in (0, 1):
                        wait_read(pe, "T", ("qkv2", c, 1, tp))
                    if sbk == 0:
                        if nth[("out2", u)] > 1:
                            pe.wait_ge(sem("o2_out"), nth[("out2", u)] - 1)
                        else:
                            pe.wait_ge(sem("o1_out"), 4 * NC)
                    off = max(0, sbk - TC * c) * P
                    for b in (0, 1):
                        ins = mm(psO[:, b, off:CH], v_tok[:, sbk, j * DH2:(j + 1) * DH2], probs[:, n % 2, b, off:CH],
                                 start=sbk == 0, stop=sbk == TC * c + TC - 1)
                    ins.then_inc(sem("pv2_done"), 1)
                elif kind == "out2":
                    u = step[1]
                    c = u[0]
                    pe.wait_ge(sem("p_sum"), nth[("score2", u, TC * c + TC - 1)])
                    for i in (0, 1):
                        m = take("M", step, i)
                        ins = mm(psM[m][:], ones[:], p_sum[:, i], start=True, stop=True)
                        filled("M", m, ins)
                elif kind == "wo2":
                    _, u, tp = step
                    c, j, hp = u
                    pe.wait_ge(sem("oT_ready"), nth[("out2", u)])
                    hi, lo = weights(("wo2", c, j))
                    m = take("M", step)
                    for i in (0, 1):
                        tc = slice((2 * tp + i) * P, (2 * tp + i + 1) * P)
                        for b in (0, 1):
                            w = slice((2 * hp + b) * D, (2 * hp + b + 1) * D)
                            ins = three(psM[m][:, i * D:(i + 1) * D], oTh[:, b, tc], oTl[:, b, tc], hi[:, w], lo[:, w],
                                        start=b == 0, stop=b == 1)
                    filled("M", m, ins)
                elif kind == "router":
                    st = step[1]
                    e_n = E1 if st == 0 else E2
                    wait_read(pe, "M", ("normT", 2 if st == 0 else 4, NC - 1, KD - 1))
                    hi, lo = weights(("rw", st))
                    m = take("M", step)
                    for t in range(NT):
                        tc = slice(t * P, (t + 1) * P)
                        for k in range(KD):
                            w = slice(k * e_n, (k + 1) * e_n)
                            ins = three(psM[m][:, t * e_n:(t + 1) * e_n], xTh[:, k, tc], xTl[:, k, tc], hi[:, w], lo[:, w],
                                        start=k == 0, stop=k == KD - 1)
                    filled("M", m, ins)
                elif kind == "gateup":
                    _, st, e, c = step
                    hi, lo = weights(("moe", st, e))
                    w_i = I1 if st == 0 else I2
                    s = take("T", step)
                    cols = slice(c * CH, (c + 1) * CH)
                    for b in (0, 1):
                        for k in range(KD):
                            w = slice((2 * k + b) * w_i, (2 * k + b + 1) * w_i)
                            ins = three(psT[s][0:w_i, b], hi[:, w], lo[:, w], xTh[:, k, cols], xTl[:, k, cols],
                                        start=k == 0, stop=k == KD - 1)
                    filled("T", s, ins)
                elif kind == "down":
                    _, st, e, c, tp = step
                    n = nth[("gateup", st, e, c)]
                    w_i = I1 if st == 0 else I2
                    pe.wait_ge(sem("act_lo"), n)
                    hi, lo = weights(("moe", st, e))
                    m = take("M", step)
                    w = slice(2 * KD * w_i, 2 * KD * w_i + D)
                    for i in (0, 1):
                        tc = slice((2 * tp + i) * P, (2 * tp + i + 1) * P)
                        ins = three(psM[m][:, i * D:(i + 1) * D], aTh[0:w_i, n % 2, tc], aTl[0:w_i, n % 2, tc],
                                    hi[0:w_i, w], lo[0:w_i, w])
                    filled("M", m, ins)
                elif kind == "proj":
                    _, w, ob = step
                    wait_read(pe, "M", ("normT", 3, NC - 1, KD - 1))
                    hi, lo = weights(("ssm", w))
                    s = take("T", step)
                    for c in range(NC):
                        cols = slice(c * CH, (c + 1) * CH)
                        for k in range(KD):
                            wc = slice(k * D + ob * P, k * D + (ob + 1) * P)
                            ins = three(psT[s][:, c], hi[:, wc], lo[:, wc], xTh[:, k, cols], xTl[:, k, cols],
                                        start=k == 0, stop=k == KD - 1)
                    filled("T", s, ins)
                elif kind == "scan":
                    _, ob, k = step
                    n = nth[step]
                    if k == 0:
                        if ob == 0:
                            pe.wait_ge(sem("o2_out"), nth[("out2", (NC - 1, KV2 - 1, 1))])
                        else:
                            pe.wait_ge(sem("y_ready"), ob)
                    pe.wait_ge(sem("scanned"), n)
                    pe.wait_ge(sem("diag_ready"), n)
                    for c in range(NC):
                        ins = mm(psO[:, c], diag[:, n % 2], state[:, n % 2, c * CH:(c + 1) * CH],
                                 start=k == 0, stop=k == NST - 1)
                    ins.then_inc(sem("scan_summed"), 1)
                elif kind == "yT":
                    tp = step[1]
                    pe.wait_ge(sem("y_ready"), KD)
                    m = take("M", step)
                    for i in (0, 1):
                        t = 2 * tp + i
                        for ob in range(KD):
                            ins = tr(psM[m][:, i * D + ob * P:i * D + (ob + 1) * P], yT[:, ob, t * P:(t + 1) * P], ident[:])
                    filled("M", m, ins)


def rope_tables():
    import numpy as np
    pos = np.arange(S, dtype=np.float32)
    inv = (1.0 / np.float32(1000000.0) ** (np.arange(0, RD, 2, dtype=np.float32) / RD)).astype(np.float32)
    ang = (pos[:, None] * inv[None, :]).astype(np.float32)
    cos, sin = np.cos(ang), np.sin(ang)
    def lay(t):
        return np.ascontiguousarray(t.astype(np.float32).reshape(NT, P, RD).transpose(1, 0, 2))
    return lay(np.concatenate([cos, cos], 1)), lay(np.concatenate([-sin, sin], 1))


INS = ["x", "weights", "bqkv", "bo", "lnw", "qkw", "cos", "sin", "rbias", "vecs", "mats"]


def kernel(**inputs):
    import numpy as np
    import concourse.bacc as bacc
    from concourse import mybir as mb
    from concourse.bass_utils import run_bass_kernel_spmd as run

    w = {k: np.asarray(v) for k, v in inputs.items()}

    def blocks(m):
        return m.reshape(-1, P, m.shape[-1]).transpose(1, 0, 2)

    def cols(vec):
        return vec.reshape(KD, P).T

    packed = np.zeros((N_PIECES, P, PIECE), np.float32)

    def put(n, *parts):
        at = 0
        for part in parts:
            part = part.reshape(part.shape[0], -1)
            packed[n, :part.shape[0], at:at + part.shape[1]] = part
            at += part.shape[1]

    for k in range(KD):
        put(k, w["L0_attn_Wqkv"][k * P:(k + 1) * P])
    put(2, blocks(w["L0_attn_Wo"]))
    put(3, blocks(w["L0_ffn_wk"]))
    put(4, blocks(w["L0_ffn_wv"]))
    for g in range(4):
        put(5 + g, blocks(w["L0_ffn_wq"][:, g * CH:(g + 1) * CH]))
    for j in range(KV2):
        put(9 + j, blocks(w["L0_ffn_wo"][j * 4 * DH2:(j + 1) * 4 * DH2]))
    put(13, blocks(w["L0_ffn_router_w"]))
    for e in range(E1):
        gu = np.stack([blocks(w["L0_ffn_wg"][e]), blocks(w["L0_ffn_wu"][e])], 2)
        put(14 + e, gu, w["L0_ffn_wd"][e])
    for n, name in enumerate(("Wdt", "Wb", "Wc")):
        put(22 + n, blocks(w["L1_attn_" + name]))
    put(25, blocks(w["L1_ffn_gate_weight"].T))
    for e in range(E2):
        put(26 + e, blocks(w["L1_ffn_gate_up_proj"][e].T), np.pad(w["L1_ffn_down_proj"][e].T, ((0, P - I2), (0, 0))))

    one = np.ones(D, np.float32)
    norms = [one, w["L0_ffn_ln1_w"], w["L0_ffn_ln2_w"], one, one]
    cos, sin = rope_tables()
    qkw = np.stack([w["L0_ffn_knorm_w"], w["L0_ffn_knorm_w"]]
                   + [w["L0_ffn_qnorm_w"][g * CH:(g + 1) * CH] for g in range(4)])
    vecs = np.stack([cols(w["L1_attn_" + n]) for n in ("bdt", "bb", "bc", "D")], 1)
    mats = np.stack([blocks(w["L1_attn_" + n]).reshape(P, -1) for n in ("a_raw", "B_base", "C_base")], 1)
    arrays = {
        "x": w["L0_attn_x"], "weights": packed, "bqkv": w["L0_attn_bqkv"], "bo": w["L0_attn_bo"],
        "lnw": np.stack([cols(n) for n in norms], 1), "qkw": qkw, "cos": cos, "sin": sin,
        "rbias": w["L0_ffn_router_bias"], "vecs": vecs, "mats": mats,
    }
    arrays = {n: np.ascontiguousarray(v) for n, v in arrays.items()}
    nc = bacc.Bacc("TRN2", target_bir_lowering=False, num_devices=1)
    aps = {n: nc.dram_tensor(n + "_dram", arrays[n].shape, mb.dt.from_np(arrays[n].dtype), kind="ExternalInput").ap()
           for n in INS}
    out = nc.dram_tensor("out_dram", (1, S, D), mb.dt.float32, kind="ExternalOutput").ap()
    build(nc, aps, out)
    r = run(nc, [{n + "_dram": v for n, v in arrays.items()}], core_ids=[0])
    return r.results[0]["out_dram"]
```

```python
from contextlib import ExitStack

import concourse.bass as bass
from concourse import mybir

F32 = mybir.dt.float32
F32R = mybir.dt.float32r
BF16 = mybir.dt.bfloat16
U32 = mybir.dt.uint32
ALU = mybir.AluOpType
ACT = mybir.ActivationFunctionType
X_AXIS = mybir.AxisListType.X

P = 128
S = 1024
D = 256
KD = D // P
NT = S // P
CH = 512
NC = S // CH
TC = CH // P
H1, HD1 = 16, 16
PR1 = H1 // 2
H2, KV2, DH2, RD = 16, 4, 128, 64
E1, I1, TOP1 = 8, 128, 2
E2, I2, TOP2 = 32, 96, 8
THRESHOLD = 0.8
NST = 16
DT_MIN = 0.0001
MASKED = -1.0e30
PIECE = 1024



def weight_stream():
    out = []
    for c in range(NC):
        out += [(("wqkv", c, k), k, 3 * D) for k in range(KD)]
        out.append((("wo1", c), 2, KD * D))
    for c in range(NC):
        out += [(("w2", c, g), 3 + g, KD * CH) for g in range(6)]
        out += [(("wo2", c, j), 9 + j, 4 * D) for j in range(KV2)]
        if c == NC - 1:
            out.insert(len(out) - KV2, (("rw", 0, 0), 13, KD * E1))
    out += [(("rw", 0, c), 13, KD * E1) for c in range(1, NC)]
    out += [(("moe", 0, e), 14 + e, 2 * KD * I1 + D) for e in range(E1)]
    out += [(("ssm", c, w), 22 + w, KD * D) for c in range(NC) for w in range(3)]
    out += [(("rw", 1, c), 25, KD * E2) for c in range(NC)]
    out += [(("moe", 1, e), 26 + e, 2 * KD * I2 + D) for e in range(E2)]
    return out


N_PIECES = 26 + E2



def spread(main, side):
    out, at = [], 0
    for n, run in enumerate(main):
        out += run
        upto = -(-(n + 1) * len(side) // len(main))
        out += side[at:upto]
        at = upto
    return out + side[at:]


def norm_steps(stage, c):
    return [("norm", stage, c)] + [("normT", stage, c, k) for k in range(KD)]


def softmax_steps(units, blocks, side):
    out, behind = [], []
    for n, u in enumerate(units):
        runs = []
        for b in blocks(u):
            runs.append([("score",) + b] + behind)
            behind = [("pv",) + b]
        out += spread(runs, side(n))
    return out + behind + side(len(units))


def attention1(c):
    def maxima(g):
        out = []
        for p in (2 * g, 2 * g + 1):
            for t in range(TC * c, TC * c + TC):
                out += [("max1", c, t, p, None)] if c == 0 else [("max1", c, t, p, i) for i in (0, 1)]
            out.append(("qT1", c, p, 1))
        return out

    def side(g):
        out = [("out1", c, g - 1)] if g else []
        if g < 3:
            out += maxima(g + 1)
        if g == 2:
            out += norm_steps(0, 1) if c == 0 else norm_steps(1, 0)
        return out

    tiles = range(TC * c, TC * c + TC)
    out = [("qkv1", tiles[0])]
    for t in tiles[1:]:
        out += [("qkv1", t)] + [("kT1", t - 1, half) for half in (0, 1)]
    out += [("kT1", tiles[-1], half) for half in (0, 1)]
    out += [("qT1", c, p, 0) for p in range(PR1)]
    out += maxima(0)
    blocks = lambda g: [(c, g, sb, i) for sb in range(TC * c + TC) for i in (0, 1)]
    out += [(s[0] + "1",) + s[1:] if s[0] in ("score", "pv") else s for s in softmax_steps(range(4), blocks, side)]
    out += [("aT1", c, k) for k in range(KD)]
    out += [("wo1", c, tp) for tp in range(TC // 2)]
    return out


def attention2(c):
    units = [(c, j, hp) for j in range(KV2) for hp in range(2)]

    def maxima(u):
        out = [("qT2", u, i) for i in (0, 1)]
        for t in range(TC * c, TC * c + TC):
            out += [("max2", u, t, None)] if c == 0 else [("max2", u, t, i) for i in (0, 1)]
        return out + [("mT2", u)]

    def side(n):
        first = [("out2", units[n - 1])] if n else []
        last = [("wo2", units[n - 1], i, tp) for tp in range(TC // 2) for i in (0, 1)] if n else []
        more = maxima(units[n + 1]) if n + 1 < len(units) else []
        if n % 2 == 0 and n + 2 < len(units):
            more = more + [("rope", c, t, units[n + 2][1]) for t in range(TC)]
        if c == NC - 1 and n == 0:
            more = more + norm_steps(2, 0) + [("router", 0, 0)]
        half = min(len(more), 5)
        return first + more[:half] + last + more[half:]

    out = [("qkv2", c, g, tp) for g in (0, 1) for tp in range(TC // 2)]
    out.append(("rms2", c, "k"))
    keys = [("rope", c, t, "k") for t in range(TC)] + [("kT2", c, j) for j in range(KV2)]
    if c == 0:
        keys += norm_steps(1, 1)
    out += spread([[("qkv2", c, g, tp)] for g in range(2, 6) for tp in range(TC // 2)], keys)
    out.append(("rms2", c, "q"))
    out += [("rope", c, t, 0) for t in range(TC)]
    out += maxima(units[0])
    blocks = lambda u: [(u, sb) for sb in range(TC * c + TC)]
    return out + [(s[0] + "2",) + s[1:] if s[0] in ("score", "pv") else s for s in softmax_steps(units, blocks, side)]


def experts(stage, n, opening, closing):
    jobs = []
    for e in range(n):
        if e in (0, n - 2):
            jobs += [(e + i, c) for c in range(NC) for i in (0, 1)]
        elif e not in (1, n - 1):
            jobs += [(e, c) for c in range(NC)]
    out = []
    for i, job in enumerate(jobs):
        if i == 1:
            out += opening
        out.append(("gateup", stage) + job)
        if i:
            out += [("down", stage) + jobs[i - 1] + (tp,) for tp in range(TC // 2)]
        if i == len(jobs) - 2:
            out += closing
    return out + [("down", stage) + jobs[-1] + (tp,) for tp in range(TC // 2)]


def all_steps():
    out = norm_steps(0, 0) + attention1(0) + attention1(1)
    for c in range(NC):
        out += attention2(c)
    out += experts(0, E1, norm_steps(2, 1) + [("router", 0, 1)], norm_steps(3, 0))
    out += [("rates",)] + [("proj", 0, w, ob) for w in range(3) for ob in range(KD)]
    out[len(out) - 5:len(out) - 5] = norm_steps(3, 1)
    out += [("proj", 1, w, ob) for w in range(3) for ob in range(KD)]
    for ob in range(KD):
        out += [("scan", ob, n) for n in range(NST)] + [("y", ob)]
    out += [("yT", tp) for tp in range(NT // 2)]
    out += norm_steps(4, 0) + [("router", 1, 0)]
    return out + experts(1, E2, norm_steps(4, 1) + [("router", 1, 1)], [])


STEPS = all_steps()

RINGS = {
    "T": {"qkv1": (1, 1), "max1": (1, 1), "score1": (1, 1), "qkv2": (1, 1), "max2": (1, 1), "score2": (1, 1),
          "gateup": (1, 1), "proj": (1, 1)},
    "M": {"normT": (1, 1), "kT1": (1, 1), "qT1": (1, 2), "out1": (1, 1), "aT1": (1, 1), "wo1": (1, 1),
          "kT2": (1, 1), "qT2": (1, 1), "mT2": (1, 1), "out2": (1, 1), "wo2": (1, 1), "router": (1, 1),
          "down": (1, 1), "yT": (1, 1)},
    "O": {"o1": (1, 0), "o2": (2, 0), "y": (2, 0), "down": (1, 1)},
}


def ring_table(ring):
    kinds = RINGS[ring]
    released, filled, n, table = [0, 0], [0, 0], 0, {}
    for step in STEPS:
        key = step
        if step[0] == "down":
            if ring != ("M", "O")[step[4]]:
                continue
        elif ring == "O":
            if step[0] == "score1" and step[3] == 0 and step[4] == 0:
                key = ("o1", step[1], step[2])
            elif step[0] == "score2" and step[2] == 0:
                key = ("o2", step[1])
            elif step[0] == "scan" and step[2] == 0:
                key = ("y", step[1])
            else:
                continue
        if key[0] not in kinds:
            continue
        slots, ends = kinds[key[0]]
        table[key] = []
        for _ in range(slots):
            s = n % 2
            filled[s] += ends > 0
            table[key].append((s, released[s], filled[s], released[s] + ends))
            released[s] += ends
            n += 1
    return table


def ordinals():
    count, out = {}, {}
    for step in STEPS:
        count[step[0]] = count.get(step[0], 0) + 1
        out[step] = count[step[0]]
    return out


def build(nc, a, out_dram):
    tab = {r: ring_table(r) for r in RINGS}
    nth = ordinals()
    stream = weight_stream()
    mts = [st for st in STEPS if st[0] == "mT2"]
    outs = [st for st in STEPS if st[0] == "out2"]
    gus = [st for st in STEPS if st[0] == "gateup"]
    order = {name: n for n, (name, _, _) in enumerate(stream)}

    with ExitStack() as ctx:
        def psum(name, shape):
            return ctx.enter_context(nc.psum_tensor(name, shape, F32))

        def sb(name, shape, dt=F32):
            return ctx.enter_context(nc.sbuf_tensor(name, shape, dt))

        sems = {}

        def sem(name):
            if name not in sems:
                sems[name] = ctx.enter_context(nc.semaphore(name))
            return sems[name]

        psT = [psum("psT0", [P, 2, CH]), psum("psT1", [P, 2, CH])]
        psO = psum("psO", [P, 2, CH])
        psM = [psum("psM0", [P, CH]), psum("psM1", [P, CH])]

        x = sb("x", [P, NT, D])
        xn = sb("xn", [P, NT, D])
        normed = sb("normed", [P, TC, D])
        onehot = normed[:].rearrange("p t (j e) -> p t j e", e=E2)
        xTh = sb("xTh", [P, KD, S], F32R)
        xTl = sb("xTl", [P, KD, S], F32R)
        w_raw = sb("w_raw", [P, 2, PIECE])
        w_hi = sb("w_hi", [P, 2, PIECE], F32R)
        w_lo = sb("w_lo", [P, 2, PIECE], F32R)
        probs = sb("probs", [P, 2, 2, CH])
        ident = sb("ident", [P, P])
        ones = sb("ones", [P, P])
        ident_b = sb("ident_b", [P, P], BF16)
        mask_q = sb("mask_q", [P, P], BF16)
        mask_k = sb("mask_k", [P, P], BF16)
        iota = sb("iota", [P, E2])
        iota_i = sb("iota_i", [P, E2], mybir.dt.int32)
        lnw = sb("lnw", [P, 5, KD])
        bn6 = sb("bn6", [P, TC, 6])
        mv = sb("mv", [P, TC, 2])
        rs = sb("rs", [P, 3, TC])
        ms = sb("ms", [P, 2, TC])
        r_q = sb("r_q", [P, TC])
        r_k = sb("r_k", [P, TC])
        FN, RN = 17440, 16 * 1024
        fr = sb("fr", [P, FN])
        rr = sb("rr", [P, RN], F32R)

        class Carve:
            def __init__(self, base, limit):
                self.base, self.limit, self.at = base, limit, 0

            def take(self, *dims):
                n = int(np_prod(dims))
                v = self.base[:, self.at:self.at + n]
                self.at += n
                assert self.at <= self.limit, (self.at, self.limit)
                if len(dims) == 2:
                    return v.rearrange("p (a b) -> p a b", b=dims[1])
                if len(dims) == 3:
                    return v.rearrange("p (a b c) -> p a b c", b=dims[1], c=dims[2])
                return v

        def np_prod(dims):
            n = 1
            for d in dims:
                n *= d
            return n

        f, r = Carve(fr, FN), Carve(rr, RN)
        bqkv_b = f.take(3 * D)
        bo_b = f.take(D)
        qkv_tok = f.take(3 * D)
        q_stack = f.take(TC, H1, 64)
        k_stack = f.take(H1, 64)
        v_aug = f.take(NT, H1, HD1 + 1)
        o1_T = f.take(CH)
        a_tok = f.take(TC, D)
        den1 = f.take(TC, 4)
        kT1 = r.take(PR1, S)
        qT1 = r.take(H1, CH)
        f, r = Carve(fr, FN), Carve(rr, RN)
        q_tok = f.take(TC, H2, DH2)
        k_tok = f.take(TC, KV2, DH2)
        p_sum = k_tok.rearrange("p a b c -> p (a b c)")[:, 0:2 * CH].rearrange("p (a b) -> p a b", b=CH)
        v_tok = f.take(NT, CH)
        qkw = f.take(2, CH)
        cos_t = f.take(NT, RD)
        sin_t = f.take(NT, RD)
        neg_max = f.take(TC, P)
        ssq = f.take(TC, 8)
        rope_tmp = f.take(2, 4, RD)
        kTh = r.take(KV2, S)
        kTl = r.take(KV2, S)
        qTh = r.take(2, 2, CH)
        qTl = r.take(2, 2, CH)
        negmT = r.take(2, CH)
        pick = r.take(2, P)
        oTh = r.take(2, CH)
        oTl = r.take(2, CH)
        f, r = Carve(fr, FN), Carve(rr, RN)
        gate = f.take(2, CH)
        act = f.take(2, CH)
        aTh = r.take(2, CH)
        aTl = r.take(2, CH)
        uT = f.take(KD, S)
        dtT = f.take(KD, S)
        bT = f.take(KD, S)
        cT = f.take(KD, S)
        decay = f.take(2, S)
        state = f.take(2, S)
        sp_a = decay[:, 0, 0:CH]
        sp_b = decay[:, 1, 0:CH]
        sp_c = state[:, 0, 0:CH]
        diag = f.take(2, P)
        yT = uT
        rbias = sb("rbias", [P, E1])
        logits = sb("logits", [P, TC, E2])
        rt = sb("rt", [P, TC, E2])
        comb = sb("comb", [P, NT, E2])
        top8 = sb("top8", [P, TC, 8])
        idx_u = sb("idx_u", [P, TC, 8], U32)
        idx_f = sb("idx_f", [P, TC, 8])
        cum = sb("cum", [P, TC, 8])
        tok1 = sb("tok1", [P, TC])
        rden = sb("rden", [P, 2, TC])
        vecs = sb("vecs", [P, 4, KD])
        mats = sb("mats", [P, 3, KD * NST])
        sp_s = sb("sp_s", [P, 3, KD * NST])
        neg_a = sb("neg_a", [P, KD * NST])
        bc_s = sb("bc_s", [P, KD * NST])

        block = ctx.enter_context(nc.Block())

        def wait_full(eng, ring, use, i=0):
            slot, _, fills, _ = tab[ring][use][i]
            eng.wait_ge(sem(f"{ring}_full{slot}"), fills)
            return slot

        def rope_part(which, t):
            if which == "k":
                return k_tok[:, t], r_k[:, t:t + 1]
            return q_tok[:, t, 4 * which:4 * which + 4], r_q[:, t:t + 1]

        def wait_read(eng, ring, use, i=0):
            slot, _, _, ends = tab[ring][use][i]
            eng.wait_ge(sem(f"{ring}_read{slot}"), ends)

        @block.sync
        def _(sp):
            for c in range(NC):
                sp.dma_start(x[:, TC * c:TC * c + TC], a["x"][:, c * CH:(c + 1) * CH].rearrange("a (t p) d -> p (a t) d", p=P))\
                    .then_inc(sem(f"x_loaded{c}"), 16)
            for dst, src in ((bqkv_b, a["bqkv"].partition_broadcast(P)), (bo_b, a["bo"].partition_broadcast(P)),
                             (lnw[:], a["lnw"]), (rbias[:], a["rbias"].partition_broadcast(P)), (vecs[:], a["vecs"]), (mats[:], a["mats"])):
                sp.dma_start(dst, src).then_inc(sem("consts_loaded"), 16)
            rows = []
            for n, (name, at, width) in enumerate(stream):
                if n >= 2:
                    sp.wait_ge(sem("w_split"), n - 1)
                sp.dma_start(w_raw[:, n % 2, 0:width], a["weights"][at, :, 0:width]).then_inc(sem(f"w_loaded{n % 2}"), 16)
                if name[0] == "w2" and name[2] != 1:
                    g = name[2]
                    if len(rows) >= 2:
                        wait_read(sp, "T", rows[-2])
                    sp.dma_start(qkw[:, len(rows) % 2], a["qkw"][g].partition_broadcast(P)).then_inc(
                        sem(f"row_loaded{len(rows) % 2}"), 16)
                    rows.append(("qkv2", name[1], g, TC // 2 - 1))
                if n == KD:
                    sp.dma_start(cos_t, a["cos"]).then_inc(sem("tables_loaded"), 16)
                    sp.dma_start(sin_t, a["sin"]).then_inc(sem("tables_loaded"), 16)
            for tp, ring in enumerate("MO"):
                wait_read(sp, ring, ("down", 1, E2 - 1, NC - 1, tp))
            sp.dma_start(out_dram.rearrange("a (t p) d -> p (a t) d", p=P), x[:]).then_inc(sem("stored"), 16)
            sp.wait_ge(sem("stored"), 16)

        @block.gpsimd
        def _(pool):
            g = nc.gpsimd
            chained = [0]

            def link(ins):
                chained[0] += 1
                ins.then_inc(sem("pool_chain"), 1)
                pool.wait_ge(sem("pool_chain"), chained[0])

            link(g.memset(ident[:], 0.0))
            g.affine_select(out=ident[:], in_=ident[:], compare_op=ALU.not_equal, fill=1.0, base=0,
                            pattern=[[-1, P]], channel_multiplier=1).then_inc(sem("ident_ready"), 1)
            g.memset(v_aug, 1.0)
            g.memset(q_stack, 0.0)
            g.memset(mask_q[:], 0.0)
            g.memset(mask_k[:], 0.0)
            link(g.memset(k_stack, 0.0))
            g.memset(k_stack[:, :, 48:49], 1.0).then_inc(sem("stacks_clear"), 1)
            pool.wait_ge(sem("ident_ready"), 1)
            g.memset(ones[:], 1.0)
            g.tensor_copy(ident_b[:], ident[:])
            g.affine_select(out=mask_q[:], in_=mask_q[:], compare_op=ALU.is_ge, fill=MASKED, base=0,
                            pattern=[[-1, P]], channel_multiplier=1)
            g.affine_select(out=mask_k[:], in_=mask_k[:], compare_op=ALU.is_ge, fill=MASKED, base=0,
                            pattern=[[1, P]], channel_multiplier=-1)
            link(g.iota(iota_i[:], pattern=[[1, E2]], base=0, channel_multiplier=0))
            g.tensor_copy(iota[:], iota_i[:]).then_inc(sem("consts_ready"), 1)

            last_use = {}
            for step in STEPS:
                kind = step[0]
                if kind == "qkv1":
                    for k in range(KD):
                        last_use[("wqkv", step[1] // TC, k)] = step
                elif kind == "wo1":
                    last_use[("wo1", step[1])] = step
                elif kind == "qkv2":
                    last_use[("w2", step[1], step[2])] = step
                elif kind == "wo2":
                    last_use[("wo2", step[1][0], step[1][1])] = step
                elif kind == "router":
                    last_use[("rw", step[1], step[2])] = step
                elif kind == "down":
                    last_use[("moe", step[1], step[2])] = step
                elif kind == "proj":
                    last_use[("ssm", step[1], step[2])] = step
            after = {}
            for n, (name, _, _) in enumerate(stream):
                after.setdefault(last_use[name], []).append(n + 2)

            split_upto = [0]

            def split_next():
                n = split_upto[0]
                if n >= len(stream):
                    return
                name, _, width = stream[n]
                pool.wait_ge(sem(f"w_loaded{n % 2}"), 16 * (n // 2 + 1))
                if n >= 2:
                    use = last_use[stream[n - 2][0]]
                    wait_full(pool, "T" if use[0] in RINGS["T"] else "O" if use[0] == "down" else "M", use)
                hi, lo, raw = w_hi[:, n % 2, 0:width], w_lo[:, n % 2, 0:width], w_raw[:, n % 2, 0:width]
                link(g.tensor_scalar(hi, raw, 1.0, 0.0, ALU.mult, ALU.add))
                g.tensor_tensor(lo, raw, hi.bitcast(F32), ALU.subtract).then_inc(sem("w_split"), 1)
                split_upto[0] += 1

            split_next()
            split_next()
            for step in STEPS:
                kind = step[0]
                if kind == "qkv2" and step[1:] == (0, 0, 0):
                    wait_read(pool, "M", ("wo1", NC - 1, TC // 2 - 1))
                    g.memset(neg_max, 0.0)
                    link(g.memset(pick.bitcast(F32), 0.0))
                    for i in (0, 1):
                        ins = g.affine_select(out=pick[:, i], in_=pick[:, i].bitcast(F32), compare_op=ALU.not_equal, fill=1.0,
                                              base=-i, pattern=[[0, P]], channel_multiplier=1)
                    ins.then_inc(sem("pick_ready"), 1)
                if kind == "score2":
                    u, sbk = step[1], step[2]
                    c = u[0]
                    off = max(0, sbk - TC * c) * P
                    n = nth[step]
                    wait_read(pool, "T", step)
                    pr = probs[:, n % 2]
                    if sbk == 0:
                        if u == (c, 0, 0):
                            wait_full(pool, "M", ("kT2", c, KV2 - 1))
                        else:
                            wait_full(pool, "M", outs[nth[("out2", u)] - 2])
                        g.tensor_scalar(p_sum, pr, 1.0, 0.0, ALU.mult, ALU.add).then_inc(sem("p_sum"), 1)
                    else:
                        pool.wait_ge(sem("p_sum"), n - 1)
                        g.tensor_tensor(p_sum[:, :, off:CH], p_sum[:, :, off:CH], pr[:, :, off:CH],
                                        ALU.add).then_inc(sem("p_sum"), 1)
                if kind == "gateup":
                    n = nth[step]
                    s = n % 2
                    pool.wait_ge(sem("act_hi"), n)
                    if n >= 3:
                        wait_full(pool, "O", ("down",) + gus[n - 3][1:] + (1,))
                    m = I1 if step[1] == 0 else I2
                    g.tensor_tensor(aTl[0:m, s], act[0:m, s], aTh[0:m, s].bitcast(F32), ALU.subtract)\
                        .then_inc(sem("act_lo"), 1)
                if kind == "scan":
                    n = nth[step]
                    if n == 1:
                        pool.wait_ge(sem("bc_ready"), 1)
                    if n >= 3:
                        pool.wait_ge(sem("scan_summed"), n - 2)
                    col = step[1] * NST + step[2]
                    g.tensor_scalar(diag[:, n % 2], ident[:], bc_s[:, col:col + 1], 1.0, ALU.mult, ALU.mult)\
                        .then_inc(sem("diag_ready"), 1)
                for _ in after.get(step, ()):
                    split_next()

        @block.scalar
        def _(sc):
            s_ = nc.scalar
            chained = [0]

            def link(ins):
                chained[0] += 1
                ins.then_inc(sem("act_chain"), 1)
                sc.wait_ge(sem("act_chain"), chained[0])

            def full(ring, use, i=0):
                return wait_full(sc, ring, use, i)

            def read(ring, slot, ins):
                ins.then_inc(sem(f"{ring}_read{slot}"), 1)

            sc.wait_ge(sem("consts_loaded"), 16 * 6)
            roots, squares = 0, 0
            for step in STEPS:
                kind = step[0]
                if kind == "norm":
                    for _ in range(1 + (step[1] == 1)):
                        roots += 1
                        sc.wait_ge(sem("var_ready"), roots)
                        s_.activation(rs[:, 1, :], rs[:, 0, :], ACT.Sqrt).then_inc(sem("root_ready"), 1)
                elif kind == "normT":
                    _, st, c, k = step
                    m = full("M", step)
                    s_.activation(xTh[:, k, c * CH:(c + 1) * CH], psM[m][:], ACT.Identity,
                                  scale=lnw[:, st, k:k + 1]).then_inc(sem("xTh_ready"), 1)
                elif kind == "qkv1":
                    t = step[1]
                    i = t % TC
                    wait_read(sc, "T", step)
                    if t == 0:
                        sc.wait_ge(sem("stacks_clear"), 1)
                    q3 = qkv_tok[:, 0:D].rearrange("p (h d) -> p h d", d=HD1)
                    k3 = qkv_tok[:, D:2 * D].rearrange("p (h d) -> p h d", d=HD1)
                    v3 = qkv_tok[:, 2 * D:3 * D].rearrange("p (h d) -> p h d", d=HD1)
                    s_.activation(q_stack[:, i, :, 0:16].bitcast(F32R), q3, ACT.Copy, scale=HD1 ** -0.5)
                    s_.activation(q_stack[:, i, :, 32:48].bitcast(F32R), q3, ACT.Copy, scale=HD1 ** -0.5)
                    if t >= 1:
                        wait_full(sc, "M", ("kT1", t - 1, 1))
                    s_.activation(k_stack[:, :, 0:16].bitcast(F32R), k3, ACT.Copy)
                    s_.activation(k_stack[:, :, 16:32].bitcast(F32R), k3, ACT.Copy)
                    s_.activation(v_aug[:, t, :, 0:HD1], v3, ACT.Copy).then_inc(sem("stack_hi"), 1)
                elif kind == "kT1":
                    t, half = step[1], step[2]
                    m = full("M", step)
                    ins = s_.activation(kT1[:, 4 * half:4 * half + 4, t * P:(t + 1) * P],
                                        psM[m][:].rearrange("p (a b) -> p a b", b=P), ACT.Copy)
                    read("M", m, ins)
                elif kind == "qT1":
                    p = step[2]
                    m = full("M", step)
                    read("M", m, s_.activation(qT1[0:64, 2 * p, :], psM[m][0:64, :], ACT.Copy))
                elif kind == "score1":
                    _, c, g, sbk, i = step
                    n = nth[step]
                    t = full("T", step)
                    if n >= 3:
                        sc.wait_ge(sem("pv1_done"), n - 2)
                    off = max(0, sbk - TC * c) * P
                    read("T", t, s_.activation(probs[:, n % 2, :, off:CH], psT[t][:, :, off:CH], ACT.Exp))
                elif kind == "out1":
                    _, c, g = step
                    o = tab["O"][("o1", c, g)][0][0]
                    sc.wait_ge(sem("pv1_done"), nth[("pv1", c, g, TC * c + TC - 1, 1)])
                    if nth[step] > 1:
                        wait_full(sc, "M", ("out1", c, g - 1) if g else ("out1", c - 1, 3))
                    s_.activation(o1_T, psO[:, o], ACT.Copy).then_inc(sem("o1_out"), 1)
                elif kind == "aT1":
                    _, c, k = step
                    m = full("M", step)
                    s_.activation(xTh[:, k, c * CH:(c + 1) * CH], psM[m][:], ACT.Copy).then_inc(sem("aT1_hi"), 1)
                elif kind == "qkv2":
                    _, c, g, tp = step
                    t = full("T", step)
                    if g == 1:
                        read("T", t, s_.activation(v_tok[:, TC * c + 2 * tp:TC * c + 2 * tp + 2], psT[t][:], ACT.Copy))
                    else:
                        if squares:
                            sc.wait_ge(sem("ssq_ready"), squares)
                        squares += 1
                        s_.activation(psO[:, 0], psT[t][:, 0], ACT.Square, accum_out=ssq[:, 2 * tp, g:g + 1])
                        s_.activation(psO[:, 1], psT[t][:, 1], ACT.Square, accum_out=ssq[:, 2 * tp + 1, g:g + 1])\
                            .then_inc(sem("ssq_ready"), 1)
                elif kind == "rms2":
                    sc.wait_ge(sem("ms_ready"), nth[step])
                    s_.activation(ms[:, 1, :], ms[:, 0, :], ACT.Sqrt).then_inc(sem("ms_root"), 1)
                elif kind == "rope":
                    _, c, t, which = step
                    sc.wait_ge(sem("r_ready"), nth[("rms2", c, "k" if which == "k" else "q")])
                    tok, r_ = rope_part(which, t)
                    s_.activation(tok[:, :, RD:DH2], tok[:, :, RD:DH2], ACT.Copy, scale=r_).then_inc(sem("pass_scaled"), 1)
                elif kind == "kT2":
                    _, c, j = step
                    m = full("M", step)
                    s_.activation(kTh[:, j, c * CH:(c + 1) * CH], psM[m][:], ACT.Copy).then_inc(sem("kT2_hi"), 1)
                elif kind == "qT2":
                    u, i = step[1], step[2]
                    m = full("M", step)
                    n = nth[("mT2", u)]
                    s_.activation(qTh[:, n % 2, i], psM[m][:], ACT.Copy).then_inc(sem("qT2_hi"), 1)
                elif kind == "mT2":
                    m = full("M", step)
                    read("M", m, s_.activation(negmT[:, nth[step] % 2], psM[m][:], ACT.Copy))
                elif kind == "score2":
                    _, u, sbk = step
                    n = nth[step]
                    t = full("T", step)
                    if n >= 3:
                        sc.wait_ge(sem("pv2_done"), n - 2)
                        sc.wait_ge(sem("p_sum"), n - 2)
                    off = max(0, sbk - TC * u[0]) * P
                    read("T", t, s_.activation(probs[:, n % 2, :, off:CH], psT[t][:, :, off:CH], ACT.Exp))
                elif kind == "out2":
                    u = step[1]
                    n = nth[step]
                    c = u[0]
                    sc.wait_ge(sem("pv2_done"), nth[("pv2", u, TC * c + TC - 1)])
                    if n > 1:
                        wait_full(sc, "M", ("wo2", outs[n - 2][1], 1, 1))
                    s_.activation(oTh, psO[:], ACT.Copy).then_inc(sem("oTh_ready"), 1)
                elif kind == "router":
                    st = step[1]
                    if st == 0:
                        m = full("M", step)
                        read("M", m, s_.activation(logits[:, :, 0:E1], psM[m][:, 0:TC * E1].rearrange("p (t e) -> p t e", e=E1),
                                                   ACT.Sigmoid))
                    else:
                        wait_read(sc, "M", step)
                        s_.activation(rt[:], logits[:], ACT.Exp).then_inc(sem("logits_out"), 1)
                elif kind == "gateup":
                    _, st, e, c = step
                    n = nth[step]
                    s = n % 2
                    m = I1 if st == 0 else I2
                    t = full("T", step)
                    if n >= 3:
                        wait_read(sc, "T", gus[n - 3])
                    s_.activation(gate[0:m, s], psT[t][0:m, 0], ACT.Silu).then_inc(sem("silu"), 1)
                    wait_read(sc, "T", step)
                    if n >= 3:
                        wait_full(sc, "O", ("down",) + gus[n - 3][1:] + (1,))
                    s_.activation(aTh[0:m, s], act[0:m, s], ACT.Copy).then_inc(sem("act_hi"), 1)
                elif kind == "rates":
                    link(s_.activation(sp_s[:, 0], mats[:, 0], ACT.Abs))
                    s_.activation(sp_s[:, 1], sp_s[:, 0], ACT.Exp, scale=-1.0).then_inc(sem("rate_exp"), 1)
                    sc.wait_ge(sem("rate_one"), 1)
                    s_.activation(sp_s[:, 0], sp_s[:, 2], ACT.Ln).then_inc(sem("rate_log"), 1)
                elif kind == "proj":
                    _, c, w, ob = step
                    if w == 0:
                        wait_read(sc, "T", step)
                        if (c, ob) != (0, 0):
                            sc.wait_ge(sem("dt_ready"), KD * c + ob)
                        link(s_.activation(sp_a, dtT[:, ob, c * CH:(c + 1) * CH], ACT.Abs))
                        s_.activation(sp_b, sp_a, ACT.Exp, scale=-1.0).then_inc(sem("sp_exp"), 1)
                        sc.wait_ge(sem("sp_one"), KD * c + ob + 1)
                        s_.activation(sp_a, sp_c, ACT.Ln).then_inc(sem("sp_log"), 1)
                elif kind == "scan":
                    _, ob, k = step
                    n = nth[step]
                    if n == 1:
                        sc.wait_ge(sem("dt_ready"), KD * NC)
                    if n >= 3:
                        sc.wait_ge(sem("scanned"), n - 2)
                    s_.activation(decay[:, n % 2], dtT[:, ob], ACT.Exp,
                                  scale=neg_a[:, ob * NST + k:ob * NST + k + 1]).then_inc(sem("decay_ready"), 1)

        @block.vector
        def _(ve):
            v = nc.vector
            chained = [0]

            def link(ins):
                chained[0] += 1
                ins.then_inc(sem("dve_chain"), 1)
                ve.wait_ge(sem("dve_chain"), chained[0])

            def full(ring, use, i=0):
                return wait_full(ve, ring, use, i)

            def read(ring, slot, ins):
                ins.then_inc(sem(f"{ring}_read{slot}"), 1)

            def stats(src, c):
                for i in range(TC):
                    v_ins = v.bn_stats(bn6[:, i], src(i))
                link(v_ins)
                for i in range(TC):
                    v_ins = v.bn_aggr(mv[:, i], bn6[:, i])
                link(v_ins)

            roots = 0
            summed = {}

            def root():
                nonlocal roots
                roots += 1
                ve.wait_ge(sem("root_ready"), roots)
                link(v.reciprocal(rs[:, 2, :], rs[:, 1, :]))

            def layernorm(c, dst):
                stats(lambda i: x[:, TC * c + i], c)
                v.tensor_scalar(rs[:, 0, :], mv[:, :, 1], 1e-5, None, ALU.add).then_inc(sem("var_ready"), 1)
                root()
                for i in range(TC):
                    ins = v.tensor_scalar(dst(i), x[:, TC * c + i], mv[:, i, 0:1], rs[:, 2, i:i + 1],
                                          ALU.subtract, ALU.mult)
                return ins

            def rmsnorm(c):
                stats(lambda i: xn[:, TC * c + i], c)
                link(v.tensor_tensor(rs[:, 1, :], mv[:, :, 0], mv[:, :, 0], ALU.mult))
                v.scalar_tensor_tensor(rs[:, 0, :], rs[:, 1, :], 1e-6, mv[:, :, 1], ALU.add, ALU.add)\
                    .then_inc(sem("var_ready"), 1)
                root()
                for i in range(TC):
                    ins = v.tensor_scalar(normed[:, i], xn[:, TC * c + i], rs[:, 2, i:i + 1], None, ALU.mult)
                return ins

            v.memset(psO[:], 0.0).then_inc(sem("psO_clear"), 1)
            link(v.memset(qT1.bitcast(F32), 0.0))
            ve.wait_ge(sem("x_loaded0"), 16)
            ve.wait_ge(sem("consts_loaded"), 16 * 6)
            for step in STEPS:
                kind = step[0]
                if kind == "norm":
                    _, st, c = step
                    if (st, c) == (0, 1):
                        ve.wait_ge(sem("x_loaded1"), 16)
                    if st == 1:
                        wait_read(ve, "M", ("wo1", c, TC // 2 - 1))
                    elif st == 2:
                        for i in (0, 1):
                            wait_read(ve, "M", ("wo2", (c, KV2 - 1, 1), i, TC // 2 - 1))
                    elif st == 3:
                        for tp, ring in enumerate("MO"):
                            wait_read(ve, ring, ("down", 0, E1 - 1, c, tp))
                    elif st == 4:
                        wait_read(ve, "M", ("yT", NT // 2 - 1))
                    if st in (0, 3, 4):
                        layernorm(c, lambda i: normed[:, i]).then_inc(sem("normed_ready"), 1)
                    elif st == 1:
                        link(layernorm(c, lambda i: xn[:, TC * c + i]))
                        rmsnorm(c).then_inc(sem("normed_ready"), 1)
                    else:
                        rmsnorm(c).then_inc(sem("normed_ready"), 1)
                        for i in range(TC):
                            t = TC * c + i
                            ins = v.tensor_tensor(x[:, t], x[:, t], xn[:, t], ALU.add)
                        link(ins)
                elif kind == "normT":
                    _, st, c, k = step
                    m = full("M", step)
                    ve.wait_ge(sem("xTh_ready"), nth[step])
                    cols = slice(c * CH, (c + 1) * CH)
                    if st == 3:
                        link(v.tensor_copy(uT[:, k, cols], psM[m][:]))
                    read("M", m, v.scalar_tensor_tensor(xTl[:, k, cols], psM[m][:], lnw[:, st, k:k + 1],
                                                        xTh[:, k, cols].bitcast(F32), ALU.mult, ALU.subtract))
                elif kind == "qkv1":
                    t = step[1]
                    i = t % TC
                    s = full("T", step)
                    if t >= 1:
                        ve.wait_ge(sem("stack_hi"), t)
                        ve.wait_ge(sem("stack_lo"), t)
                    read("T", s, v.tensor_tensor(qkv_tok, psT[s][:].rearrange("p a b -> p (a b)")[:, 0:3 * D], bqkv_b, ALU.add))
                    ve.wait_ge(sem("stack_hi"), nth[step])
                    q3 = qkv_tok[:, 0:D].rearrange("p (h d) -> p h d", d=HD1)
                    k3 = qkv_tok[:, D:2 * D].rearrange("p (h d) -> p h d", d=HD1)
                    if t >= TC:
                        v.memset(q_stack[:, i, :, 48:49], 0.0)
                    v.scalar_tensor_tensor(q_stack[:, i, :, 16:32].bitcast(F32R), q3, HD1 ** -0.5,
                                           q_stack[:, i, :, 0:16], ALU.mult, ALU.subtract)
                    v.tensor_tensor(k_stack[:, :, 32:48].bitcast(F32R), k3, k_stack[:, :, 0:16], ALU.subtract)\
                        .then_inc(sem("stack_lo"), 1)
                elif kind == "qT1":
                    p = step[2]
                    m = full("M", step)
                    read("M", m, v.tensor_copy(qT1[64:P, 2 * p + 1, :], psM[m][64:P, :]))
                elif kind == "max1":
                    _, c, t, p, i = step
                    s = full("T", step)
                    w = (t + 1) * P
                    if i is None:
                        dst = q_stack[:, t % TC, 2 * p:2 * p + 2, 48]
                        src = psT[s][:, :, 0:w]
                    else:
                        dst = q_stack[:, t % TC, 2 * p + i, 48:49]
                        src = psT[s][:].rearrange("p a b -> p (a b)")[:, 0:w]
                    read("T", s, v.tensor_reduce(dst, src, X_AXIS, ALU.max, negate=True))
                elif kind == "out1":
                    _, c, g = step
                    m = full("M", step)
                    o4 = psM[m][:].rearrange("p (t h e) -> p t h e", t=TC, h=4)
                    if nth[step] > 1:
                        wait_read(ve, "M", ("out1", c, g - 1) if g else ("out1", c - 1, 3))
                    link(v.reciprocal(den1, o4[:, :, :, HD1]))
                    read("M", m, v.tensor_tensor(a_tok.rearrange("p t (h d) -> p t h d", d=HD1)[:, :, 4 * g:4 * g + 4],
                                         o4[:, :, :, 0:HD1],
                                         den1.unsqueeze(3).to_broadcast([P, TC, 4, HD1]), ALU.mult))
                elif kind == "aT1":
                    _, c, k = step
                    m = full("M", step)
                    ve.wait_ge(sem("aT1_hi"), nth[step])
                    read("M", m, v.tensor_tensor(xTl[:, k, c * CH:(c + 1) * CH], psM[m][:],
                                         xTh[:, k, c * CH:(c + 1) * CH].bitcast(F32), ALU.subtract))
                elif kind == "wo1":
                    _, c, tp = step
                    m = full("M", step)
                    for i in (0, 1):
                        t = TC * c + 2 * tp + i
                        ins = v.tensor_tensor(x[:, t], x[:, t], bo_b, ALU.add)
                    link(ins)
                    t = TC * c + 2 * tp
                    read("M", m, v.tensor_tensor(x[:, t:t + 2], x[:, t:t + 2], psM[m][:].rearrange("p (a b) -> p a b", b=D), ALU.add))
                elif kind == "qkv2":
                    _, c, g, tp = step
                    if g == 1:
                        continue
                    s = full("T", step)
                    rows = 5 * c + (0 if g == 0 else g - 1)
                    ve.wait_ge(sem(f"row_loaded{rows % 2}"), 16 * (rows // 2 + 1))
                    ve.wait_ge(sem("ssq_ready"), 2 * rows + tp + 1)
                    if c == 1 and g == 0 and tp == 0:
                        ve.wait_ge(sem("oT_ready"), 2 * KV2)
                    if g == 0:
                        dst = k_tok[:, 2 * tp:2 * tp + 2].rearrange("p a b c -> p a (b c)")
                    else:
                        dst = q_tok[:, 2 * tp:2 * tp + 2, 4 * (g - 2):4 * (g - 2) + 4].rearrange("p a b c -> p a (b c)")
                    read("T", s, v.tensor_tensor(dst, psT[s][:], qkw[:, rows % 2].unsqueeze(1).to_broadcast([P, 2, CH]), ALU.mult))
                elif kind == "rms2":
                    _, c, which = step
                    if which == "k":
                        v.tensor_scalar(ms[:, 0, :], ssq[:, :, 0], 1.0 / (KV2 * DH2), 1e-6, ALU.mult, ALU.add)\
                            .then_inc(sem("ms_ready"), 1)
                    else:
                        link(v.tensor_reduce(ms[:, 0, :], ssq[:, :, 2:6], X_AXIS, ALU.add))
                        v.tensor_scalar(ms[:, 0, :], ms[:, 0, :], 1.0 / (H2 * DH2), 1e-6, ALU.mult, ALU.add)\
                            .then_inc(sem("ms_ready"), 1)
                    ve.wait_ge(sem("ms_root"), nth[step])
                    if which == "k":
                        v.reciprocal(r_k[:], ms[:, 1, :]).then_inc(sem("r_ready"), 1)
                    else:
                        link(v.reciprocal(r_q[:], ms[:, 1, :]))
                        v.tensor_scalar(r_q[:], r_q[:], DH2 ** -0.5, None, ALU.mult).then_inc(sem("r_ready"), 1)
                    ve.wait_ge(sem("r_ready"), nth[step])
                elif kind == "rope":
                    _, c, t, which = step
                    if nth[step] == 1:
                        ve.wait_ge(sem("tables_loaded"), 32)
                    nh = 4
                    tok, r_ = rope_part(which, t)
                    HR = RD // 2
                    t1, t2 = rope_tmp[:, 0], rope_tmp[:, 1]
                    ct = cos_t[:, TC * c + t].unsqueeze(1).to_broadcast([P, nh, RD])
                    sn = sin_t[:, TC * c + t].unsqueeze(1)
                    if nth[step] > 1:
                        ve.wait_ge(sem("roped"), nth[step] - 1)
                    v.scalar_tensor_tensor(t1, tok[:, :, 0:RD], r_, ct, ALU.mult, ALU.mult)
                    v.scalar_tensor_tensor(t2[:, :, 0:HR], tok[:, :, HR:RD], r_,
                                           sn[:, :, 0:HR].to_broadcast([P, nh, HR]), ALU.mult, ALU.mult)
                    link(v.scalar_tensor_tensor(t2[:, :, HR:RD], tok[:, :, 0:HR], r_,
                                                sn[:, :, HR:RD].to_broadcast([P, nh, HR]), ALU.mult, ALU.mult))
                    v.tensor_tensor(tok[:, :, 0:RD], t1, t2, ALU.add).then_inc(sem("roped"), 1)
                elif kind == "kT2":
                    _, c, j = step
                    m = full("M", step)
                    ve.wait_ge(sem("kT2_hi"), nth[step])
                    cols = slice(c * CH, (c + 1) * CH)
                    read("M", m, v.tensor_tensor(kTl[:, j, cols], psM[m][:], kTh[:, j, cols].bitcast(F32), ALU.subtract))
                elif kind == "qT2":
                    u, i = step[1], step[2]
                    m = full("M", step)
                    n = nth[("mT2", u)]
                    ve.wait_ge(sem("qT2_hi"), nth[step])
                    read("M", m, v.tensor_tensor(qTl[:, n % 2, i], psM[m][:], qTh[:, n % 2, i].bitcast(F32), ALU.subtract))
                elif kind == "max2":
                    _, u, t, i = step
                    s = full("T", step)
                    if t == TC * u[0] and i in (None, 0):
                        if nth[("mT2", u)] == 1:
                            ve.wait_ge(sem("pick_ready"), 1)
                        else:
                            wait_full(ve, "M", mts[nth[("mT2", u)] - 2])
                    w = (t + 1) * P
                    if i is None:
                        dst, src = neg_max[:, t % TC, 0:2], psT[s][:, :, 0:w]
                    else:
                        dst, src = neg_max[:, t % TC, i:i + 1], psT[s][:].rearrange("p a b -> p (a b)")[:, 0:w]
                    read("T", s, v.tensor_reduce(dst, src, X_AXIS, ALU.max, negate=True))
                elif kind == "out2":
                    u = step[1]
                    n = nth[step]
                    ve.wait_ge(sem("oTh_ready"), n)
                    v.tensor_tensor(oTl, psO[:], oTh.bitcast(F32), ALU.subtract).then_inc(sem("oT_ready"), 1)
                    m = full("M", step)
                    if n > 1:
                        for tp in range(TC // 2):
                            wait_read(ve, "M", ("wo2", outs[n - 2][1], 1, tp))
                    read("M", m, v.reciprocal(rden[:], psM[m][:, 0:2 * TC].rearrange("p (a b) -> p a b", b=TC)))
                elif kind == "wo2":
                    _, u, i, tp = step
                    m = full("M", step)
                    wait_read(ve, "M", ("out2", u))
                    if i or u[1] or u[2]:
                        wait_read(ve, "M", ("wo2", u, 0, tp) if i else ("wo2", outs[nth[("out2", u)] - 2][1], 1, tp))
                    for b in (0, 1):
                        t = 2 * tp + b
                        ins = v.scalar_tensor_tensor(xn[:, TC * u[0] + t], psM[m][:, b * D:(b + 1) * D], rden[:, i, t:t + 1],
                                                     xn[:, TC * u[0] + t], ALU.mult, ALU.add)
                    read("M", m, ins)
                elif kind == "router":
                    _, st, c = step
                    if st == 0:
                        wait_read(ve, "M", step)
                        link(v.tensor_tensor(rt[:, :, 0:E1], logits[:, :, 0:E1],
                                             rbias[:].unsqueeze(1).to_broadcast([P, TC, E1]), ALU.add))
                    else:
                        m = full("M", step)
                        lg = psM[m][:, 0:TC * E2].rearrange("p (t e) -> p t e", e=E2)
                        link(v.tensor_reduce(tok1[:], lg, X_AXIS, ALU.max))
                        read("M", m, v.tensor_tensor(logits[:], lg, tok1[:].unsqueeze(2).to_broadcast([P, TC, E2]), ALU.subtract))
                        ve.wait_ge(sem("logits_out"), c + 1)
                        link(v.tensor_reduce(tok1[:], rt[:], X_AXIS, ALU.add))
                        link(v.reciprocal(tok1[:], tok1[:]))
                        link(v.tensor_tensor(rt[:], rt[:], tok1[:].unsqueeze(2).to_broadcast([P, TC, E2]), ALU.mult))
                    e_n, top = (E1, TOP1) if st == 0 else (E2, TOP2)
                    for t in range(TC):
                        ins = v.max(top8[:, t], rt[:, t, 0:e_n])
                    link(ins)
                    for t in range(TC):
                        ins = v.max_index(idx_u[:, t], top8[:, t], rt[:, t, 0:e_n])
                    link(ins)
                    link(v.tensor_copy(idx_f[:], idx_u[:]))
                    for j in range(top):
                        ins = v.tensor_tensor(onehot[:, :, j, 0:e_n], iota[:, 0:e_n].unsqueeze(1).to_broadcast([P, TC, e_n]),
                                              idx_f[:, :, j:j + 1].to_broadcast([P, TC, e_n]), ALU.is_equal)
                    link(ins)
                    if st == 0:
                        link(v.tensor_tensor(comb[:, TC * c:TC * c + TC, 0:E1], onehot[:, :, 0, 0:E1], onehot[:, :, 1, 0:E1], ALU.add))
                        link(v.tensor_tensor(comb[:, TC * c:TC * c + TC, 0:E1], comb[:, TC * c:TC * c + TC, 0:E1], logits[:, :, 0:E1], ALU.mult))
                        link(v.tensor_reduce(tok1[:], comb[:, TC * c:TC * c + TC, 0:E1], X_AXIS, ALU.add))
                        link(v.reciprocal(tok1[:], tok1[:]))
                        link(v.tensor_tensor(comb[:, TC * c:TC * c + TC, 0:E1], comb[:, TC * c:TC * c + TC, 0:E1],
                                             tok1[:].unsqueeze(2).to_broadcast([P, TC, E1]), ALU.mult))
                    else:
                        link(v.tensor_reduce(tok1[:], top8[:], X_AXIS, ALU.add))
                        link(v.tensor_scalar(tok1[:], tok1[:], 1e-12, None, ALU.max))
                        link(v.reciprocal(tok1[:], tok1[:]))
                        link(v.tensor_tensor(cum[:], top8[:], tok1[:].unsqueeze(2).to_broadcast([P, TC, 8]), ALU.mult))
                        for j in range(1, TOP2):
                            link(v.tensor_tensor(cum[:, :, j], cum[:, :, j], cum[:, :, j - 1], ALU.add))
                        link(v.tensor_scalar(cum[:], cum[:], THRESHOLD, None, ALU.is_lt))
                        link(v.tensor_tensor(top8[:, :, 1:8], top8[:, :, 1:8], cum[:, :, 0:7], ALU.mult))
                        link(v.tensor_reduce(tok1[:], top8[:], X_AXIS, ALU.add))
                        link(v.tensor_scalar(tok1[:], tok1[:], 1e-12, None, ALU.max))
                        link(v.reciprocal(tok1[:], tok1[:]))
                        link(v.tensor_tensor(top8[:], top8[:], tok1[:].unsqueeze(2).to_broadcast([P, TC, 8]), ALU.mult))
                        for j in range(top):
                            ins = v.tensor_tensor(onehot[:, :, j], onehot[:, :, j],
                                                  top8[:, :, j:j + 1].to_broadcast([P, TC, E2]), ALU.mult)
                        link(ins)
                        link(v.tensor_tensor(onehot[:, :, 0:4], onehot[:, :, 0:4], onehot[:, :, 4:8], ALU.add))
                        link(v.tensor_tensor(onehot[:, :, 0:2], onehot[:, :, 0:2], onehot[:, :, 2:4], ALU.add))
                        link(v.tensor_tensor(comb[:, TC * c:TC * c + TC], onehot[:, :, 0], onehot[:, :, 1], ALU.add))
                elif kind == "gateup":
                    _, st, e, c = step
                    n = nth[step]
                    s = n % 2
                    m = I1 if st == 0 else I2
                    t = full("T", step)
                    ve.wait_ge(sem("silu"), n)
                    if n >= 3:
                        ve.wait_ge(sem("act_lo"), n - 2)
                    read("T", t, v.tensor_tensor(act[0:m, s], gate[0:m, s], psT[t][0:m, 1], ALU.mult))
                elif kind == "down":
                    _, st, e, c, tp = step
                    ring, ps = (("M", psM), ("O", [psO[:, 0], psO[:, 1]]))[tp]
                    m = full(ring, step)
                    if (st, c, tp) in summed:
                        wait_read(ve, ring, summed[st, c, tp])
                    summed[st, c, tp] = step
                    for i in (0, 1):
                        t = TC * c + 2 * tp + i
                        ins = v.scalar_tensor_tensor(x[:, t], ps[m][:, i * D:(i + 1) * D], comb[:, t, e:e + 1], x[:, t],
                                                     ALU.mult, ALU.add)
                    read(ring, m, ins)
                elif kind == "rates":
                    ve.wait_ge(sem("rate_exp"), 1)
                    v.tensor_tensor(bc_s[:], mats[:, 1], mats[:, 2], ALU.mult).then_inc(sem("bc_ready"), 1)
                    v.tensor_scalar(sp_s[:, 2], sp_s[:, 1], 1.0, None, ALU.add).then_inc(sem("rate_one"), 1)
                    ve.wait_ge(sem("rate_one"), 1)
                    link(v.scalar_tensor_tensor(sp_s[:, 1], sp_s[:, 2], -1.0, sp_s[:, 1], ALU.add, ALU.subtract))
                    ve.wait_ge(sem("rate_log"), 1)
                    link(v.tensor_tensor(sp_s[:, 0], sp_s[:, 0], sp_s[:, 1], ALU.subtract))
                    link(v.scalar_tensor_tensor(sp_s[:, 0], mats[:, 0], 0.0, sp_s[:, 0], ALU.max, ALU.add))
                    link(v.tensor_scalar(neg_a[:], sp_s[:, 0], -1.0, None, ALU.mult))
                elif kind == "proj":
                    _, c, w, ob = step
                    cols = slice(c * CH, (c + 1) * CH)
                    nw = KD * c + ob + 1
                    t = full("T", step)
                    src = psT[t][:, 0]
                    if w == 0:
                        read("T", t, v.tensor_scalar(dtT[:, ob, cols], src, vecs[:, 0, ob:ob + 1], None, ALU.add))
                        ve.wait_ge(sem("sp_exp"), nw)
                        v.tensor_scalar(sp_c, sp_b, 1.0, None, ALU.add).then_inc(sem("sp_one"), 1)
                        ve.wait_ge(sem("sp_one"), nw)
                        link(v.scalar_tensor_tensor(sp_b, sp_c, -1.0, sp_b, ALU.add, ALU.subtract))
                        ve.wait_ge(sem("sp_log"), nw)
                        link(v.tensor_tensor(sp_b, sp_a, sp_b, ALU.subtract))
                        link(v.scalar_tensor_tensor(sp_b, dtT[:, ob, cols], 0.0, sp_b, ALU.max, ALU.add))
                        v.tensor_scalar(dtT[:, ob, cols], sp_b, DT_MIN, None, ALU.add).then_inc(sem("dt_ready"), 1)
                        ve.wait_ge(sem("dt_ready"), nw)
                    elif w == 1:
                        read("T", t, v.scalar_tensor_tensor(bT[:, ob, cols], src, vecs[:, 1, ob:ob + 1], dtT[:, ob, cols], ALU.add, ALU.mult))
                        wait_read(ve, "T", step)
                        link(v.tensor_tensor(bT[:, ob, cols], bT[:, ob, cols], uT[:, ob, cols], ALU.mult))
                    else:
                        read("T", t, v.tensor_scalar(cT[:, ob, cols], src, vecs[:, 2, ob:ob + 1], None, ALU.add))
                elif kind == "scan":
                    _, ob, k = step
                    n = nth[step]
                    ve.wait_ge(sem("decay_ready"), n)
                    if n >= 3:
                        ve.wait_ge(sem("scan_summed"), n - 2)
                    v.tensor_tensor_scan(state[:, n % 2], decay[:, n % 2], bT[:, ob], 0.0, ALU.mult, ALU.add)\
                        .then_inc(sem("scanned"), 1)
                elif kind == "y":
                    ob = step[1]
                    ve.wait_ge(sem("scan_summed"), nth[("scan", ob, NST - 1)])
                    link(v.tensor_tensor(cT[:, ob], psO[:].rearrange("p a b -> p (a b)"), cT[:, ob], ALU.mult))
                    v.scalar_tensor_tensor(yT[:, ob], uT[:, ob], vecs[:, 3, ob:ob + 1], cT[:, ob], ALU.mult, ALU.add)\
                        .then_inc(sem("y_ready"), 1)
                elif kind == "yT":
                    tp = step[1]
                    m = full("M", step)
                    read("M", m, v.tensor_tensor(x[:, 2 * tp:2 * tp + 2], x[:, 2 * tp:2 * tp + 2],
                                         psM[m][:].rearrange("p (a b) -> p a b", b=D), ALU.add))

        @block.tensor
        def _(pe):
            mm = nc.tensor.matmul
            tr = nc.tensor.transpose

            def take(ring, key, i=0):
                slot, releases, _, _ = tab[ring][key][i]
                if releases:
                    pe.wait_ge(sem(f"{ring}_read{slot}"), releases)
                return slot

            def filled(ring, slot, ins):
                ins.then_inc(sem(f"{ring}_full{slot}"), 1)

            def weights(name):
                n = order[name]
                pe.wait_ge(sem("w_split"), n + 1)
                return w_hi[:, n % 2], w_lo[:, n % 2]

            def three(out, hi, lo, rhi, rlo, start=True, stop=True):
                mm(out, hi, rlo, start=start, stop=False)
                mm(out, lo, rhi, start=False, stop=False)
                return mm(out, hi, rhi, start=False, stop=stop)

            pe.wait_ge(sem("ident_ready"), 1)
            pe.wait_ge(sem("psO_clear"), 1)
            for step in STEPS:
                kind = step[0]
                if kind == "normT":
                    _, st, c, k = step
                    pe.wait_ge(sem("normed_ready"), nth[("norm", st, c)])
                    m = take("M", step)
                    for i in range(TC):
                        ins = tr(psM[m][:, i * P:(i + 1) * P], normed[:, i, k * P:(k + 1) * P], ident[:])
                    filled("M", m, ins)
                elif kind == "qkv1":
                    t = step[1]
                    c = t // TC
                    wait_read(pe, "M", ("normT", 0, c, KD - 1))
                    s = take("T", step)
                    tc = slice(t * P, (t + 1) * P)
                    wk = [weights(("wqkv", c, k)) for k in range(KD)]
                    for k in range(KD):
                        hi, lo = wk[k]
                        for b, (a0, a1) in enumerate(((0, CH), (CH, 3 * D))):
                            ins = three(psT[s][:, b, 0:a1 - a0], xTh[:, k, tc], xTl[:, k, tc], hi[:, a0:a1], lo[:, a0:a1],
                                        start=k == 0, stop=k == KD - 1)
                        if k == KD - 1:
                            filled("T", s, ins)
                elif kind == "kT1":
                    t, half = step[1], step[2]
                    pe.wait_ge(sem("stack_lo"), t + 1)
                    m = take("M", step)
                    ks = k_stack.rearrange("p h e -> p (h e)")
                    for j in range(4):
                        a0 = (4 * half + j) * P
                        ins = tr(psM[m][:, j * P:(j + 1) * P], ks[:, a0:a0 + P], ident[:])
                    filled("M", m, ins)
                elif kind == "qT1":
                    _, c, p, again = step
                    pe.wait_ge(sem("stack_lo"), TC * (c + 1))
                    if again:
                        for use in [k for k in tab["T"] if k[0] == "max1" and k[1] == c and k[3] == p][-2:]:
                            wait_read(pe, "T", use)
                    m = take("M", step)
                    qs = q_stack.rearrange("p t h e -> p t (h e)")
                    for i in range(TC):
                        ins = tr(psM[m][:, i * P:(i + 1) * P], qs[:, i, p * P:(p + 1) * P], ident[:])
                    filled("M", m, ins)
                elif kind == "max1":
                    _, c, t, p, i = step
                    for half in (0, 1):
                        wait_read(pe, "M", ("kT1", TC * c + TC - 1, half))
                    wait_read(pe, "M", ("qT1", c, p, 0))
                    if nth[step] == 1:
                        pe.wait_ge(sem("consts_ready"), 1)
                    s = take("T", step)
                    tc = slice((t % TC) * P, (t % TC + 1) * P)
                    w = (t + 1) * P
                    for b in (0, 1):
                        if i is None:
                            h, a0, a1 = 2 * p + b, 0, w
                        else:
                            h, a0, a1 = 2 * p + i, b * CH, min(w, b * CH + CH)
                        last = a1 == w
                        ins = mm(psT[s][:, b, 0:a1 - a0], qT1[:, h, tc], kT1[:, p, a0:a1], start=True, stop=not last)
                        if last:
                            ins = mm(psT[s][:, b, a1 - a0 - P:a1 - a0], ident_b[:], mask_q[:], start=False, stop=True)
                    filled("T", s, ins)
                elif kind == "score1":
                    _, c, g, sbk, i = step
                    p = 2 * g + i
                    wait_read(pe, "M", ("qT1", c, p, 1))
                    s = take("T", step)
                    diag_block = sbk >= TC * c
                    off = max(0, sbk - TC * c) * P
                    for b in (0, 1):
                        ins = mm(psT[s][:, b, off:CH], kT1[:, p, sbk * P:(sbk + 1) * P], qT1[:, 2 * p + b, off:CH],
                                 start=True, stop=not diag_block)
                        if diag_block:
                            ins = mm(psT[s][:, b, off:off + P], ident_b[:], mask_k[:], start=False, stop=True)
                    filled("T", s, ins)
                elif kind == "pv1":
                    _, c, g, sbk, i = step
                    n = nth[step]
                    wait_read(pe, "T", ("score1",) + step[1:])
                    o = tab["O"][("o1", c, g)][0][0]
                    if sbk == 0 and i == 0 and nth[("out1", c, g)] > 2:
                        pe.wait_ge(sem("o1_out"), nth[("out1", c, g)] - 2)
                    off = max(0, sbk - TC * c) * P
                    for b in (0, 1):
                        h = 4 * g + 2 * i + b
                        q0 = 32 * (2 * i + b)
                        ins = mm(psO[q0:q0 + HD1 + 1, o, off:CH], v_aug[:, sbk, h], probs[:, n % 2, b, off:CH],
                                 start=sbk == 0, stop=sbk == TC * c + TC - 1)
                    ins.then_inc(sem("pv1_done"), 1)
                elif kind == "out1":
                    _, c, g = step
                    pe.wait_ge(sem("o1_out"), nth[step])
                    m = take("M", step)
                    for i in range(TC):
                        ins = tr(psM[m][:, i * P:(i + 1) * P], o1_T[:, i * P:(i + 1) * P], ident[:])
                    filled("M", m, ins)
                elif kind == "aT1":
                    _, c, k = step
                    for g in range(4):
                        wait_read(pe, "M", ("out1", c, g))
                    m = take("M", step)
                    for i in range(TC):
                        ins = tr(psM[m][:, i * P:(i + 1) * P], a_tok[:, i, k * P:(k + 1) * P], ident[:])
                    filled("M", m, ins)
                elif kind == "wo1":
                    _, c, tp = step
                    for k in range(KD):
                        wait_read(pe, "M", ("aT1", c, k))
                    hi, lo = weights(("wo1", c))
                    m = take("M", step)
                    for i in (0, 1):
                        for k in range(KD):
                            tc = slice((TC * c + 2 * tp + i) * P, (TC * c + 2 * tp + i + 1) * P)
                            ins = three(psM[m][:, i * D:(i + 1) * D], xTh[:, k, tc], xTl[:, k, tc],
                                        hi[:, k * D:(k + 1) * D], lo[:, k * D:(k + 1) * D], start=k == 0, stop=k == KD - 1)
                    filled("M", m, ins)
                elif kind == "qkv2":
                    _, c, g, tp = step
                    wait_read(pe, "M", ("normT", 1, c, KD - 1))
                    hi, lo = weights(("w2", c, g))
                    s = take("T", step)
                    for i in (0, 1):
                        t = TC * c + 2 * tp + i
                        tc = slice(t * P, (t + 1) * P)
                        for k in range(KD):
                            ins = three(psT[s][:, i], xTh[:, k, tc], xTl[:, k, tc], hi[:, k * CH:(k + 1) * CH],
                                        lo[:, k * CH:(k + 1) * CH], start=k == 0, stop=k == KD - 1)
                    filled("T", s, ins)
                elif kind == "kT2":
                    _, c, j = step
                    pe.wait_ge(sem("roped"), nth[("rope", c, TC - 1, "k")])
                    pe.wait_ge(sem("pass_scaled"), nth[("rope", c, TC - 1, "k")])
                    m = take("M", step)
                    for i in range(TC):
                        ins = tr(psM[m][:, i * P:(i + 1) * P], k_tok[:, i, j], ident[:])
                    filled("M", m, ins)
                elif kind == "qT2":
                    u, i = step[1], step[2]
                    c, j, hp = u
                    pe.wait_ge(sem("roped"), nth[("rope", c, TC - 1, j)])
                    pe.wait_ge(sem("pass_scaled"), nth[("rope", c, TC - 1, j)])
                    m = take("M", step)
                    for t in range(TC):
                        ins = tr(psM[m][:, t * P:(t + 1) * P], q_tok[:, t, 4 * j + 2 * hp + i], ident[:])
                    filled("M", m, ins)
                elif kind == "max2":
                    _, u, t, i = step
                    c, j, hp = u
                    for h in (0, 1):
                        wait_read(pe, "M", ("qT2", u, h))
                    wait_read(pe, "M", ("kT2", c, KV2 - 2))
                    wait_read(pe, "M", ("kT2", c, KV2 - 1))
                    s = take("T", step)
                    n = nth[("mT2", u)]
                    tc = slice((t % TC) * P, (t % TC + 1) * P)
                    w = (t + 1) * P
                    for b in (0, 1):
                        if i is None:
                            h, a0, a1 = b, 0, w
                        else:
                            h, a0, a1 = i, b * CH, min(w, b * CH + CH)
                        last = a1 == w
                        ins = mm(psT[s][:, b, 0:a1 - a0], qTh[:, n % 2, h, tc], kTh[:, j, a0:a1], start=True, stop=not last)
                        if last:
                            ins = mm(psT[s][:, b, a1 - a0 - P:a1 - a0], ident_b[:], mask_q[:], start=False, stop=True)
                    filled("T", s, ins)
                elif kind == "mT2":
                    u = step[1]
                    keys = [k for k in tab["T"] if k[0] == "max2" and k[1] == u][-2:]
                    for key in keys:
                        wait_read(pe, "T", key)
                    m = take("M", step)
                    for i in range(TC):
                        ins = tr(psM[m][:, i * P:(i + 1) * P], neg_max[:, i], ident[:])
                    filled("M", m, ins)
                elif kind == "score2":
                    _, u, sbk = step
                    c, j, hp = u
                    n = nth[("mT2", u)]
                    wait_read(pe, "M", ("mT2", u))
                    s = take("T", step)
                    diag_block = sbk >= TC * c
                    off = max(0, sbk - TC * c) * P
                    kb = slice(sbk * P, (sbk + 1) * P)
                    for b in (0, 1):
                        out = psT[s][:, b, off:CH]
                        three(out, kTh[:, j, kb], kTl[:, j, kb], qTh[:, n % 2, b, off:CH], qTl[:, n % 2, b, off:CH], stop=False)
                        ins = mm(out, pick[:, b], negmT[:, n % 2, off:CH], start=False, stop=not diag_block)
                        if diag_block:
                            ins = mm(psT[s][:, b, off:off + P], ident_b[:], mask_k[:], start=False, stop=True)
                    filled("T", s, ins)
                elif kind == "pv2":
                    _, u, sbk = step
                    c, j, hp = u
                    n = nth[step]
                    wait_read(pe, "T", ("score2",) + step[1:])
                    for tp in (0, 1):
                        wait_read(pe, "T", ("qkv2", c, 1, tp))
                    if sbk == 0:
                        if nth[("out2", u)] > 1:
                            pe.wait_ge(sem("oT_ready"), nth[("out2", u)] - 1)
                        else:
                            pe.wait_ge(sem("o1_out"), 4 * NC)
                    off = max(0, sbk - TC * c) * P
                    for b in (0, 1):
                        ins = mm(psO[:, b, off:CH], v_tok[:, sbk, j * DH2:(j + 1) * DH2], probs[:, n % 2, b, off:CH],
                                 start=sbk == 0, stop=sbk == TC * c + TC - 1)
                    ins.then_inc(sem("pv2_done"), 1)
                elif kind == "out2":
                    u = step[1]
                    c = u[0]
                    pe.wait_ge(sem("p_sum"), nth[("score2", u, TC * c + TC - 1)])
                    m = take("M", step)
                    for i in (0, 1):
                        for t in range(TC):
                            at = i * TC + t
                            ins = mm(psM[m][:, at:at + 1], p_sum[:, i, t * P:(t + 1) * P], ones[:, 0:1], start=True, stop=True)
                    filled("M", m, ins)
                elif kind == "wo2":
                    _, u, i, tp = step
                    c, j, hp = u
                    pe.wait_ge(sem("oT_ready"), nth[("out2", u)])
                    hi, lo = weights(("wo2", c, j))
                    m = take("M", step)
                    w = slice((2 * hp + i) * D, (2 * hp + i + 1) * D)
                    for b in (0, 1):
                        tc = slice((2 * tp + b) * P, (2 * tp + b + 1) * P)
                        ins = three(psM[m][:, b * D:(b + 1) * D], oTh[:, i, tc], oTl[:, i, tc], hi[:, w], lo[:, w])
                    filled("M", m, ins)
                elif kind == "router":
                    _, st, c = step
                    e_n = E1 if st == 0 else E2
                    wait_read(pe, "M", ("normT", 2 if st == 0 else 4, c, KD - 1))
                    hi, lo = weights(("rw", st, c))
                    m = take("M", step)
                    for t in range(TC):
                        tc = slice(c * CH + t * P, c * CH + (t + 1) * P)
                        for k in range(KD):
                            w = slice(k * e_n, (k + 1) * e_n)
                            ins = three(psM[m][:, t * e_n:(t + 1) * e_n], xTh[:, k, tc], xTl[:, k, tc], hi[:, w], lo[:, w],
                                        start=k == 0, stop=k == KD - 1)
                    filled("M", m, ins)
                elif kind == "gateup":
                    _, st, e, c = step
                    hi, lo = weights(("moe", st, e))
                    w_i = I1 if st == 0 else I2
                    s = take("T", step)
                    cols = slice(c * CH, (c + 1) * CH)
                    for b in (0, 1):
                        for k in range(KD):
                            w = slice((2 * k + b) * w_i, (2 * k + b + 1) * w_i)
                            ins = three(psT[s][0:w_i, b], hi[:, w], lo[:, w], xTh[:, k, cols], xTl[:, k, cols],
                                        start=k == 0, stop=k == KD - 1)
                    filled("T", s, ins)
                elif kind == "down":
                    _, st, e, c, tp = step
                    n = nth[("gateup", st, e, c)]
                    w_i = I1 if st == 0 else I2
                    pe.wait_ge(sem("act_lo"), n)
                    hi, lo = weights(("moe", st, e))
                    ring, ps = (("M", psM), ("O", [psO[:, 0], psO[:, 1]]))[tp]
                    m = take(ring, step)
                    w = slice(2 * KD * w_i, 2 * KD * w_i + D)
                    for i in (0, 1):
                        tc = slice((2 * tp + i) * P, (2 * tp + i + 1) * P)
                        ins = three(ps[m][:, i * D:(i + 1) * D], aTh[0:w_i, n % 2, tc], aTl[0:w_i, n % 2, tc],
                                    hi[0:w_i, w], lo[0:w_i, w])
                    filled(ring, m, ins)
                elif kind == "proj":
                    _, c, w, ob = step
                    wait_read(pe, "M", ("normT", 3, c, KD - 1))
                    hi, lo = weights(("ssm", c, w))
                    s = take("T", step)
                    cols = slice(c * CH, (c + 1) * CH)
                    for k in range(KD):
                        wc = slice(k * D + ob * P, k * D + (ob + 1) * P)
                        ins = three(psT[s][:, 0], hi[:, wc], lo[:, wc], xTh[:, k, cols], xTl[:, k, cols],
                                    start=k == 0, stop=k == KD - 1)
                    filled("T", s, ins)
                elif kind == "scan":
                    _, ob, k = step
                    n = nth[step]
                    if k == 0:
                        if ob == 0:
                            wait_read(pe, "O", ("down", 0, E1 - 1, NC - 1, 1))
                            wait_read(pe, "O", ("down", 0, E1 - 2, NC - 1, 1))
                        else:
                            pe.wait_ge(sem("y_ready"), ob)
                    pe.wait_ge(sem("scanned"), n)
                    pe.wait_ge(sem("diag_ready"), n)
                    for c in range(NC):
                        ins = mm(psO[:, c], diag[:, n % 2], state[:, n % 2, c * CH:(c + 1) * CH],
                                 start=k == 0, stop=k == NST - 1)
                    ins.then_inc(sem("scan_summed"), 1)
                elif kind == "yT":
                    tp = step[1]
                    pe.wait_ge(sem("y_ready"), KD)
                    m = take("M", step)
                    for i in (0, 1):
                        t = 2 * tp + i
                        for ob in range(KD):
                            ins = tr(psM[m][:, i * D + ob * P:i * D + (ob + 1) * P], yT[:, ob, t * P:(t + 1) * P], ident[:])
                    filled("M", m, ins)


def rope_tables():
    import numpy as np
    pos = np.arange(S, dtype=np.float32)
    inv = (1.0 / np.float32(1000000.0) ** (np.arange(0, RD, 2, dtype=np.float32) / RD)).astype(np.float32)
    ang = (pos[:, None] * inv[None, :]).astype(np.float32)
    cos, sin = np.cos(ang), np.sin(ang)
    def lay(t):
        return np.ascontiguousarray(t.astype(np.float32).reshape(NT, P, RD).transpose(1, 0, 2))
    return lay(np.concatenate([cos, cos], 1)), lay(np.concatenate([-sin, sin], 1))


INS = ["x", "weights", "bqkv", "bo", "lnw", "qkw", "cos", "sin", "rbias", "vecs", "mats"]


def kernel(**inputs):
    import numpy as np
    import concourse.bacc as bacc
    from concourse import mybir as mb
    from concourse.bass_utils import run_bass_kernel_spmd as run

    w = {k: np.asarray(v) for k, v in inputs.items()}

    def blocks(m):
        return m.reshape(-1, P, m.shape[-1]).transpose(1, 0, 2)

    def cols(vec):
        return vec.reshape(KD, P).T

    packed = np.zeros((N_PIECES, P, PIECE), np.float32)

    def put(n, *parts):
        at = 0
        for part in parts:
            part = part.reshape(part.shape[0], -1)
            packed[n, :part.shape[0], at:at + part.shape[1]] = part
            at += part.shape[1]

    for k in range(KD):
        put(k, w["L0_attn_Wqkv"][k * P:(k + 1) * P])
    put(2, blocks(w["L0_attn_Wo"]))
    put(3, blocks(w["L0_ffn_wk"]))
    put(4, blocks(w["L0_ffn_wv"]))
    for g in range(4):
        put(5 + g, blocks(w["L0_ffn_wq"][:, g * CH:(g + 1) * CH]))
    for j in range(KV2):
        put(9 + j, blocks(w["L0_ffn_wo"][j * 4 * DH2:(j + 1) * 4 * DH2]))
    put(13, blocks(w["L0_ffn_router_w"]))
    for e in range(E1):
        gu = np.stack([blocks(w["L0_ffn_wg"][e]), blocks(w["L0_ffn_wu"][e])], 2)
        put(14 + e, gu, w["L0_ffn_wd"][e])
    for n, name in enumerate(("Wdt", "Wb", "Wc")):
        put(22 + n, blocks(w["L1_attn_" + name]))
    put(25, blocks(w["L1_ffn_gate_weight"].T))
    for e in range(E2):
        put(26 + e, blocks(w["L1_ffn_gate_up_proj"][e].T), np.pad(w["L1_ffn_down_proj"][e].T, ((0, P - I2), (0, 0))))

    one = np.ones(D, np.float32)
    norms = [one, w["L0_ffn_ln1_w"], w["L0_ffn_ln2_w"], one, one]
    cos, sin = rope_tables()
    qkw = np.stack([w["L0_ffn_knorm_w"], w["L0_ffn_knorm_w"]]
                   + [w["L0_ffn_qnorm_w"][g * CH:(g + 1) * CH] for g in range(4)])
    vecs = np.stack([cols(w["L1_attn_" + n]) for n in ("bdt", "bb", "bc", "D")], 1)
    mats = np.stack([blocks(w["L1_attn_" + n]).reshape(P, -1) for n in ("a_raw", "B_base", "C_base")], 1)
    arrays = {
        "x": w["L0_attn_x"], "weights": packed, "bqkv": w["L0_attn_bqkv"], "bo": w["L0_attn_bo"],
        "lnw": np.stack([cols(n) for n in norms], 1), "qkw": qkw, "cos": cos, "sin": sin,
        "rbias": w["L0_ffn_router_bias"], "vecs": vecs, "mats": mats,
    }
    arrays = {n: np.ascontiguousarray(v) for n, v in arrays.items()}
    nc = bacc.Bacc("TRN2", target_bir_lowering=False, num_devices=1)
    aps = {n: nc.dram_tensor(n + "_dram", arrays[n].shape, mb.dt.from_np(arrays[n].dtype), kind="ExternalInput").ap()
           for n in INS}
    out = nc.dram_tensor("out_dram", (1, S, D), mb.dt.float32, kind="ExternalOutput").ap()
    build(nc, aps, out)
    r = run(nc, [{n + "_dram": v for n, v in arrays.items()}], core_ids=[0])
    return r.results[0]["out_dram"]
```

```python
from contextlib import ExitStack
from math import prod

import concourse.bass as bass
from concourse import mybir

F32 = mybir.dt.float32
F32R = mybir.dt.float32r
BF16 = mybir.dt.bfloat16
U32 = mybir.dt.uint32
ALU = mybir.AluOpType
ACT = mybir.ActivationFunctionType
X_AXIS = mybir.AxisListType.X

P = 128
S = 1024
D = 256
KD = D // P
NT = S // P
CH = 512
NC = S // CH
TC = CH // P
H1, HD1 = 16, 16
PR1 = H1 // 2
H2, KV2, DH2, RD = 16, 4, 128, 64
E1, I1, TOP1 = 8, 128, 2
E2, I2, TOP2 = 32, 96, 8
WIDTH = (I1, I2)
BLOCKS = (E1 * I1 // P, E2 * I2 // P)
THRESHOLD = 0.8
NST = 16
DT_MIN = 0.0001
MASKED = -1.0e30
PIECE = 1024



GROUPS = (0, 2, 3, 4, 5, 1)
SCAN_INPUTS = ((0, 0), (0, 2), (1, 0), (0, 1), (1, 2), (1, 1))


def weight_stream():
    out = []
    for c in range(NC):
        out += [(("wqkv", c, k), k, 3 * D) for k in range(KD)]
        out.append((("wo1", c), 2, KD * D))
    for c in range(NC):
        out += [(("w2", c, g), 3 + g, KD * CH) for g in GROUPS]
        out += [(("wo2", c, j), 9 + j, 4 * D) for j in range(KV2)]
    out += [(("moe", 0, b), 13 + b, 2 * KD * P + D) for b in range(BLOCKS[0])]
    out += [(("ssm", c, w), 21 + w, KD * D) for c, w in SCAN_INPUTS]
    out += [(("moe", 1, b), 24 + b, 2 * KD * P + D) for b in range(BLOCKS[1])]
    return out


N_PIECES = 24 + BLOCKS[1]



def spread(main, side):
    out, at = [], 0
    for n, run in enumerate(main):
        out += run
        upto = -(-(n + 1) * len(side) // len(main))
        out += side[at:upto]
        at = upto
    return out + side[at:]


def norm_steps(stage, c):
    return [("norm", stage, c)] + [("normT", stage, c, k) for k in range(KD)]


def softmax_steps(units, blocks, side):
    out, behind = [], []
    for n, u in enumerate(units):
        extra = dict(side(n))
        for k, b in enumerate(blocks(u)):
            out.append(("score",) + b)
            out += extra.pop((k, 0), [])
            out += behind + extra.pop((k, 1), [])
            behind = [("pv",) + b]
        assert not extra, extra
    return out + behind + [step for steps in side(len(units)).values() for step in steps]


def place(*pairs):
    out = {}
    for steps, places in pairs:
        assert len(steps) == len(places), (steps, places)
        for step, at in zip(steps, places):
            out.setdefault(at, []).extend(step if isinstance(step, list) else [step])
    return out


ALL = "all"


def tile_range(c):
    return (0, NT) if c == ALL else (TC * c, TC * c + TC)


def norm_ring(stage):
    return "T" if stage == 3 else "M"


def attention1(c):
    def maxima(p):
        out = []
        for t in range(TC * c, TC * c + TC):
            ends = [[("max1", c, t, p, i, c)] for i in (0, 1)]
            if (t + 1) * P - c * CH <= CH // 2:
                ends = [ends[0] + ends[1]]
            out += [[("max1", c, t, p, i, half)] for half in range(c) for i in (0, 1)] + ends
        out[-1].append(("join1", c, p))
        return out

    def side(g):
        at = [(k, h) for k in range(2 * (TC * c + TC)) for h in (0, 1)][1:]
        parts = []
        if g:
            parts.append(([[("out1", c, g - 1)]], at[:1]))
        if g < 3:
            pairs = [maxima(2 * g + 2 + i) for i in (0, 1)]
            n = len(pairs[0])
            parts += [(pairs[0], at[:n]), ([[("qT1", c, 2 * g + 2, 1)]], [at[n + 1]]),
                      (pairs[1], at[n:2 * n]), ([[("qT1", c, 2 * g + 3, 1)]], [at[2 * n + 1]])]
        if g == 3:
            if c == 0:
                parts.append((norm_steps(0, 1), [(0, 1), (6, 1), (7, 0)]))
            else:
                parts += [(norm_steps(1, 0), [(2, 1), (12, 1), (13, 1)]), ([("root", 1, 0, i) for i in (0, 1)], [(4, 0), (6, 0)])]
        return place(*parts)

    tiles = range(TC * c, TC * c + TC)
    out = [("qkv1", tiles[0])]
    for t in tiles[1:]:
        out += [("qkv1", t)] + [("kT1", t - 1, half) for half in (0, 1)]
    out += [("kT1", tiles[-1], half) for half in (0, 1)]
    out += [("qT1", c, p, 0) for p in range(PR1)]
    for p in (0, 1):
        out += [step for steps in maxima(p) for step in steps] + [("qT1", c, p, 1)]
    blocks = lambda g: [(c, g, sb, i) for sb in range(TC * c + TC) for i in (0, 1)]
    out += [(s[0] + "1",) + s[1:] if s[0] in ("score", "pv") else s for s in softmax_steps(range(4), blocks, side)]
    out += [("aT1", c, k) for k in range(KD)]
    out += [("wo1", c, tp) for tp in range(TC // 2)]
    return out


def attention2(c):
    units = [(c, j, hp) for j in range(KV2) for hp in range(2)]

    def maxima(u):
        out = []
        for t in range(TC * c, TC * c + TC):
            out += [("max2", u, t, None)] if c == 0 else [("max2", u, t, i) for i in (0, 1)]
        return out

    def side(n):
        parts = []
        if n:
            wo = [("wo2", units[n - 1], i, tp) for tp in range(TC // 2) for i in (0, 1)]
            places = [(2, 1), (2, 1), (3, 0), (3, 1)] if c == 0 else [(2, 1), (3, 1), (4, 1), (5, 1)]
            parts += [([("out2", units[n - 1])], [(0, 1)]), (wo, places)]
        if n + 1 < len(units):
            places = [(0, 1), (1, 0), (1, 1), (2, 0)] if c == 0 else [(0, 1), (1, 0), (1, 1), (2, 0), (3, 0), (4, 0), (5, 0), (6, 0)]
            parts += [(maxima(units[n + 1]), places), ([("mT2", units[n + 1])], [(3, 0) if c == 0 else (7, 0)])]
        if n % 2 == 0 and n + 2 < len(units):
            places = [(1, 0), (1, 1), (2, 0), (2, 1)] if c == 0 else [(2, 0), (3, 0), (4, 0), (5, 0)]
            parts.append(([("rope", c, t, units[n + 2][1]) for t in range(TC)], places))
        if n + 2 < len(units):
            last = (TC * c + TC - 1, 1)
            parts.append(([("qT2", units[n + 2], i) for i in (0, 1)], [last, last]))
        if c == 0 and n == len(units) - 1:
            parts += [(norm_steps(1, 1), [(0, 1), (3, 1), (3, 1)]), ([("root", 1, 1, i) for i in (0, 1)], [(1, 1), (2, 1)])]
        if c == NC - 1 and n == 0:
            parts.append((norm_steps(2, 0) + [("router", 0, 0), ("logits", 0, 0), ("pick", 0, 0), ("combine", 0, 0),
                           ("combT", 0, 0)], [(1, 1), (2, 1), (3, 1), (4, 0), (4, 1), (5, 1), (6, 1), (6, 1)]))
        return place(*parts)

    out = [("qkv2", c, 0, tp) for tp in range(TC // 2)]
    out.append(("rms2", c, "k"))
    keys = [("rope", c, t, "k") for t in range(TC)] + [("kT2", c, j) for j in range(KV2)]
    out += spread([[("qkv2", c, g, tp)] for g in range(2, 6) for tp in range(TC // 2)], keys)
    out.append(("rms2", c, "q"))
    out += spread([[("qkv2", c, 1, tp)] for tp in range(TC // 2)], [("rope", c, t, 0) for t in range(TC)])
    out += [("qT2", units[0], i) for i in (0, 1)] + maxima(units[0]) + [("mT2", units[0])]
    out += [("qT2", units[1], i) for i in (0, 1)]
    blocks = lambda u: [(u, sb) for sb in range(TC * c + TC)]
    return out + [(s[0] + "2",) + s[1:] if s[0] in ("score", "pv") else s for s in softmax_steps(units, blocks, side)]


ACT_SLOTS, PART_SLOTS, SHARE_SLOTS = 6, 3, 4


HEAD, TAIL = 3, 2


def expert_jobs(stage):
    n, jobs = BLOCKS[stage], []
    for first, last in [(0, HEAD)] + [(b, b + 1) for b in range(HEAD, n - TAIL)] + [(n - TAIL, n)]:
        jobs += [(b, c) for c in range(NC) for b in range(first, last)]
    return jobs


def experts(stage, ready, opening, closing):
    jobs, out, ready = expert_jobs(stage), [], set(ready)
    weighed = downs = 0

    def weigh(upto):
        nonlocal weighed
        while weighed < upto and jobs[weighed][1] in ready and weighed - downs < PART_SLOTS:
            out.append(("weigh", stage) + jobs[weighed])
            weighed += 1

    for i, job in enumerate(jobs):
        while any(b <= job[0] - 3 for b, _ in jobs[downs:i]):
            weigh(i)
            out.append(("down", stage) + jobs[downs])
            downs += 1
            weigh(i)
        before = weighed
        assert i - weighed < ACT_SLOTS
        out.append(("gateup", stage) + job)
        weigh(i + 1)
        for step in opening.get(i, []):
            out.append(step)
            if step[0] == "combT":
                ready.add(step[2])
        weigh(i + 1)
        if i == len(jobs) - 1:
            out.append(("add", stage, 0))
        while downs < before and downs <= i - 2:
            out.append(("down", stage) + jobs[downs])
            downs += 1
            weigh(i + 1)
    out += [("sumT", stage, 0)] + closing
    while downs < len(jobs):
        weigh(len(jobs))
        out.append(("down", stage) + jobs[downs])
        downs += 1
    return out


def all_steps():
    out = norm_steps(0, 0) + attention1(0) + attention1(1)
    for c in range(NC):
        out += attention2(c)
    out += experts(0, [0], {0: [("norm", 2, 1)],
                            1: [*[("normT", 2, 1, k) for k in range(KD)]],
                            2: [("router", 0, 1)],
                            3: [("logits", 0, 1), ("pick", 0, 1), ("combine", 0, 1)],
                            4: [("combT", 0, 1)]},
                   [("norm", 3, 0)])
    out += [("normT", 3, 0, k) for k in range(KD)] + [("add", 0, 1), ("sumT", 0, 1), ("norm", 3, 1), ("rates",)]
    for n, (c, w) in enumerate(SCAN_INPUTS):
        out += [("proj", c, w, ob) for ob in range(KD)]
        if (c, w) == (0, 0):
            out.append(("soft", 0))
        elif (c, w) == (0, 2):
            out += [("normT", 3, 1, k) for k in range(KD)]
        elif (c, w) == (0, 1):
            out.append(("soft", 1))
    for ob in range(KD):
        out += [("scan", ob, n) for n in range(NST)] + [("y", ob)]
    out += [("yT", tp) for tp in range(NT // 2)]
    out += norm_steps(4, 0) + [("norm", 4, 1)]
    return out + experts(1, [], {0: [*[("normT", 4, 1, k) for k in range(KD)]],
                            1: [*[("router", 1, c) for c in range(NC)], ("logits", 1, ALL), ("pick", 1, ALL)],
                            2: [("combine", 1, ALL)],
                            3: [("share", 1, ALL)],
                            5: [*[("combT", 1, c) for c in range(NC)]]},
                         []) + [("add", 1, 1), ("sumT", 1, 1)]


STEPS = all_steps()

RINGS = {
    "T": {"qkv1": (1, 1), "score1": (1, 1), "qkv2": (1, 1), "max2": (1, 1), "score2": (1, 1),
          "gateup": (1, 1), "sumT": (1, 1), "proj": (1, 1), "normT": (1, 1)},
    "M": {"normT": (1, 1), "max1": (1, 1), "kT1": (1, 1), "qT1": (1, 2), "out1": (1, 1), "aT1": (1, 1), "wo1": (1, 1),
          "kT2": (1, 1), "qT2": (1, 1), "mT2": (1, 1), "out2": (1, 1), "wo2": (1, 1), "router": (1, 1), "logits": (1, 1),
          "combT": (1, 1), "acc": (2, 1), "yT": (1, 1)},
    "O": {"o1": (1, 0), "o2": (2, 0), "y": (2, 0), "acc": (2, 1)},
}


def ring_table(ring):
    kinds = RINGS[ring]
    released, filled, n, table = [0, 0], [0, 0], 0, {}
    for step in STEPS:
        key = step
        if step[0] == "normT" and ring != norm_ring(step[1]):
            continue
        if step[0] == "down":
            key = ("acc", step[1], step[3])
            if key in table or ring != ("O", "M")[step[3]]:
                continue
        elif ring == "O":
            if step[0] == "score1" and step[3] == 0 and step[4] == 0:
                key = ("o1", step[1], step[2])
            elif step[0] == "score2" and step[2] == 0:
                key = ("o2", step[1])
            elif step[0] == "scan" and step[2] == 0:
                key = ("y", step[1])
            else:
                continue
        if key[0] not in kinds:
            continue
        slots, ends = kinds[key[0]]
        table[key] = []
        for _ in range(slots):
            s = n % 2
            filled[s] += ends > 0 and key[0] != "acc"
            table[key].append((s, released[s], filled[s], released[s] + ends))
            released[s] += ends
            n += 1
    return table


def ordinals():
    count, out = {}, {}
    for step in STEPS:
        count[step[0]] = count.get(step[0], 0) + 1
        out[step] = count[step[0]]
    return out


def build(nc, a, out_dram):
    tab = {r: ring_table(r) for r in RINGS}
    nth = ordinals()
    stream = weight_stream()
    mts = [st for st in STEPS if st[0] == "mT2"]
    outs = [st for st in STEPS if st[0] == "out2"]
    sums = [st for st in STEPS if st[0] == "sumT"]
    gus = [st for st in STEPS if st[0] == "gateup"]
    order = {name: n for n, (name, _, _) in enumerate(stream)}

    with ExitStack() as ctx:
        def psum(name, shape):
            return ctx.enter_context(nc.psum_tensor(name, shape, F32))

        def sb(name, shape, dt=F32):
            return ctx.enter_context(nc.sbuf_tensor(name, shape, dt))

        sems = {}

        def sem(name):
            if name not in sems:
                sems[name] = ctx.enter_context(nc.semaphore(name))
            return sems[name]

        psT = [psum("psT0", [P, 2, CH]), psum("psT1", [P, 2, CH])]
        psO = psum("psO", [P, 2, CH])
        psM = [psum("psM0", [P, CH]), psum("psM1", [P, CH])]

        x = sb("x", [P, NT, D])
        xn = sb("xn", [P, NT, D])
        normed = sb("normed", [P, TC, D])
        xTh = sb("xTh", [P, KD, S], F32R)
        xTl = sb("xTl", [P, KD, S], F32R)
        w_raw = sb("w_raw", [P, 2, PIECE])
        w_hi = sb("w_hi", [P, 2, PIECE], F32R)
        w_lo = sb("w_lo", [P, 2, PIECE], F32R)
        probs = sb("probs", [P, 2, 2, CH])
        ident = sb("ident", [P, P])
        ones = sb("ones", [P, P])
        ident_b = sb("ident_b", [P, P], BF16)
        mask_q = sb("mask_q", [P, P], BF16)
        mask_k = sb("mask_k", [P, P], BF16)
        max_parts = sb("max_parts", [P, 2, NC, TC, 2])
        iota = sb("iota", [P, E2])
        iota_i = sb("iota_i", [P, E2], mybir.dt.int32)
        lnw = sb("lnw", [P, 5, KD])
        bn6 = sb("bn6", [P, TC, 6])
        mv = sb("mv", [P, TC, 2])
        rs = sb("rs", [P, 3, TC])
        ms = sb("ms", [P, 2, TC])
        r_q = sb("r_q", [P, TC])
        r_k = sb("r_k", [P, TC])
        FN, RN = 17440, 16 * 1024
        fr = sb("fr", [P, FN])
        rr = sb("rr", [P, RN], F32R)

        class Carve:
            def __init__(self, base, limit):
                self.base, self.limit, self.at = base, limit, 0

            def take(self, *dims):
                n = prod(dims)
                v = self.base[:, self.at:self.at + n]
                self.at += n
                assert self.at <= self.limit, (self.at, self.limit)
                if len(dims) == 2:
                    return v.rearrange("p (a b) -> p a b", b=dims[1])
                if len(dims) == 3:
                    return v.rearrange("p (a b c) -> p a b c", b=dims[1], c=dims[2])
                return v

        f, r = Carve(fr, FN), Carve(rr, RN)
        bqkv_b = f.take(3 * D)
        bo_b = f.take(D)
        qkv_tok = f.take(3 * D)
        q_stack = f.take(TC, H1, 64)
        k_stack = f.take(H1, 64)
        v_aug = f.take(NT, H1, HD1 + 1)
        o1_T = f.take(CH)
        a_tok = f.take(TC, D)
        den1 = f.take(TC, 4)
        kT1 = r.take(PR1, S)
        qT1 = r.take(H1, CH)
        f, r = Carve(fr, FN), Carve(rr, RN)
        q_tok = f.take(TC, H2, DH2)
        k_tok = f.take(TC, KV2, DH2)
        p_sum = k_tok.rearrange("p a b c -> p (a b c)")[:, 0:2 * CH].rearrange("p (a b) -> p a b", b=CH)
        v_tok = f.take(NT, CH)
        qkw = f.take(2, CH)
        cos_t = f.take(NT, RD)
        sin_t = f.take(NT, RD)
        neg_max = f.take(TC, P)
        ssq = f.take(TC, 8)
        rope_tmp = f.take(2, 4, RD)
        kTh = r.take(KV2, S)
        kTl = r.take(KV2, S)
        qTh = r.take(2, 2, CH)
        qTl = r.take(2, 2, CH)
        negmT = r.take(2, CH)
        pick = r.take(2, P)
        oTh = r.take(2, CH)
        oTl = r.take(2, CH)
        combT = qkw[:, 0]
        f, r = Carve(fr, FN), Carve(rr, RN)
        gate = f.take(2, CH)
        act = f.take(ACT_SLOTS, CH)
        aTh = r.take(PART_SLOTS, CH)
        aTl = r.take(PART_SLOTS, CH)
        share = probs[:].rearrange("p a b c -> p (a b) c")
        accT = xn[:].rearrange("p t d -> p (t d)")[:, 0:KD * CH].rearrange("p (k c) -> p k c", c=CH)
        w_hi3, w_lo3 = r.take(PIECE), r.take(PIECE)
        uT = f.take(KD, S)
        dtT = f.take(KD, S)
        bT = f.take(KD, S)
        cT = f.take(KD, S)
        decay = f.take(2, S)
        state = f.take(2, S)
        sp_a, sp_b, sp_c = (v.rearrange("p (k c) -> p k c", c=CH) for v in (decay[:, 0], decay[:, 1], state[:, 0]))
        diag = f.take(2, P)
        routed = ((qkw[:, 1], qkw[:, 1]), (decay[:, 0, 0:CH], decay[:, 0, CH:S]))
        onehots = (normed[:].rearrange("p t (j e) -> p t j e", e=E2),
                   state.rearrange("p a (t j e) -> p (a t) j e", j=8, e=E2))
        yT = uT
        rbias = sb("rbias", [P, E1])
        rw = sb("rw", [P, KD, E1 + E2])
        logits = sb("logits", [P, NT, E2])
        rt = sb("rt", [P, NT, E2])
        comb = sb("comb", [P, NT, E2])
        top8 = sb("top8", [P, NT, 8])
        idx_u = sb("idx_u", [P, NT, 8], U32)
        idx_f = sb("idx_f", [P, NT, 8])
        cum = idx_f
        tok1 = sb("tok1", [P, NT])
        rden = sb("rden", [P, 2, TC])
        vecs = sb("vecs", [P, 4, KD])
        mats = sb("mats", [P, 3, KD * NST])
        sp_s = sb("sp_s", [P, 3, KD * NST])
        neg_a = sb("neg_a", [P, KD * NST])
        bc_s = sb("bc_s", [P, KD * NST])

        scratch = nc.dram_tensor("share_scratch", (2, E2, S), F32).ap()

        n0 = order[("moe", 0, 0)]

        def w_slot(n):
            return n % 2 if n < n0 else (n0 % 2, (n0 + 1) % 2, 2)[(n - n0) % 3]

        def w_before(n):
            return n - 2 if n < n0 + 2 else None if n == n0 + 2 else n - 3

        def split_views(n):
            i = w_slot(n)
            return (w_hi3, w_lo3) if i == 2 else (w_hi[:, i], w_lo[:, i])

        jobs = [(st, b, c) for st in (0, 1) for b, c in expert_jobs(st)]
        share_dmas, loaded = {}, [0] * SHARE_SLOTS
        for n, (st, b, c) in enumerate(jobs):
            rows = [(e, max(0, e * WIDTH[st] - b * P), min(P, (e + 1) * WIDTH[st] - b * P))
                    for e in range(b * P // WIDTH[st], ((b + 1) * P - 1) // WIDTH[st] + 1)]
            loaded[n % SHARE_SLOTS] += 16 * len(rows)
            share_dmas[st, b, c] = (n, rows, loaded[n % SHARE_SLOTS])

        def last_down(st, c):
            return nth[[("down",) + j for j in jobs if (j[0], j[2]) == (st, c)][-1]]

        def acc_bank(c, ring_slot):
            return psM[ring_slot][:] if c else psO[:, ring_slot]

        block = ctx.enter_context(nc.Block())

        def wait_full(eng, ring, use, i=0):
            slot, _, fills, _ = tab[ring][use][i]
            eng.wait_ge(sem(f"{ring}_full{slot}"), fills)
            return slot

        def rope_part(which, t):
            if which == "k":
                return k_tok[:, t], r_k[:, t:t + 1]
            return q_tok[:, t, 4 * which:4 * which + 4], r_q[:, t:t + 1]

        def wait_read(eng, ring, use, i=0):
            slot, _, _, ends = tab[ring][use][i]
            eng.wait_ge(sem(f"{ring}_read{slot}"), ends)

        def wait_read_all(eng, ring, uses):
            for slot in (0, 1):
                ends = [tab[ring][u][0][3] for u in uses if tab[ring][u][0][0] == slot]
                if ends:
                    eng.wait_ge(sem(f"{ring}_read{slot}"), max(ends))

        @block.sync
        def _(sp):
            def load_x(c):
                sp.dma_start(x[:, TC * c:TC * c + TC], a["x"][:, c * CH:(c + 1) * CH].rearrange("a (t p) d -> p (a t) d", p=P))\
                    .then_inc(sem(f"x_loaded{c}"), 16)

            load_x(0)
            rows, to_share = [], list(jobs)

            def spread_shares(stage, upto):
                while to_share and to_share[0][0] == stage and to_share[0][1] <= upto:
                    job = to_share.pop(0)
                    st, b, c = job
                    n, segments, _ = share_dmas[job]
                    if b == 0:
                        k = nth[("combT", st, c)]
                        wait_read(sp, "M", ("combT", st, c))
                        e_n = (E1, E2)[st]
                        sp.dma_start(scratch[st, 0:e_n, c * CH:(c + 1) * CH], combT[0:e_n]).then_inc(sem("combT_stored"), 16)
                        sp.wait_ge(sem("combT_stored"), 16 * k)
                    if n == 0:
                        wait_full(sp, "M", [k for k in STEPS if k[0] == "wo2"][-1])
                    if n >= SHARE_SLOTS:
                        sp.wait_ge(sem("weighed"), n - SHARE_SLOTS + 1)
                    for e, r0, r1 in segments:
                        sp.dma_start(share[r0:r1, n % SHARE_SLOTS], scratch[st, e, c * CH:(c + 1) * CH].partition_broadcast(r1 - r0))\
                            .then_inc(sem(f"share_loaded{n % SHARE_SLOTS}"), 16)

            for n, (name, at, width) in enumerate(stream):
                if n >= 2:
                    sp.wait_ge(sem("w_split"), n - 1)
                sp.dma_start(w_raw[:, n % 2, 0:width], a["weights"][at, :, 0:width]).then_inc(sem(f"w_loaded{n % 2}"), 16)
                if name[0] == "w2" and name[2] != 1:
                    g = name[2]
                    if len(rows) >= 2:
                        wait_read(sp, "T", rows[-2])
                    sp.dma_start(qkw[:, len(rows) % 2], a["qkw"][g].partition_broadcast(P)).then_inc(
                        sem(f"row_loaded{len(rows) % 2}"), 16)
                    rows.append(("qkv2", name[1], g, TC // 2 - 1))
                if n == KD - 1:
                    for dst, src in ((lnw[:], a["lnw"]), (bqkv_b, a["bqkv"].partition_broadcast(P)), (bo_b, a["bo"].partition_broadcast(P)),
                                     (rbias[:], a["rbias"].partition_broadcast(P)), (rw[:], a["rw"]), (vecs[:], a["vecs"]),
                                     (mats[:], a["mats"])):
                        sp.dma_start(dst, src).then_inc(sem("consts_loaded"), 16)
                    load_x(1)
                if n == KD:
                    sp.dma_start(cos_t, a["cos"]).then_inc(sem("tables_loaded"), 16)
                    sp.dma_start(sin_t, a["sin"]).then_inc(sem("tables_loaded"), 16)
                if name[0] == "moe":
                    b = name[2]
                    spread_shares(name[1], BLOCKS[name[1]] if b == BLOCKS[name[1]] - 1 else b - 2)
            for c in range(NC):
                wait_read(sp, "T", ("sumT", 1, c))
                sp.dma_start(out_dram[:, c * CH:(c + 1) * CH].rearrange("a (t p) d -> p (a t) d", p=P),
                             x[:, TC * c:TC * c + TC]).then_inc(sem("stored"), 16)
            sp.wait_ge(sem("stored"), 16 * NC)

        @block.gpsimd
        def _(pool):
            g = nc.gpsimd
            chained = [0]

            def link(ins):
                chained[0] += 1
                ins.then_inc(sem("pool_chain"), 1)
                pool.wait_ge(sem("pool_chain"), chained[0])

            link(g.memset(ident[:], 0.0))
            g.affine_select(out=ident[:], in_=ident[:], compare_op=ALU.not_equal, fill=1.0, base=0,
                            pattern=[[-1, P]], channel_multiplier=1).then_inc(sem("ident_ready"), 1)
            last_use = {}
            for step in STEPS:
                kind = step[0]
                if kind == "qkv1":
                    for k in range(KD):
                        last_use[("wqkv", step[1] // TC, k)] = step
                elif kind == "wo1":
                    last_use[("wo1", step[1])] = step
                elif kind == "qkv2":
                    last_use[("w2", step[1], step[2])] = step
                elif kind == "wo2":
                    last_use[("wo2", step[1][0], step[1][1])] = step
                elif kind == "down":
                    last_use[("moe", step[1], step[2])] = step
                elif kind == "proj":
                    last_use[("ssm", step[1], step[2])] = step
            after = {}
            for n in range(2, len(stream)):
                before = w_before(n)
                use = [k for k in STEPS if k[0] == "wo2"][-1] if before is None else last_use[stream[before][0]]
                after.setdefault(use, []).append(n)

            split_upto = [0]

            def split_next():
                n = split_upto[0]
                name, _, width = stream[n]
                pool.wait_ge(sem(f"w_loaded{n % 2}"), 16 * (n // 2 + 1))
                if n >= 2:
                    before = w_before(n)
                    use = [k for k in STEPS if k[0] == "wo2"][-1] if before is None else last_use[stream[before][0]]
                    if use[0] == "down":
                        pool.wait_ge(sem("down_done"), nth[use])
                    else:
                        wait_full(pool, "T" if use[0] in RINGS["T"] else "M", use)
                hi, lo = (view[:, 0:width] for view in split_views(n))
                raw = w_raw[:, n % 2, 0:width]
                link(g.tensor_scalar(hi, raw, 1.0, 0.0, ALU.mult, ALU.add))
                g.tensor_tensor(lo, raw, hi.bitcast(F32), ALU.subtract).then_inc(sem("w_split"), 1)
                split_upto[0] += 1

            split_next()
            split_next()
            g.memset(v_aug, 1.0)
            g.memset(q_stack, 0.0)
            g.memset(mask_q[:], 0.0)
            g.memset(mask_k[:], 0.0)
            link(g.memset(k_stack, 0.0))
            g.memset(k_stack[:, :, 48:49], 1.0).then_inc(sem("stacks_clear"), 1)
            pool.wait_ge(sem("ident_ready"), 1)
            g.memset(ones[:], 1.0)
            g.tensor_copy(ident_b[:], ident[:])
            g.affine_select(out=mask_q[:], in_=mask_q[:], compare_op=ALU.is_ge, fill=MASKED, base=0,
                            pattern=[[-1, P]], channel_multiplier=1)
            g.affine_select(out=mask_k[:], in_=mask_k[:], compare_op=ALU.is_ge, fill=MASKED, base=0,
                            pattern=[[1, P]], channel_multiplier=-1)
            link(g.iota(iota_i[:], pattern=[[1, E2]], base=0, channel_multiplier=0))
            g.tensor_copy(iota[:], iota_i[:]).then_inc(sem("consts_ready"), 1)

            for step in STEPS:
                kind = step[0]
                if kind == "qkv2" and step[1:] == (0, 0, 0):
                    wait_read(pool, "M", ("wo1", NC - 1, TC // 2 - 1))
                    g.memset(neg_max, 0.0)
                    link(g.memset(pick.bitcast(F32), 0.0))
                    for i in (0, 1):
                        ins = g.affine_select(out=pick[:, i], in_=pick[:, i].bitcast(F32), compare_op=ALU.not_equal, fill=1.0,
                                              base=-i, pattern=[[0, P]], channel_multiplier=1)
                    ins.then_inc(sem("pick_ready"), 1)
                if kind == "score2":
                    u, sbk = step[1], step[2]
                    c = u[0]
                    off = max(0, sbk - TC * c) * P
                    n = nth[step]
                    wait_read(pool, "T", step)
                    pr = probs[:, n % 2]
                    if sbk == 0:
                        if u == (c, 0, 0):
                            wait_full(pool, "M", ("kT2", c, KV2 - 1))
                        else:
                            wait_full(pool, "M", outs[nth[("out2", u)] - 2])
                        g.tensor_scalar(p_sum, pr, 1.0, 0.0, ALU.mult, ALU.add).then_inc(sem("p_sum"), 1)
                    else:
                        pool.wait_ge(sem("p_sum"), n - 1)
                        g.tensor_tensor(p_sum[:, :, off:CH], p_sum[:, :, off:CH], pr[:, :, off:CH],
                                        ALU.add).then_inc(sem("p_sum"), 1)
                if kind == "weigh":
                    n = nth[step]
                    s, at = n % PART_SLOTS, n % ACT_SLOTS
                    pool.wait_ge(sem("act_hi"), n)
                    if n > PART_SLOTS:
                        pool.wait_ge(sem("down_done"), n - PART_SLOTS)
                    g.tensor_tensor(aTl[:, s], act[:, at], aTh[:, s].bitcast(F32), ALU.subtract).then_inc(sem("act_lo"), 1)
                if kind == "scan":
                    n = nth[step]
                    if n == 1:
                        pool.wait_ge(sem("bc_ready"), 1)
                    if n >= 3:
                        pool.wait_ge(sem("scan_summed"), n - 2)
                    col = step[1] * NST + step[2]
                    g.tensor_scalar(diag[:, n % 2], ident[:], bc_s[:, col:col + 1], 1.0, ALU.mult, ALU.mult)\
                        .then_inc(sem("diag_ready"), 1)
                for n in after.get(step, ()):
                    assert n == split_upto[0]
                    split_next()

        @block.scalar
        def _(sc):
            s_ = nc.scalar
            chained = [0]

            def link(ins):
                chained[0] += 1
                ins.then_inc(sem("act_chain"), 1)
                sc.wait_ge(sem("act_chain"), chained[0])

            def full(ring, use, i=0):
                return wait_full(sc, ring, use, i)

            def read(ring, slot, ins):
                ins.then_inc(sem(f"{ring}_read{slot}"), 1)

            sc.wait_ge(sem("consts_loaded"), 16 * 7)
            roots, squares = 0, 0
            for step in STEPS:
                kind = step[0]
                if kind == "root" or kind == "norm" and step[1] != 1:
                    roots += 1
                    sc.wait_ge(sem("var_ready"), roots)
                    s_.activation(rs[:, 1, :], rs[:, 0, :], ACT.Sqrt).then_inc(sem("root_ready"), 1)
                elif kind == "normT":
                    _, st, c, k = step
                    m = full(norm_ring(st), step)
                    src = psT[m][:, 0] if st == 3 else psM[m][:]
                    s_.activation(xTh[:, k, c * CH:(c + 1) * CH], src, ACT.Identity,
                                  scale=lnw[:, st, k:k + 1]).then_inc(sem("xTh_ready"), 1)
                elif kind == "qkv1":
                    t = step[1]
                    i = t % TC
                    wait_read(sc, "T", step)
                    if t == 0:
                        sc.wait_ge(sem("stacks_clear"), 1)
                    q3 = qkv_tok[:, 0:D].rearrange("p (h d) -> p h d", d=HD1)
                    k3 = qkv_tok[:, D:2 * D].rearrange("p (h d) -> p h d", d=HD1)
                    v3 = qkv_tok[:, 2 * D:3 * D].rearrange("p (h d) -> p h d", d=HD1)
                    s_.activation(q_stack[:, i, :, 0:16].bitcast(F32R), q3, ACT.Copy, scale=HD1 ** -0.5)
                    s_.activation(q_stack[:, i, :, 32:48].bitcast(F32R), q3, ACT.Copy, scale=HD1 ** -0.5)
                    if t >= 1:
                        wait_full(sc, "M", ("kT1", t - 1, 1))
                    s_.activation(k_stack[:, :, 0:16].bitcast(F32R), k3, ACT.Copy)
                    s_.activation(k_stack[:, :, 16:32].bitcast(F32R), k3, ACT.Copy)
                    s_.activation(v_aug[:, t, :, 0:HD1], v3, ACT.Copy).then_inc(sem("stack_hi"), 1)
                elif kind == "kT1":
                    t, half = step[1], step[2]
                    m = full("M", step)
                    ins = s_.activation(kT1[:, 4 * half:4 * half + 4, t * P:(t + 1) * P],
                                        psM[m][:].rearrange("p (a b) -> p a b", b=P), ACT.Copy)
                    read("M", m, ins)
                elif kind == "qT1":
                    p = step[2]
                    m = full("M", step)
                    sc.wait_ge(sem("qT1_clear"), 2)
                    read("M", m, s_.activation(qT1[0:64, 2 * p, :], psM[m][0:64, :], ACT.Copy))
                elif kind == "score1":
                    _, c, g, sbk, i = step
                    n = nth[step]
                    t = full("T", step)
                    if n >= 3:
                        sc.wait_ge(sem("pv1_done"), n - 2)
                    off = max(0, sbk - TC * c) * P
                    read("T", t, s_.activation(probs[:, n % 2, :, off:CH], psT[t][:, :, off:CH], ACT.Exp))
                elif kind == "out1":
                    _, c, g = step
                    o = tab["O"][("o1", c, g)][0][0]
                    sc.wait_ge(sem("pv1_done"), nth[("pv1", c, g, TC * c + TC - 1, 1)])
                    if nth[step] > 1:
                        wait_full(sc, "M", ("out1", c, g - 1) if g else ("out1", c - 1, 3))
                    s_.activation(o1_T, psO[:, o], ACT.Copy).then_inc(sem("o1_out"), 1)
                elif kind == "aT1":
                    _, c, k = step
                    m = full("M", step)
                    s_.activation(xTh[:, k, c * CH:(c + 1) * CH], psM[m][:], ACT.Copy).then_inc(sem("aT1_hi"), 1)
                elif kind == "qkv2":
                    _, c, g, tp = step
                    t = full("T", step)
                    if g == 1:
                        read("T", t, s_.activation(v_tok[:, TC * c + 2 * tp:TC * c + 2 * tp + 2], psT[t][:], ACT.Copy))
                    else:
                        if squares:
                            sc.wait_ge(sem("ssq_ready"), squares)
                        squares += 1
                        s_.activation(psO[:, 0], psT[t][:, 0], ACT.Square, accum_out=ssq[:, 2 * tp, g:g + 1])
                        s_.activation(psO[:, 1], psT[t][:, 1], ACT.Square, accum_out=ssq[:, 2 * tp + 1, g:g + 1])\
                            .then_inc(sem("ssq_ready"), 1)
                elif kind == "rms2":
                    sc.wait_ge(sem("ms_ready"), nth[step])
                    s_.activation(ms[:, 1, :], ms[:, 0, :], ACT.Sqrt).then_inc(sem("ms_root"), 1)
                elif kind == "rope":
                    _, c, t, which = step
                    sc.wait_ge(sem("r_ready"), nth[("rms2", c, "k" if which == "k" else "q")])
                    tok, r_ = rope_part(which, t)
                    s_.activation(tok[:, :, RD:DH2], tok[:, :, RD:DH2], ACT.Copy, scale=r_).then_inc(sem("pass_scaled"), 1)
                elif kind == "kT2":
                    _, c, j = step
                    m = full("M", step)
                    s_.activation(kTh[:, j, c * CH:(c + 1) * CH], psM[m][:], ACT.Copy).then_inc(sem("kT2_hi"), 1)
                elif kind == "qT2":
                    u, i = step[1], step[2]
                    m = full("M", step)
                    n = nth[("mT2", u)]
                    s_.activation(qTh[:, n % 2, i], psM[m][:], ACT.Copy).then_inc(sem("qT2_hi"), 1)
                elif kind == "mT2":
                    m = full("M", step)
                    read("M", m, s_.activation(negmT[:, nth[step] % 2], psM[m][:], ACT.Copy))
                elif kind == "score2":
                    _, u, sbk = step
                    n = nth[step]
                    t = full("T", step)
                    if n >= 3:
                        sc.wait_ge(sem("pv2_done"), n - 2)
                        sc.wait_ge(sem("p_sum"), n - 2)
                    off = max(0, sbk - TC * u[0]) * P
                    read("T", t, s_.activation(probs[:, n % 2, :, off:CH], psT[t][:, :, off:CH], ACT.Exp))
                elif kind == "out2":
                    u = step[1]
                    n = nth[step]
                    c = u[0]
                    sc.wait_ge(sem("pv2_done"), nth[("pv2", u, TC * c + TC - 1)])
                    if n > 1:
                        wait_full(sc, "M", ("wo2", outs[n - 2][1], 1, 1))
                    s_.activation(oTh, psO[:], ACT.Copy).then_inc(sem("oTh_ready"), 1)
                elif kind == "router":
                    _, st, c = step
                    m = full("M", step)
                    e_n = (E1, E2)[st]
                    if st == 0 and c:
                        wait_full(sc, "M", ("logits", 0, c - 1))
                    read("M", m, s_.activation(routed[st][c][0:e_n], psM[m][0:e_n, :], ACT.Copy))
                elif kind == "logits":
                    st = step[1]
                    if st == 0:
                        m = full("M", step)
                        read("M", m, s_.activation(logits[:, 0:TC, 0:E1], psM[m][:, 0:TC * E1].rearrange("p (t e) -> p t e", e=E1),
                                                   ACT.Sigmoid))
                    else:
                        wait_read(sc, "M", step)
                        s_.activation(rt[:], logits[:], ACT.Exp).then_inc(sem("logits_out"), 1)
                elif kind == "combT":
                    st, c = step[1:]
                    m = full("M", step)
                    e_n = (E1, E2)[st]
                    if nth[step] > 1:
                        sc.wait_ge(sem("combT_stored"), 16 * (nth[step] - 1))
                    read("M", m, s_.activation(combT[0:e_n], psM[m][0:e_n, :], ACT.Copy))
                elif kind == "gateup":
                    _, st, b, c = step
                    n = nth[step]
                    t = full("T", step)
                    if n >= 3:
                        wait_read(sc, "T", gus[n - 3])
                    s_.activation(gate[:, n % 2], psT[t][:, 0], ACT.Silu).then_inc(sem("silu"), 1)
                elif kind == "weigh":
                    n = nth[step]
                    s, at = n % PART_SLOTS, n % ACT_SLOTS
                    sc.wait_ge(sem("weighed"), n)
                    if n > PART_SLOTS:
                        sc.wait_ge(sem("down_done"), n - PART_SLOTS)
                    s_.activation(aTh[:, s], act[:, at], ACT.Copy).then_inc(sem("act_hi"), 1)
                elif kind == "add":
                    _, st, c = step
                    sc.wait_ge(sem("down_done"), last_down(st, c))
                    if nth[step] > 1:
                        wait_full(sc, "T", sums[nth[step] - 2])
                    ring = ("O", "M")[c]
                    m = tab[ring][("acc", st, c)][0][0]
                    read(ring, m, s_.activation(accT[:, 0], acc_bank(c, m), ACT.Copy))
                elif kind == "rates":
                    link(s_.activation(sp_s[:, 0], mats[:, 0], ACT.Abs))
                    s_.activation(sp_s[:, 1], sp_s[:, 0], ACT.Exp, scale=-1.0).then_inc(sem("rate_exp"), 1)
                    sc.wait_ge(sem("rate_one"), 1)
                    s_.activation(sp_s[:, 0], sp_s[:, 2], ACT.Ln).then_inc(sem("rate_log"), 1)
                elif kind == "soft":
                    c = step[1]
                    if c:
                        sc.wait_ge(sem("dt_ready"), c)
                    for ob in range(KD):
                        wait_read(sc, "T", ("proj", c, 0, ob))
                    link(s_.activation(sp_a, dtT[:, :, c * CH:(c + 1) * CH], ACT.Abs))
                    s_.activation(sp_b, sp_a, ACT.Exp, scale=-1.0).then_inc(sem("sp_exp"), 1)
                    sc.wait_ge(sem("sp_one"), c + 1)
                    s_.activation(sp_a, sp_c, ACT.Ln).then_inc(sem("sp_log"), 1)
                elif kind == "scan":
                    _, ob, k = step
                    n = nth[step]
                    if n == 1:
                        sc.wait_ge(sem("dt_ready"), NC)
                    if n >= 3:
                        sc.wait_ge(sem("scanned"), n - 2)
                    s_.activation(decay[:, n % 2], dtT[:, ob], ACT.Exp,
                                  scale=neg_a[:, ob * NST + k:ob * NST + k + 1]).then_inc(sem("decay_ready"), 1)

        @block.vector
        def _(ve):
            v = nc.vector
            chained = [0]

            def link(ins):
                chained[0] += 1
                ins.then_inc(sem("dve_chain"), 1)
                ve.wait_ge(sem("dve_chain"), chained[0])

            def full(ring, use, i=0):
                return wait_full(ve, ring, use, i)

            def read(ring, slot, ins):
                ins.then_inc(sem(f"{ring}_read{slot}"), 1)

            def stats(src, c):
                for i in range(TC):
                    v_ins = v.bn_stats(bn6[:, i], src(i))
                link(v_ins)
                for i in range(TC):
                    v_ins = v.bn_aggr(mv[:, i], bn6[:, i])
                link(v_ins)

            roots = 0

            def root():
                nonlocal roots
                roots += 1
                ve.wait_ge(sem("root_ready"), roots)
                link(v.reciprocal(rs[:, 2, :], rs[:, 1, :]))

            def layernorm(c, dst):
                stats(lambda i: x[:, TC * c + i], c)
                v.tensor_scalar(rs[:, 0, :], mv[:, :, 1], 1e-5, None, ALU.add).then_inc(sem("var_ready"), 1)
                root()
                for i in range(TC):
                    ins = v.tensor_scalar(dst(i), x[:, TC * c + i], mv[:, i, 0:1], rs[:, 2, i:i + 1],
                                          ALU.subtract, ALU.mult)
                return ins

            def rmsnorm(c):
                stats(lambda i: xn[:, TC * c + i], c)
                link(v.tensor_tensor(rs[:, 1, :], mv[:, :, 0], mv[:, :, 0], ALU.mult))
                v.scalar_tensor_tensor(rs[:, 0, :], rs[:, 1, :], 1e-6, mv[:, :, 1], ALU.add, ALU.add)\
                    .then_inc(sem("var_ready"), 1)
                root()
                for i in range(TC):
                    ins = v.tensor_scalar(normed[:, i], xn[:, TC * c + i], rs[:, 2, i:i + 1], None, ALU.mult)
                return ins

            v.memset(psO[:], 0.0).then_inc(sem("psO_clear"), 1)
            early = 6
            v.memset(qT1[:, 0:early].bitcast(F32), 0.0).then_inc(sem("qT1_clear"), 1)
            ve.wait_ge(sem("x_loaded0"), 16)
            for step in STEPS:
                kind = step[0]
                if kind == "norm":
                    _, st, c = step
                    if (st, c) == (0, 1):
                        ve.wait_ge(sem("x_loaded1"), 16)
                    if st == 1:
                        wait_read(ve, "M", ("wo1", c, TC // 2 - 1))
                    elif st == 2:
                        for i in (0, 1):
                            wait_read(ve, "M", ("wo2", (c, KV2 - 1, 1), i, TC // 2 - 1))
                    elif st == 3:
                        wait_read(ve, "T", ("sumT", 0, c))
                    elif st == 4:
                        wait_read(ve, "M", ("yT", NT // 2 - 1))
                    if st in (0, 3, 4):
                        layernorm(c, lambda i: normed[:, i]).then_inc(sem("normed_ready"), 1)
                    elif st == 1:
                        link(layernorm(c, lambda i: xn[:, TC * c + i]))
                        rmsnorm(c).then_inc(sem("normed_ready"), 1)
                    else:
                        rmsnorm(c).then_inc(sem("normed_ready"), 1)
                        for i in range(TC):
                            t = TC * c + i
                            ins = v.tensor_tensor(x[:, t], x[:, t], xn[:, t], ALU.add)
                        link(ins)
                elif kind == "normT":
                    _, st, c, k = step
                    m = full(norm_ring(st), step)
                    src = psT[m][:, 0] if st == 3 else psM[m][:]
                    if step == ("normT", 0, 0, 0):
                        ve.wait_ge(sem("consts_loaded"), 16 * 7)
                    ve.wait_ge(sem("xTh_ready"), nth[step])
                    cols = slice(c * CH, (c + 1) * CH)
                    if st == 3:
                        link(v.tensor_copy(uT[:, k, cols], src))
                    read(norm_ring(st), m, v.scalar_tensor_tensor(xTl[:, k, cols], src, lnw[:, st, k:k + 1],
                                                        xTh[:, k, cols].bitcast(F32), ALU.mult, ALU.subtract))
                    if step == ("normT", 0, 0, KD - 1):
                        v.memset(qT1[:, early:].bitcast(F32), 0.0).then_inc(sem("qT1_clear"), 1)
                elif kind == "qkv1":
                    t = step[1]
                    i = t % TC
                    s = full("T", step)
                    if t >= 1:
                        ve.wait_ge(sem("stack_hi"), t)
                        ve.wait_ge(sem("stack_lo"), t)
                    read("T", s, v.tensor_tensor(qkv_tok, psT[s][:].rearrange("p a b -> p (a b)")[:, 0:3 * D], bqkv_b, ALU.add))
                    ve.wait_ge(sem("stack_hi"), nth[step])
                    q3 = qkv_tok[:, 0:D].rearrange("p (h d) -> p h d", d=HD1)
                    k3 = qkv_tok[:, D:2 * D].rearrange("p (h d) -> p h d", d=HD1)
                    if t >= TC:
                        v.memset(q_stack[:, i, :, 48:49], 0.0)
                    v.scalar_tensor_tensor(q_stack[:, i, :, 16:32].bitcast(F32R), q3, HD1 ** -0.5,
                                           q_stack[:, i, :, 0:16], ALU.mult, ALU.subtract)
                    v.tensor_tensor(k_stack[:, :, 32:48].bitcast(F32R), k3, k_stack[:, :, 0:16], ALU.subtract)\
                        .then_inc(sem("stack_lo"), 1)
                elif kind == "qT1":
                    p = step[2]
                    m = full("M", step)
                    ve.wait_ge(sem("qT1_clear"), 2)
                    read("M", m, v.tensor_copy(qT1[64:P, 2 * p + 1, :], psM[m][64:P, :]))
                elif kind == "max1":
                    _, c, t, p, i, half = step
                    m = full("M", step)
                    n = nth[("join1", c, p)]
                    if (t % TC, i, half) == (0, 0, 0) and n > 2:
                        ve.wait_ge(sem("joined"), n - 2)
                    w = min((t + 1) * P - half * CH, CH)
                    read("M", m, v.tensor_reduce(max_parts[:, n % 2, half, t % TC, i:i + 1], psM[m][:, 0:w], X_AXIS, ALU.max, negate=True))
                elif kind == "join1":
                    _, c, p = step
                    n = nth[step]
                    wait_read_all(ve, "M", [k for k in tab["M"] if k[0] == "max1" and (k[1], k[3]) == (c, p)])
                    parts = max_parts[:, n % 2]
                    v.tensor_tensor(q_stack[:, :, 2 * p:2 * p + 2, 48], parts[:, 0], parts[:, c], ALU.min).then_inc(sem("joined"), 1)
                elif kind == "out1":
                    _, c, g = step
                    m = full("M", step)
                    o4 = psM[m][:].rearrange("p (t h e) -> p t h e", t=TC, h=4)
                    if nth[step] > 1:
                        wait_read(ve, "M", ("out1", c, g - 1) if g else ("out1", c - 1, 3))
                    link(v.reciprocal(den1, o4[:, :, :, HD1]))
                    read("M", m, v.tensor_tensor(a_tok.rearrange("p t (h d) -> p t h d", d=HD1)[:, :, 4 * g:4 * g + 4],
                                         o4[:, :, :, 0:HD1],
                                         den1.unsqueeze(3).to_broadcast([P, TC, 4, HD1]), ALU.mult))
                elif kind == "aT1":
                    _, c, k = step
                    m = full("M", step)
                    ve.wait_ge(sem("aT1_hi"), nth[step])
                    read("M", m, v.tensor_tensor(xTl[:, k, c * CH:(c + 1) * CH], psM[m][:],
                                         xTh[:, k, c * CH:(c + 1) * CH].bitcast(F32), ALU.subtract))
                elif kind == "wo1":
                    _, c, tp = step
                    m = full("M", step)
                    for i in (0, 1):
                        t = TC * c + 2 * tp + i
                        ins = v.tensor_tensor(x[:, t], x[:, t], bo_b, ALU.add)
                    link(ins)
                    t = TC * c + 2 * tp
                    read("M", m, v.tensor_tensor(x[:, t:t + 2], x[:, t:t + 2], psM[m][:].rearrange("p (a b) -> p a b", b=D), ALU.add))
                elif kind == "qkv2":
                    _, c, g, tp = step
                    if g == 1:
                        continue
                    s = full("T", step)
                    rows = 5 * c + (0 if g == 0 else g - 1)
                    ve.wait_ge(sem(f"row_loaded{rows % 2}"), 16 * (rows // 2 + 1))
                    ve.wait_ge(sem("ssq_ready"), 2 * rows + tp + 1)
                    if c == 1 and g == 0 and tp == 0:
                        ve.wait_ge(sem("oT_ready"), 2 * KV2)
                    if g == 0:
                        dst = k_tok[:, 2 * tp:2 * tp + 2].rearrange("p a b c -> p a (b c)")
                    else:
                        dst = q_tok[:, 2 * tp:2 * tp + 2, 4 * (g - 2):4 * (g - 2) + 4].rearrange("p a b c -> p a (b c)")
                    read("T", s, v.tensor_tensor(dst, psT[s][:], qkw[:, rows % 2].unsqueeze(1).to_broadcast([P, 2, CH]), ALU.mult))
                elif kind == "rms2":
                    _, c, which = step
                    if which == "k":
                        v.tensor_scalar(ms[:, 0, :], ssq[:, :, 0], 1.0 / (KV2 * DH2), 1e-6, ALU.mult, ALU.add)\
                            .then_inc(sem("ms_ready"), 1)
                    else:
                        link(v.tensor_reduce(ms[:, 0, :], ssq[:, :, 2:6], X_AXIS, ALU.add))
                        v.tensor_scalar(ms[:, 0, :], ms[:, 0, :], 1.0 / (H2 * DH2), 1e-6, ALU.mult, ALU.add)\
                            .then_inc(sem("ms_ready"), 1)
                    ve.wait_ge(sem("ms_root"), nth[step])
                    if which == "k":
                        v.reciprocal(r_k[:], ms[:, 1, :]).then_inc(sem("r_ready"), 1)
                    else:
                        link(v.reciprocal(r_q[:], ms[:, 1, :]))
                        v.tensor_scalar(r_q[:], r_q[:], DH2 ** -0.5, None, ALU.mult).then_inc(sem("r_ready"), 1)
                    ve.wait_ge(sem("r_ready"), nth[step])
                elif kind == "rope":
                    _, c, t, which = step
                    if nth[step] == 1:
                        ve.wait_ge(sem("tables_loaded"), 32)
                    nh = 4
                    tok, r_ = rope_part(which, t)
                    HR = RD // 2
                    t1, t2 = rope_tmp[:, 0], rope_tmp[:, 1]
                    ct = cos_t[:, TC * c + t].unsqueeze(1).to_broadcast([P, nh, RD])
                    sn = sin_t[:, TC * c + t].unsqueeze(1)
                    if nth[step] > 1:
                        ve.wait_ge(sem("roped"), nth[step] - 1)
                    v.scalar_tensor_tensor(t1, tok[:, :, 0:RD], r_, ct, ALU.mult, ALU.mult)
                    v.scalar_tensor_tensor(t2[:, :, 0:HR], tok[:, :, HR:RD], r_,
                                           sn[:, :, 0:HR].to_broadcast([P, nh, HR]), ALU.mult, ALU.mult)
                    link(v.scalar_tensor_tensor(t2[:, :, HR:RD], tok[:, :, 0:HR], r_,
                                                sn[:, :, HR:RD].to_broadcast([P, nh, HR]), ALU.mult, ALU.mult))
                    v.tensor_tensor(tok[:, :, 0:RD], t1, t2, ALU.add).then_inc(sem("roped"), 1)
                elif kind == "kT2":
                    _, c, j = step
                    m = full("M", step)
                    ve.wait_ge(sem("kT2_hi"), nth[step])
                    cols = slice(c * CH, (c + 1) * CH)
                    read("M", m, v.tensor_tensor(kTl[:, j, cols], psM[m][:], kTh[:, j, cols].bitcast(F32), ALU.subtract))
                elif kind == "qT2":
                    u, i = step[1], step[2]
                    m = full("M", step)
                    n = nth[("mT2", u)]
                    ve.wait_ge(sem("qT2_hi"), nth[step])
                    read("M", m, v.tensor_tensor(qTl[:, n % 2, i], psM[m][:], qTh[:, n % 2, i].bitcast(F32), ALU.subtract))
                elif kind == "max2":
                    _, u, t, i = step
                    s = full("T", step)
                    if t == TC * u[0] and i in (None, 0):
                        if nth[("mT2", u)] == 1:
                            ve.wait_ge(sem("pick_ready"), 1)
                        else:
                            wait_full(ve, "M", mts[nth[("mT2", u)] - 2])
                    w = (t + 1) * P
                    if i is None:
                        dst, src = neg_max[:, t % TC, 0:2], psT[s][:, :, 0:w]
                    else:
                        dst, src = neg_max[:, t % TC, i:i + 1], psT[s][:].rearrange("p a b -> p (a b)")[:, 0:w]
                    read("T", s, v.tensor_reduce(dst, src, X_AXIS, ALU.max, negate=True))
                elif kind == "out2":
                    u = step[1]
                    n = nth[step]
                    ve.wait_ge(sem("oTh_ready"), n)
                    v.tensor_tensor(oTl, psO[:], oTh.bitcast(F32), ALU.subtract).then_inc(sem("oT_ready"), 1)
                    m = full("M", step)
                    if n > 1:
                        for tp in range(TC // 2):
                            wait_read(ve, "M", ("wo2", outs[n - 2][1], 1, tp))
                    read("M", m, v.reciprocal(rden[:], psM[m][:, 0:2 * TC].rearrange("p (a b) -> p a b", b=TC)))
                elif kind == "wo2":
                    _, u, i, tp = step
                    m = full("M", step)
                    wait_read(ve, "M", ("out2", u))
                    if i or u[1] or u[2]:
                        wait_read(ve, "M", ("wo2", u, 0, tp) if i else ("wo2", outs[nth[("out2", u)] - 2][1], 1, tp))
                    for b in (0, 1):
                        t = 2 * tp + b
                        ins = v.scalar_tensor_tensor(xn[:, TC * u[0] + t], psM[m][:, b * D:(b + 1) * D], rden[:, i, t:t + 1],
                                                     xn[:, TC * u[0] + t], ALU.mult, ALU.add)
                    read("M", m, ins)
                elif kind == "logits":
                    _, st, c = step
                    if st == 0:
                        wait_read(ve, "M", step)
                        link(v.tensor_tensor(rt[:, 0:TC, 0:E1], logits[:, 0:TC, 0:E1],
                                             rbias[:].unsqueeze(1).to_broadcast([P, TC, E1]), ALU.add))
                    else:
                        m = full("M", step)
                        lg = psM[m][:, 0:NT * E2].rearrange("p (t e) -> p t e", e=E2)
                        link(v.tensor_reduce(tok1[:], lg, X_AXIS, ALU.max))
                        read("M", m, v.tensor_tensor(logits[:], lg, tok1[:].unsqueeze(2).to_broadcast([P, NT, E2]), ALU.subtract))
                elif kind == "pick":
                    _, st, c = step
                    t0, t1 = tile_range(c)
                    n = t1 - t0
                    if st == 1:
                        ve.wait_ge(sem("logits_out"), 1)
                        link(v.tensor_reduce(tok1[:], rt[:], X_AXIS, ALU.add))
                        link(v.reciprocal(tok1[:], tok1[:]))
                        link(v.tensor_tensor(rt[:], rt[:], tok1[:].unsqueeze(2).to_broadcast([P, NT, E2]), ALU.mult))
                    e_n = (E1, E2)[st]
                    for t in range(n):
                        ins = v.max(top8[:, t], rt[:, t, 0:e_n])
                    link(ins)
                    for t in range(n):
                        ins = v.max_index(idx_u[:, t], top8[:, t], rt[:, t, 0:e_n])
                    link(ins)
                    link(v.tensor_copy(idx_f[:, 0:n], idx_u[:, 0:n]))
                elif kind == "combine":
                    _, st, c = step
                    t0, t1 = tile_range(c)
                    n = t1 - t0
                    e_n, top = ((E1, TOP1), (E2, TOP2))[st]
                    onehot = onehots[st]
                    for j in range(top):
                        ins = v.tensor_tensor(onehot[:, :, j, 0:e_n], iota[:, 0:e_n].unsqueeze(1).to_broadcast([P, n, e_n]),
                                              idx_f[:, 0:n, j:j + 1].to_broadcast([P, n, e_n]), ALU.is_equal)
                    link(ins)
                    if st == 0:
                        w = comb[:, t0:t1, 0:E1]
                        link(v.tensor_tensor(w, onehot[:, :, 0, 0:E1], onehot[:, :, 1, 0:E1], ALU.add))
                        link(v.tensor_tensor(w, w, logits[:, 0:n, 0:E1], ALU.mult))
                        link(v.tensor_reduce(tok1[:, 0:n], w, X_AXIS, ALU.add))
                        link(v.reciprocal(tok1[:, 0:n], tok1[:, 0:n]))
                        v.tensor_tensor(w, w, tok1[:, 0:n].unsqueeze(2).to_broadcast([P, n, E1]), ALU.mult)\
                            .then_inc(sem("comb_ready"), 1)
                    else:
                        link(v.tensor_reduce(tok1[:], top8[:], X_AXIS, ALU.add))
                        link(v.tensor_scalar(tok1[:], tok1[:], 1e-12, None, ALU.max))
                        link(v.reciprocal(tok1[:], tok1[:]))
                        link(v.tensor_tensor(cum[:], top8[:], tok1[:].unsqueeze(2).to_broadcast([P, NT, 8]), ALU.mult))
                        for j in range(1, TOP2):
                            link(v.tensor_tensor(cum[:, :, j], cum[:, :, j], cum[:, :, j - 1], ALU.add))
                elif kind == "share":
                    onehot = onehots[1]
                    link(v.tensor_scalar(cum[:], cum[:], THRESHOLD, None, ALU.is_lt))
                    link(v.tensor_tensor(top8[:, :, 1:8], top8[:, :, 1:8], cum[:, :, 0:7], ALU.mult))
                    link(v.tensor_reduce(tok1[:], top8[:], X_AXIS, ALU.add))
                    link(v.tensor_scalar(tok1[:], tok1[:], 1e-12, None, ALU.max))
                    link(v.reciprocal(tok1[:], tok1[:]))
                    link(v.tensor_tensor(top8[:], top8[:], tok1[:].unsqueeze(2).to_broadcast([P, NT, 8]), ALU.mult))
                    for j in range(TOP2):
                        ins = v.tensor_tensor(onehot[:, :, j], onehot[:, :, j],
                                              top8[:, :, j:j + 1].to_broadcast([P, NT, E2]), ALU.mult)
                    link(ins)
                    link(v.tensor_tensor(onehot[:, :, 0:4], onehot[:, :, 0:4], onehot[:, :, 4:8], ALU.add))
                    link(v.tensor_tensor(onehot[:, :, 0:2], onehot[:, :, 0:2], onehot[:, :, 2:4], ALU.add))
                    v.tensor_tensor(comb[:], onehot[:, :, 0], onehot[:, :, 1], ALU.add).then_inc(sem("comb_ready"), 1)
                elif kind == "gateup":
                    n = nth[step]
                    at = n % ACT_SLOTS
                    t = full("T", step)
                    ve.wait_ge(sem("silu"), n)
                    if n > ACT_SLOTS:
                        ve.wait_ge(sem("act_lo"), n - ACT_SLOTS)
                    read("T", t, v.tensor_tensor(act[:, at], gate[:, n % 2], psT[t][:, 1], ALU.mult))
                elif kind == "weigh":
                    n = nth[step]
                    at = n % ACT_SLOTS
                    job, _, loaded_by = share_dmas[step[1:]]
                    ve.wait_ge(sem(f"share_loaded{job % SHARE_SLOTS}"), loaded_by)
                    wait_read(ve, "T", ("gateup",) + step[1:])
                    v.tensor_tensor(act[:, at], act[:, at], share[:, job % SHARE_SLOTS], ALU.mult).then_inc(sem("weighed"), 1)
                elif kind == "add":
                    _, st, c = step
                    ve.wait_ge(sem("down_done"), last_down(st, c))
                    if nth[step] > 1:
                        wait_full(ve, "T", sums[nth[step] - 2])
                    ring = ("O", "M")[c]
                    m = tab[ring][("acc", st, c)][1][0]
                    read(ring, m, v.tensor_copy(accT[:, 1], acc_bank(c, m)))
                elif kind == "sumT":
                    _, st, c = step
                    m = full("T", step)
                    ts = slice(TC * c, TC * c + TC)
                    read("T", m, v.tensor_tensor(x[:, ts], x[:, ts], psT[m][:].rearrange("p a (b d) -> p (a b) d", d=D), ALU.add))
                elif kind == "rates":
                    ve.wait_ge(sem("rate_exp"), 1)
                    v.tensor_tensor(bc_s[:], mats[:, 1], mats[:, 2], ALU.mult).then_inc(sem("bc_ready"), 1)
                    v.tensor_scalar(sp_s[:, 2], sp_s[:, 1], 1.0, None, ALU.add).then_inc(sem("rate_one"), 1)
                    ve.wait_ge(sem("rate_one"), 1)
                    link(v.scalar_tensor_tensor(sp_s[:, 1], sp_s[:, 2], -1.0, sp_s[:, 1], ALU.add, ALU.subtract))
                    ve.wait_ge(sem("rate_log"), 1)
                    link(v.tensor_tensor(sp_s[:, 0], sp_s[:, 0], sp_s[:, 1], ALU.subtract))
                    link(v.scalar_tensor_tensor(sp_s[:, 0], mats[:, 0], 0.0, sp_s[:, 0], ALU.max, ALU.add))
                    link(v.tensor_scalar(neg_a[:], sp_s[:, 0], -1.0, None, ALU.mult))
                elif kind == "proj":
                    _, c, w, ob = step
                    cols = slice(c * CH, (c + 1) * CH)
                    t = full("T", step)
                    src = psT[t][:, 0]
                    if w == 0:
                        read("T", t, v.tensor_scalar(dtT[:, ob, cols], src, vecs[:, 0, ob:ob + 1], None, ALU.add))
                    elif w == 1:
                        if ob == 0:
                            ve.wait_ge(sem("dt_ready"), c + 1)
                        read("T", t, v.scalar_tensor_tensor(bT[:, ob, cols], src, vecs[:, 1, ob:ob + 1], dtT[:, ob, cols], ALU.add, ALU.mult))
                        wait_read(ve, "T", step)
                        link(v.tensor_tensor(bT[:, ob, cols], bT[:, ob, cols], uT[:, ob, cols], ALU.mult))
                    else:
                        read("T", t, v.tensor_scalar(cT[:, ob, cols], src, vecs[:, 2, ob:ob + 1], None, ALU.add))
                elif kind == "soft":
                    c = step[1]
                    cols = slice(c * CH, (c + 1) * CH)
                    ve.wait_ge(sem("sp_exp"), c + 1)
                    v.tensor_scalar(sp_c, sp_b, 1.0, None, ALU.add).then_inc(sem("sp_one"), 1)
                    ve.wait_ge(sem("sp_one"), c + 1)
                    link(v.scalar_tensor_tensor(sp_b, sp_c, -1.0, sp_b, ALU.add, ALU.subtract))
                    for ob in range(KD):
                        wait_read(ve, "T", ("proj", c, 0, ob))
                    link(v.tensor_scalar(dtT[:, :, cols], dtT[:, :, cols], 0.0, DT_MIN, ALU.max, ALU.add))
                    link(v.tensor_tensor(dtT[:, :, cols], dtT[:, :, cols], sp_b, ALU.subtract))
                    ve.wait_ge(sem("sp_log"), c + 1)
                    v.tensor_tensor(dtT[:, :, cols], dtT[:, :, cols], sp_a, ALU.add).then_inc(sem("dt_ready"), 1)
                elif kind == "scan":
                    _, ob, k = step
                    n = nth[step]
                    ve.wait_ge(sem("decay_ready"), n)
                    if n >= 3:
                        ve.wait_ge(sem("scan_summed"), n - 2)
                    v.tensor_tensor_scan(state[:, n % 2], decay[:, n % 2], bT[:, ob], 0.0, ALU.mult, ALU.add)\
                        .then_inc(sem("scanned"), 1)
                elif kind == "y":
                    ob = step[1]
                    ve.wait_ge(sem("scan_summed"), nth[("scan", ob, NST - 1)])
                    link(v.tensor_tensor(cT[:, ob], psO[:].rearrange("p a b -> p (a b)"), cT[:, ob], ALU.mult))
                    v.scalar_tensor_tensor(yT[:, ob], uT[:, ob], vecs[:, 3, ob:ob + 1], cT[:, ob], ALU.mult, ALU.add)\
                        .then_inc(sem("y_ready"), 1)
                elif kind == "yT":
                    tp = step[1]
                    m = full("M", step)
                    read("M", m, v.tensor_tensor(x[:, 2 * tp:2 * tp + 2], x[:, 2 * tp:2 * tp + 2],
                                         psM[m][:].rearrange("p (a b) -> p a b", b=D), ALU.add))

        @block.tensor
        def _(pe):
            mm = nc.tensor.matmul
            tr = nc.tensor.transpose

            def take(ring, key, i=0):
                slot, releases, _, _ = tab[ring][key][i]
                if releases:
                    pe.wait_ge(sem(f"{ring}_read{slot}"), releases)
                return slot

            def filled(ring, slot, ins):
                ins.then_inc(sem(f"{ring}_full{slot}"), 1)

            def weights(name):
                n = order[name]
                pe.wait_ge(sem("w_split"), n + 1)
                return split_views(n)

            def three(out, hi, lo, rhi, rlo, start=True, stop=True):
                mm(out, hi, rlo, start=start, stop=False)
                mm(out, lo, rhi, start=False, stop=False)
                return mm(out, hi, rhi, start=False, stop=stop)

            pe.wait_ge(sem("ident_ready"), 1)
            pe.wait_ge(sem("psO_clear"), 1)
            for step in STEPS:
                kind = step[0]
                if kind == "normT":
                    _, st, c, k = step
                    pe.wait_ge(sem("normed_ready"), nth[("norm", st, c)])
                    ring = norm_ring(st)
                    m = take(ring, step)
                    dst = psT[m][:, 0] if st == 3 else psM[m][:]
                    for i in range(TC):
                        ins = tr(dst[:, i * P:(i + 1) * P], normed[:, i, k * P:(k + 1) * P], ident[:])
                    filled(ring, m, ins)
                elif kind == "qkv1":
                    t = step[1]
                    c = t // TC
                    wait_read(pe, "M", ("normT", 0, c, KD - 1))
                    s = take("T", step)
                    tc = slice(t * P, (t + 1) * P)
                    wk = [weights(("wqkv", c, k)) for k in range(KD)]
                    for k in range(KD):
                        hi, lo = wk[k]
                        for b, (a0, a1) in enumerate(((0, CH), (CH, 3 * D))):
                            ins = three(psT[s][:, b, 0:a1 - a0], xTh[:, k, tc], xTl[:, k, tc], hi[:, a0:a1], lo[:, a0:a1],
                                        start=k == 0, stop=k == KD - 1)
                        if k == KD - 1:
                            filled("T", s, ins)
                elif kind == "kT1":
                    t, half = step[1], step[2]
                    pe.wait_ge(sem("stack_lo"), t + 1)
                    m = take("M", step)
                    ks = k_stack.rearrange("p h e -> p (h e)")
                    for j in range(4):
                        a0 = (4 * half + j) * P
                        ins = tr(psM[m][:, j * P:(j + 1) * P], ks[:, a0:a0 + P], ident[:])
                    filled("M", m, ins)
                elif kind == "qT1":
                    _, c, p, again = step
                    pe.wait_ge(sem("stack_lo"), TC * (c + 1))
                    if again:
                        pe.wait_ge(sem("joined"), nth[("join1", c, p)])
                    m = take("M", step)
                    qs = q_stack.rearrange("p t h e -> p t (h e)")
                    for i in range(TC):
                        ins = tr(psM[m][:, i * P:(i + 1) * P], qs[:, i, p * P:(p + 1) * P], ident[:])
                    filled("M", m, ins)
                elif kind == "max1":
                    _, c, t, p, i, half = step
                    for part in (0, 1):
                        wait_read(pe, "M", ("kT1", TC * c + TC - 1, part))
                    wait_read(pe, "M", ("qT1", c, p, 0))
                    if nth[step] == 1:
                        pe.wait_ge(sem("consts_ready"), 1)
                    m = take("M", step)
                    tc = slice((t % TC) * P, (t % TC + 1) * P)
                    a0, a1 = half * CH, min((t + 1) * P, half * CH + CH)
                    last = a1 == (t + 1) * P
                    ins = mm(psM[m][:, 0:a1 - a0], qT1[:, 2 * p + i, tc], kT1[:, p, a0:a1], start=True, stop=not last)
                    if last:
                        ins = mm(psM[m][:, a1 - a0 - P:a1 - a0], ident_b[:], mask_q[:], start=False, stop=True)
                    filled("M", m, ins)
                elif kind == "score1":
                    _, c, g, sbk, i = step
                    p = 2 * g + i
                    wait_read(pe, "M", ("qT1", c, p, 1))
                    s = take("T", step)
                    diag_block = sbk >= TC * c
                    off = max(0, sbk - TC * c) * P
                    for b in (0, 1):
                        ins = mm(psT[s][:, b, off:CH], kT1[:, p, sbk * P:(sbk + 1) * P], qT1[:, 2 * p + b, off:CH],
                                 start=True, stop=not diag_block)
                        if diag_block:
                            ins = mm(psT[s][:, b, off:off + P], ident_b[:], mask_k[:], start=False, stop=True)
                    filled("T", s, ins)
                elif kind == "pv1":
                    _, c, g, sbk, i = step
                    n = nth[step]
                    wait_read(pe, "T", ("score1",) + step[1:])
                    o = tab["O"][("o1", c, g)][0][0]
                    if sbk == 0 and i == 0 and nth[("out1", c, g)] > 2:
                        pe.wait_ge(sem("o1_out"), nth[("out1", c, g)] - 2)
                    off = max(0, sbk - TC * c) * P
                    for b in (0, 1):
                        h = 4 * g + 2 * i + b
                        q0 = 32 * (2 * i + b)
                        ins = mm(psO[q0:q0 + HD1 + 1, o, off:CH], v_aug[:, sbk, h], probs[:, n % 2, b, off:CH],
                                 start=sbk == 0, stop=sbk == TC * c + TC - 1)
                    ins.then_inc(sem("pv1_done"), 1)
                elif kind == "out1":
                    _, c, g = step
                    pe.wait_ge(sem("o1_out"), nth[step])
                    m = take("M", step)
                    for i in range(TC):
                        ins = tr(psM[m][:, i * P:(i + 1) * P], o1_T[:, i * P:(i + 1) * P], ident[:])
                    filled("M", m, ins)
                elif kind == "aT1":
                    _, c, k = step
                    for g in range(4):
                        wait_read(pe, "M", ("out1", c, g))
                    m = take("M", step)
                    for i in range(TC):
                        ins = tr(psM[m][:, i * P:(i + 1) * P], a_tok[:, i, k * P:(k + 1) * P], ident[:])
                    filled("M", m, ins)
                elif kind == "wo1":
                    _, c, tp = step
                    for k in range(KD):
                        wait_read(pe, "M", ("aT1", c, k))
                    hi, lo = weights(("wo1", c))
                    m = take("M", step)
                    for i in (0, 1):
                        for k in range(KD):
                            tc = slice((TC * c + 2 * tp + i) * P, (TC * c + 2 * tp + i + 1) * P)
                            ins = three(psM[m][:, i * D:(i + 1) * D], xTh[:, k, tc], xTl[:, k, tc],
                                        hi[:, k * D:(k + 1) * D], lo[:, k * D:(k + 1) * D], start=k == 0, stop=k == KD - 1)
                    filled("M", m, ins)
                elif kind == "qkv2":
                    _, c, g, tp = step
                    wait_read(pe, "M", ("normT", 1, c, KD - 1))
                    hi, lo = weights(("w2", c, g))
                    s = take("T", step)
                    for i in (0, 1):
                        t = TC * c + 2 * tp + i
                        tc = slice(t * P, (t + 1) * P)
                        for k in range(KD):
                            ins = three(psT[s][:, i], xTh[:, k, tc], xTl[:, k, tc], hi[:, k * CH:(k + 1) * CH],
                                        lo[:, k * CH:(k + 1) * CH], start=k == 0, stop=k == KD - 1)
                    filled("T", s, ins)
                elif kind == "kT2":
                    _, c, j = step
                    pe.wait_ge(sem("roped"), nth[("rope", c, TC - 1, "k")])
                    pe.wait_ge(sem("pass_scaled"), nth[("rope", c, TC - 1, "k")])
                    m = take("M", step)
                    for i in range(TC):
                        ins = tr(psM[m][:, i * P:(i + 1) * P], k_tok[:, i, j], ident[:])
                    filled("M", m, ins)
                elif kind == "qT2":
                    u, i = step[1], step[2]
                    c, j, hp = u
                    pe.wait_ge(sem("roped"), nth[("rope", c, TC - 1, j)])
                    pe.wait_ge(sem("pass_scaled"), nth[("rope", c, TC - 1, j)])
                    m = take("M", step)
                    for t in range(TC):
                        ins = tr(psM[m][:, t * P:(t + 1) * P], q_tok[:, t, 4 * j + 2 * hp + i], ident[:])
                    filled("M", m, ins)
                elif kind == "max2":
                    _, u, t, i = step
                    c, j, hp = u
                    pe.wait_ge(sem("qT2_hi"), nth[("qT2", u, 1)])
                    wait_read(pe, "M", ("kT2", c, KV2 - 2))
                    wait_read(pe, "M", ("kT2", c, KV2 - 1))
                    s = take("T", step)
                    n = nth[("mT2", u)]
                    tc = slice((t % TC) * P, (t % TC + 1) * P)
                    w = (t + 1) * P
                    for b in (0, 1):
                        if i is None:
                            h, a0, a1 = b, 0, w
                        else:
                            h, a0, a1 = i, b * CH, min(w, b * CH + CH)
                        last = a1 == w
                        ins = mm(psT[s][:, b, 0:a1 - a0], qTh[:, n % 2, h, tc], kTh[:, j, a0:a1], start=True, stop=not last)
                        if last:
                            ins = mm(psT[s][:, b, a1 - a0 - P:a1 - a0], ident_b[:], mask_q[:], start=False, stop=True)
                    filled("T", s, ins)
                elif kind == "mT2":
                    u = step[1]
                    keys = [k for k in tab["T"] if k[0] == "max2" and k[1] == u][-2:]
                    for key in keys:
                        wait_read(pe, "T", key)
                    m = take("M", step)
                    for i in range(TC):
                        ins = tr(psM[m][:, i * P:(i + 1) * P], neg_max[:, i], ident[:])
                    filled("M", m, ins)
                elif kind == "score2":
                    _, u, sbk = step
                    c, j, hp = u
                    n = nth[("mT2", u)]
                    wait_read(pe, "M", ("mT2", u))
                    for i in (0, 1):
                        wait_read(pe, "M", ("qT2", u, i))
                    s = take("T", step)
                    diag_block = sbk >= TC * c
                    off = max(0, sbk - TC * c) * P
                    kb = slice(sbk * P, (sbk + 1) * P)
                    for b in (0, 1):
                        out = psT[s][:, b, off:CH]
                        three(out, kTh[:, j, kb], kTl[:, j, kb], qTh[:, n % 2, b, off:CH], qTl[:, n % 2, b, off:CH], stop=False)
                        ins = mm(out, pick[:, b], negmT[:, n % 2, off:CH], start=False, stop=not diag_block)
                        if diag_block:
                            ins = mm(psT[s][:, b, off:off + P], ident_b[:], mask_k[:], start=False, stop=True)
                    filled("T", s, ins)
                elif kind == "pv2":
                    _, u, sbk = step
                    c, j, hp = u
                    n = nth[step]
                    wait_read(pe, "T", ("score2",) + step[1:])
                    for tp in (0, 1):
                        wait_read(pe, "T", ("qkv2", c, 1, tp))
                    if sbk == 0:
                        if nth[("out2", u)] > 1:
                            pe.wait_ge(sem("oT_ready"), nth[("out2", u)] - 1)
                        else:
                            pe.wait_ge(sem("o1_out"), 4 * NC)
                    off = max(0, sbk - TC * c) * P
                    for b in (0, 1):
                        ins = mm(psO[:, b, off:CH], v_tok[:, sbk, j * DH2:(j + 1) * DH2], probs[:, n % 2, b, off:CH],
                                 start=sbk == 0, stop=sbk == TC * c + TC - 1)
                    ins.then_inc(sem("pv2_done"), 1)
                elif kind == "out2":
                    u = step[1]
                    c = u[0]
                    pe.wait_ge(sem("p_sum"), nth[("score2", u, TC * c + TC - 1)])
                    m = take("M", step)
                    for i in (0, 1):
                        for t in range(TC):
                            at = i * TC + t
                            ins = mm(psM[m][:, at:at + 1], p_sum[:, i, t * P:(t + 1) * P], ones[:, 0:1], start=True, stop=True)
                    filled("M", m, ins)
                elif kind == "wo2":
                    _, u, i, tp = step
                    c, j, hp = u
                    pe.wait_ge(sem("oT_ready"), nth[("out2", u)])
                    hi, lo = weights(("wo2", c, j))
                    m = take("M", step)
                    w = slice((2 * hp + i) * D, (2 * hp + i + 1) * D)
                    for b in (0, 1):
                        tc = slice((2 * tp + b) * P, (2 * tp + b + 1) * P)
                        ins = three(psM[m][:, b * D:(b + 1) * D], oTh[:, i, tc], oTl[:, i, tc], hi[:, w], lo[:, w])
                    filled("M", m, ins)
                elif kind == "router":
                    _, st, c = step
                    e_n = (E1, E2)[st]
                    wait_read(pe, "M", ("normT", 2 if st == 0 else 4, c, KD - 1))
                    m = take("M", step)
                    for k in range(KD):
                        for part in (xTh, xTl):
                            ins = mm(psM[m][0:e_n, :], rw[:, k, st * E1:st * E1 + e_n], part[:, k, c * CH:(c + 1) * CH].bitcast(F32),
                                     start=k == 0 and part is xTh, stop=k == KD - 1 and part is xTl)
                    filled("M", m, ins)
                elif kind == "logits":
                    _, st, c = step
                    e_n = (E1, E2)[st]
                    t0, t1 = tile_range(c)
                    for cc in range(t0 // TC, t1 // TC):
                        wait_read(pe, "M", ("router", st, cc))
                    m = take("M", step)
                    for t in range(t0, t1):
                        src = routed[st][t // TC][0:e_n, (t % TC) * P:(t % TC + 1) * P]
                        ins = tr(psM[m][:, (t - t0) * e_n:(t - t0 + 1) * e_n], src, ident[0:e_n, 0:e_n])
                    filled("M", m, ins)
                elif kind == "combT":
                    _, st, c = step
                    e_n = (E1, E2)[st]
                    pe.wait_ge(sem("comb_ready"), nth[("combine", st, c)] if st == 0 else 3)
                    m = take("M", step)
                    for i in range(TC):
                        ins = tr(psM[m][0:e_n, i * P:(i + 1) * P], comb[:, TC * c + i, 0:e_n], ident[:])
                    filled("M", m, ins)
                elif kind == "gateup":
                    _, st, b, c = step
                    wait_read(pe, "M", ("normT", 2 if st == 0 else 4, c, KD - 1))
                    hi, lo = weights(("moe", st, b))
                    s = take("T", step)
                    cols = slice(c * CH, (c + 1) * CH)
                    for up in (0, 1):
                        for k in range(KD):
                            w = slice((2 * k + up) * P, (2 * k + up + 1) * P)
                            ins = three(psT[s][:, up], hi[:, w], lo[:, w], xTh[:, k, cols], xTl[:, k, cols],
                                        start=k == 0, stop=k == KD - 1)
                    filled("T", s, ins)
                elif kind == "down":
                    _, st, b, c = step
                    n = nth[step]
                    pe.wait_ge(sem("act_lo"), n)
                    hi, lo = weights(("moe", st, b))
                    ring = ("O", "M")[c]
                    if b == 0:
                        if c == 0:
                            if st == 0:
                                pe.wait_ge(sem("oT_ready"), nth[outs[-1]])
                            else:
                                pe.wait_ge(sem("y_ready"), KD)
                        for i in (0, 1):
                            take(ring, ("acc", st, c), i)
                    for k in range(KD):
                        w = slice((2 * KD + k) * P, (2 * KD + k + 1) * P)
                        ins = three(acc_bank(c, tab[ring][("acc", st, c)][k][0]), hi[:, w], lo[:, w],
                                    aTh[:, n % PART_SLOTS], aTl[:, n % PART_SLOTS], start=b == 0, stop=b == BLOCKS[st] - 1)
                    ins.then_inc(sem("down_done"), 1)
                elif kind == "sumT":
                    _, st, c = step
                    for i in (0, 1):
                        wait_read(pe, ("O", "M")[c], ("acc", st, c), i)
                    s = take("T", step)
                    for t in range(TC):
                        for k in range(KD):
                            at = (t % 2) * D + k * P
                            ins = tr(psT[s][:, t // 2, at:at + P], accT[:, k, t * P:(t + 1) * P], ident[:])
                    filled("T", s, ins)
                elif kind == "proj":
                    _, c, w, ob = step
                    wait_read(pe, "T", ("normT", 3, c, KD - 1))
                    hi, lo = weights(("ssm", c, w))
                    s = take("T", step)
                    cols = slice(c * CH, (c + 1) * CH)
                    for k in range(KD):
                        wc = slice(k * D + ob * P, k * D + (ob + 1) * P)
                        ins = three(psT[s][:, 0], hi[:, wc], lo[:, wc], xTh[:, k, cols], xTl[:, k, cols],
                                    start=k == 0, stop=k == KD - 1)
                    filled("T", s, ins)
                elif kind == "scan":
                    _, ob, k = step
                    n = nth[step]
                    if k == 0:
                        if ob == 0:
                            for i in (0, 1):
                                wait_read(pe, "O", ("acc", 0, 0), i)
                        else:
                            pe.wait_ge(sem("y_ready"), ob)
                    pe.wait_ge(sem("scanned"), n)
                    pe.wait_ge(sem("diag_ready"), n)
                    for c in range(NC):
                        ins = mm(psO[:, c], diag[:, n % 2], state[:, n % 2, c * CH:(c + 1) * CH],
                                 start=k == 0, stop=k == NST - 1)
                    ins.then_inc(sem("scan_summed"), 1)
                elif kind == "yT":
                    tp = step[1]
                    pe.wait_ge(sem("y_ready"), KD)
                    m = take("M", step)
                    for i in (0, 1):
                        t = 2 * tp + i
                        for ob in range(KD):
                            ins = tr(psM[m][:, i * D + ob * P:i * D + (ob + 1) * P], yT[:, ob, t * P:(t + 1) * P], ident[:])
                    filled("M", m, ins)


def rope_tables():
    import numpy as np
    pos = np.arange(S, dtype=np.float32)
    inv = (1.0 / np.float32(1000000.0) ** (np.arange(0, RD, 2, dtype=np.float32) / RD)).astype(np.float32)
    ang = (pos[:, None] * inv[None, :]).astype(np.float32)
    cos, sin = np.cos(ang), np.sin(ang)
    def lay(t):
        return np.ascontiguousarray(t.astype(np.float32).reshape(NT, P, RD).transpose(1, 0, 2))
    return lay(np.concatenate([cos, cos], 1)), lay(np.concatenate([-sin, sin], 1))


INS = ["rw", "x", "weights", "bqkv", "bo", "lnw", "qkw", "cos", "sin", "rbias", "vecs", "mats"]


def kernel(**inputs):
    import numpy as np
    import concourse.bacc as bacc
    from concourse import mybir as mb
    from concourse.bass_utils import run_bass_kernel_spmd as run

    w = {k: np.asarray(v) for k, v in inputs.items()}

    def blocks(m):
        return m.reshape(-1, P, m.shape[-1]).transpose(1, 0, 2)

    def cols(vec):
        return vec.reshape(KD, P).T

    packed = np.zeros((N_PIECES, P, PIECE), np.float32)

    def put(n, *parts):
        at = 0
        for part in parts:
            part = part.reshape(part.shape[0], -1)
            packed[n, :part.shape[0], at:at + part.shape[1]] = part
            at += part.shape[1]

    for k in range(KD):
        put(k, w["L0_attn_Wqkv"][k * P:(k + 1) * P])
    put(2, blocks(w["L0_attn_Wo"]))
    put(3, blocks(w["L0_ffn_wk"]))
    put(4, blocks(w["L0_ffn_wv"]))
    for g in range(4):
        put(5 + g, blocks(w["L0_ffn_wq"][:, g * CH:(g + 1) * CH]))
    for j in range(KV2):
        put(9 + j, blocks(w["L0_ffn_wo"][j * 4 * DH2:(j + 1) * 4 * DH2]))
    for b in range(BLOCKS[0]):
        gu = np.stack([blocks(w["L0_ffn_wg"][b]), blocks(w["L0_ffn_wu"][b])], 2)
        put(13 + b, gu, w["L0_ffn_wd"][b])
    for n, name in enumerate(("Wdt", "Wb", "Wc")):
        put(21 + n, blocks(w["L1_attn_" + name]))
    gate_rows = w["L1_ffn_gate_up_proj"][:, :I2].reshape(E2 * I2, D)
    up_rows = w["L1_ffn_gate_up_proj"][:, I2:].reshape(E2 * I2, D)
    down_rows = w["L1_ffn_down_proj"].transpose(0, 2, 1).reshape(E2 * I2, D)
    for b in range(BLOCKS[1]):
        rows = slice(b * P, (b + 1) * P)
        put(24 + b, np.stack([blocks(gate_rows[rows].T), blocks(up_rows[rows].T)], 2), down_rows[rows])

    one = np.ones(D, np.float32)
    norms = [one, w["L0_ffn_ln1_w"], w["L0_ffn_ln2_w"], one, one]
    cos, sin = rope_tables()
    qkw = np.stack([w["L0_ffn_knorm_w"], w["L0_ffn_knorm_w"]]
                   + [w["L0_ffn_qnorm_w"][g * CH:(g + 1) * CH] for g in range(4)])
    vecs = np.stack([cols(w["L1_attn_" + n]) for n in ("bdt", "bb", "bc", "D")], 1)
    mats = np.stack([blocks(w["L1_attn_" + n]).reshape(P, -1) for n in ("a_raw", "B_base", "C_base")], 1)
    arrays = {
        "rw": np.concatenate([blocks(w["L0_ffn_router_w"]), blocks(w["L1_ffn_gate_weight"].T)], 2),
        "x": w["L0_attn_x"], "weights": packed, "bqkv": w["L0_attn_bqkv"], "bo": w["L0_attn_bo"],
        "lnw": np.stack([cols(n) for n in norms], 1), "qkw": qkw, "cos": cos, "sin": sin,
        "rbias": w["L0_ffn_router_bias"], "vecs": vecs, "mats": mats,
    }
    arrays = {n: np.ascontiguousarray(v) for n, v in arrays.items()}
    nc = bacc.Bacc("TRN2", target_bir_lowering=False, num_devices=1)
    aps = {n: nc.dram_tensor(n + "_dram", arrays[n].shape, mb.dt.from_np(arrays[n].dtype), kind="ExternalInput").ap()
           for n in INS}
    out = nc.dram_tensor("out_dram", (1, S, D), mb.dt.float32, kind="ExternalOutput").ap()
    build(nc, aps, out)
    r = run(nc, [{n + "_dram": v for n, v in arrays.items()}], core_ids=[0])
    return r.results[0]["out_dram"]
```
